# Optimizing a Trainium2 kernel written in Bass

```python
import numpy as np
import jax
import jax.numpy as jnp

def _softmax(x, axis=-1):
    return jax.nn.softmax(x, axis=axis)

def _gelu(x):
    return jax.nn.gelu(x, approximate=True)

def _silu(x):
    return jax.nn.silu(x)

def _sigmoid(x):
    return jax.nn.sigmoid(x)

def _layernorm(x, axis=-1, eps=1e-05):
    m = jnp.mean(x, axis=axis, keepdims=True)
    v = jnp.var(x, axis=axis, keepdims=True)
    return (x - m) / jnp.sqrt(v + eps)

def _scatter_add(tgt, idx, src, axis=0):
    return tgt.at[idx].add(src)

def _segment_sum(src, seg, n):
    return jax.ops.segment_sum(src, seg, n)
kernel_name = 'mk_flamingo_gated_d1_seqx_r4_378b94'

def setup_inputs(seed: int=0):
    np.random.seed(seed)
    _w = jnp.asarray

    def _rec_inputs():
        import jax
        import jax.numpy as jnp
        _rk = jax.random.key(seed)
        x = 0.002226 + 0.9996 * jax.random.normal(jax.random.fold_in(_rk, 1), (16, 256, 256), jnp.float32)
        _lenS = 256 - jax.random.randint(jax.random.fold_in(_rk, 7), (16,), 0, max(1, 256 // 4) + 1, jnp.int32)
        _lenS2 = 256 - jax.random.randint(jax.random.fold_in(_rk, 8), (16,), 0, max(1, 256 // 4) + 1, jnp.int32)
        _ctx_1024P = jax.random.normal(jax.random.fold_in(_rk, 11), (16, 16, 256), jnp.float32)
        _ctx_1024c = jax.random.dirichlet(jax.random.fold_in(_rk, 511), 0.3 * jnp.ones((16,), jnp.float32), (16, 256))
        _ctx_1024t = jnp.einsum('bsk,bkd->bsd', _ctx_1024c, _ctx_1024P)
        _ctx_1024t = _ctx_1024t * jax.lax.rsqrt(jnp.mean(jnp.square(_ctx_1024t)) + 1e-12) * 0.953939
        ctx_1024 = -0.000125008 + 0.999885 * (_ctx_1024t + 0.3 * jax.random.normal(jax.random.fold_in(_rk, 611), (16, 256, 256), jnp.float32))
        _g = jax.random.normal(jax.random.fold_in(_rk, 9001), (2, 1), jnp.float32)
        _g = jnp.sign(_g) * jnp.maximum(jnp.abs(_g), 1.0) + (_g == 0) * 1.0
        g_xattn = _g[0]
        g_ffn = _g[1]
        return (x, ctx_1024, g_xattn, g_ffn)
    x, ctx_1024, g_xattn, g_ffn = _rec_inputs()

    def _L0_xattn_setup():
        import jax, jax.numpy as jnp
        import numpy as np
        B, M, N, DIM, DH, H = (8, 1024, 64, 256, 128, 8)
        INNER = DH * H
        EPS = 1e-05

        def _layernorm(x, g, b):
            mu = jnp.mean(x, axis=-1, keepdims=True)
            var = jnp.var(x, axis=-1, keepdims=True)
            return (x - mu) * jax.lax.rsqrt(var + EPS) * g + b
        key = jax.random.key(seed)
        ks = jax.random.split(key, 8)
        sd = 0.02
        return {'x': jax.random.normal(ks[0], (B, M, DIM), jnp.float32), 'latents': jax.random.normal(ks[1], (B, N, DIM), jnp.float32), 'gamma_media': jnp.ones((DIM,), jnp.float32), 'beta_media': jnp.zeros((DIM,), jnp.float32), 'gamma_lat': jnp.ones((DIM,), jnp.float32), 'beta_lat': jnp.zeros((DIM,), jnp.float32), 'Wq': jax.random.normal(ks[2], (DIM, INNER), jnp.float32) * sd, 'bq': jnp.zeros((INNER,), jnp.float32), 'Wkv': jax.random.normal(ks[3], (DIM, 2 * INNER), jnp.float32) * sd, 'bkv': jnp.zeros((2 * INNER,), jnp.float32), 'Wo': jax.random.normal(ks[4], (INNER, DIM), jnp.float32) * sd, 'bo': jnp.zeros((DIM,), jnp.float32)}
    _L0_xattn_all = _L0_xattn_setup()
    _L0_xattn_in = {k: v for k, v in _L0_xattn_all.items() if k in ('gamma_media', 'beta_media', 'gamma_lat', 'beta_lat', 'Wq', 'bq', 'Wkv', 'bkv', 'Wo', 'bo')}
    del _L0_xattn_all

    def _L0_ffn_setup():
        import jax, jax.numpy as jnp
        import numpy as np
        TOP_K = 2
        TEMP = 1.0
        key = jax.random.key(seed)
        ks = jax.random.split(key, 5)
        B, S, D, E = (4, 512, 256, 8)
        F = 4 * D
        x = jax.random.normal(ks[0], (B, S, D), dtype=jnp.float32)
        Wg = jax.random.normal(ks[1], (D, E), dtype=jnp.float32) * (1.0 / np.sqrt(D))
        bg = jnp.zeros((E,), dtype=jnp.float32)
        W1 = jax.random.normal(ks[2], (E, D, F), dtype=jnp.float32) * (1.0 / np.sqrt(D))
        b1 = jnp.zeros((E, F), dtype=jnp.float32)
        W2 = jax.random.normal(ks[3], (E, F, D), dtype=jnp.float32) * (1.0 / np.sqrt(F))
        b2 = jnp.zeros((E, D), dtype=jnp.float32)
        return {'x': x, 'Wg': Wg, 'bg': bg, 'W1': W1, 'b1': b1, 'W2': W2, 'b2': b2}
    _L0_ffn_all = _L0_ffn_setup()
    _L0_ffn_in = {k: v for k, v in _L0_ffn_all.items() if k in ('Wg', 'bg', 'W1', 'b1', 'W2', 'b2')}
    del _L0_ffn_all
    return {'x': x, 'ctx_1024': ctx_1024, 'g_xattn': g_xattn, 'g_ffn': g_ffn, 'L0_xattn_gamma_media': _L0_xattn_in['gamma_media'], 'L0_xattn_beta_media': _L0_xattn_in['beta_media'], 'L0_xattn_gamma_lat': _L0_xattn_in['gamma_lat'], 'L0_xattn_beta_lat': _L0_xattn_in['beta_lat'], 'L0_xattn_Wq': _L0_xattn_in['Wq'], 'L0_xattn_bq': _L0_xattn_in['bq'], 'L0_xattn_Wkv': _L0_xattn_in['Wkv'], 'L0_xattn_bkv': _L0_xattn_in['bkv'], 'L0_xattn_Wo': _L0_xattn_in['Wo'], 'L0_xattn_bo': _L0_xattn_in['bo'], 'L0_ffn_Wg': _L0_ffn_in['Wg'], 'L0_ffn_bg': _L0_ffn_in['bg'], 'L0_ffn_W1': _L0_ffn_in['W1'], 'L0_ffn_b1': _L0_ffn_in['b1'], 'L0_ffn_W2': _L0_ffn_in['W2'], 'L0_ffn_b2': _L0_ffn_in['b2']}

def reference(x, ctx_1024, g_xattn, g_ffn, L0_xattn_gamma_media, L0_xattn_beta_media, L0_xattn_gamma_lat, L0_xattn_beta_lat, L0_xattn_Wq, L0_xattn_bq, L0_xattn_Wkv, L0_xattn_bkv, L0_xattn_Wo, L0_xattn_bo, L0_ffn_Wg, L0_ffn_bg, L0_ffn_W1, L0_ffn_b1, L0_ffn_W2, L0_ffn_b2):
    import jax
    import jax.numpy as jnp

    def _L0_xattn_ref(x, latents, gamma_media, beta_media, gamma_lat, beta_lat, Wq, bq, Wkv, bkv, Wo, bo):
        import jax, jax.numpy as jnp
        import numpy as np
        B, M, N, DIM, DH, H = (8, 1024, 64, 256, 128, 8)
        INNER = DH * H
        EPS = 1e-05

        def _layernorm(x, g, b):
            mu = jnp.mean(x, axis=-1, keepdims=True)
            var = jnp.var(x, axis=-1, keepdims=True)
            return (x - mu) * jax.lax.rsqrt(var + EPS) * g + b
        b = x.shape[0]
        xn = _layernorm(x, gamma_media, beta_media)
        ln = _layernorm(latents, gamma_lat, beta_lat)
        q = ln @ Wq + bq
        kv_input = jnp.concatenate([xn, ln], axis=1)
        kv = kv_input @ Wkv + bkv
        k, v = jnp.split(kv, 2, axis=-1)

        def to_heads(t):
            return t.reshape(b, t.shape[1], H, DH).transpose(0, 2, 1, 3)
        q, k, v = (to_heads(q), to_heads(k), to_heads(v))
        q = q * DH ** (-0.5)
        sim = jnp.einsum('bhid,bhjd->bhij', q, k)
        attn = jax.nn.softmax(sim, axis=-1)
        out = jnp.einsum('bhij,bhjd->bhid', attn, v)
        out = out.transpose(0, 2, 1, 3).reshape(b, -1, INNER)
        return out @ Wo + bo

    def _L0_ffn_ref(x, Wg, bg, W1, b1, W2, b2):
        import jax, jax.numpy as jnp
        import numpy as np
        TOP_K = 2
        TEMP = 1.0
        gates = (jnp.einsum('bsd,de->bse', x, Wg) + bg) / (TEMP + 1e-06)
        weights, indices = jax.lax.top_k(gates, TOP_K)
        weights = jax.nn.softmax(weights, axis=-1)
        h = jax.nn.silu(jnp.einsum('bsd,edf->bsef', x, W1) + b1)
        all_out = jnp.einsum('bsef,efd->bsed', h, W2) + b2
        gathered = jnp.take_along_axis(all_out, indices[..., None], axis=2)
        out = jnp.sum(gathered * weights[..., None], axis=2)
        return out
    x = x + jnp.tanh(g_xattn[0]) * _L0_xattn_ref(ctx_1024, _layernorm(x, axis=-1), L0_xattn_gamma_media, L0_xattn_beta_media, L0_xattn_gamma_lat, L0_xattn_beta_lat, L0_xattn_Wq, L0_xattn_bq, L0_xattn_Wkv, L0_xattn_bkv, L0_xattn_Wo, L0_xattn_bo)
    x = x + jnp.tanh(g_ffn[0]) * _L0_ffn_ref(_layernorm(x, axis=-1), L0_ffn_Wg, L0_ffn_bg, L0_ffn_W1, L0_ffn_b1, L0_ffn_W2, L0_ffn_b2)
    return x

_drawn_inputs = setup_inputs


def setup_inputs(seed=0):
    import zlib

    import numpy as np

    out = dict(_drawn_inputs(seed))
    spreads = {'L0_xattn_gamma_media': (1.0, 0.2),
     'L0_xattn_beta_media': (0.0, 0.345),
     'L0_xattn_gamma_lat': (1.0, 0.6),
     'L0_xattn_beta_lat': (0.0, 0.3),
     'L0_xattn_bq': (0.0, 0.8),
     'L0_xattn_bkv': (0.0, 0.1),
     'L0_xattn_bo': (0.0, 0.1),
     'L0_ffn_bg': (0.0, 0.1),
     'L0_ffn_b1': (0.0, 0.1),
     'L0_ffn_b2': (0.0, 0.1)}
    factors = {'L0_xattn_Wq': 4.826}
    for name, (base, spread) in spreads.items():
        noise = np.random.default_rng([zlib.crc32(name.encode()), seed]).standard_normal(out[name].shape)
        drawn = base * np.exp(spread * noise) if base else spread * noise
        out[name] = jnp.asarray(drawn.astype(out[name].dtype))
    for name, factor in factors.items():
        out[name] = (out[name] * factor).astype(out[name].dtype)
    return out
```

```python
from contextlib import ExitStack

import concourse.bass as bass
from concourse import mybir

F32 = mybir.dt.float32
F32R = mybir.dt.float32r
BF16 = mybir.dt.bfloat16
I32 = mybir.dt.int32
U32 = mybir.dt.uint32
ALU = mybir.AluOpType
ACT = mybir.ActivationFunctionType
AX_X = mybir.AxisListType.X

P = 128
B, T, D = 16, 256, 256
H, DH = 8, 128
INNER = H * DH
KEYS = 2 * T
E, F, TOP = 8, 1024, 2
TEMP = 1.0 + 1e-06
EPS = 1e-5
SCALE = float(DH) ** -0.5
KD = D // P
TT = T // P
JT = KEYS // P
STEPS = B * H
TOKENS = B * T
TOK_TILES = TOKENS // P
PAIRS = TOKENS * TOP
N_TILES = (PAIRS + E * (P - 1)) // P
ROW = D + E
HALF = INNER // 2
RING = 3

A_STEP = 6
B_STEP = 0
Z_STEP = 2
R_STEP = 1
T_STEP = 3
G_STEP = 4
W_STEP = 5


def plan_units():
    before = [("z", (0, k)) for k in range(KD)] + [("k", 0), ("q", 0)] + [("v", (0, w)) for w in range(JT)]
    steps = []
    for i in range(STEPS + H):
        units = []
        if i + 1 < STEPS:
            units += [("k", i + 1), ("q", i + 1)]
        m, w = (i - 1) // JT + 1, (i - 1) % JT
        if i and m < 2 * B:
            units.append(("v", (m, w)))
        if 1 <= i <= STEPS:
            units.append(("o", i - 1))
        b, h = i // H, i % H
        if h == Z_STEP and b + 1 < B:
            units += [("z", (b + 1, k)) for k in range(KD)]
        if h == T_STEP and b >= 1:
            units.append(("t", b - 1))
        if h == G_STEP and b >= 1:
            units.append(("g", b - 1))
        steps.append(units)
    return before, steps


class Later:

    def __init__(self, eng, sem):
        self.eng, self.sem, self.n = eng, sem, 0

    def mark(self, instruction):
        self.n += 1
        instruction.then_inc(self.sem, 1)

    def wait(self):
        self.eng.wait_ge(self.sem, self.n)


def build(nc, A):
    before, steps = plan_units()
    order = before + [u for s in steps for u in s]
    number = {u: n for n, u in enumerate(order)}
    hi_order = [u for u in order if u[0] in "kqvo"]
    hi_number = {u: n for n, u in enumerate(hi_order)}
    read_number = {u: n for group in ("zt", "kqvog")
                   for n, u in enumerate(u for u in order if u[0] in group)}

    with ExitStack() as top:
        def sem(name):
            return top.enter_context(nc.semaphore(name))

        def alloc(stack, name, shape, dt=F32):
            return stack.enter_context(nc.sbuf_tensor(name, shape, dt))

        ident = alloc(top, "ident", [P, P])
        onehot = alloc(top, "onehot", [P, TOP, E, TOK_TILES])
        iota8 = alloc(top, "iota8", [P, E])
        xhat_dram = nc.dram_tensor("xhat_rows", (TOKENS, ROW), F32, kind="Internal").ap()

        attention(nc, A, sem, alloc, ident, onehot, iota8, xhat_dram,
                  before, steps, number, hi_number, read_number)
        experts(nc, A, sem, alloc, ident, onehot, iota8, xhat_dram)


def attention(nc, A, sem, alloc, ident, onehot, iota8, xhat_dram, before, steps, number, hi_number, read_number):
    with ExitStack() as ctx:
        def sb(name, shape, dt=F32):
            return alloc(ctx, name, shape, dt)

        def bank(name):
            return ctx.enter_context(nc.psum_tensor(name, [P, 512], F32))

        wkv = [sb(f"wkv_{s}", [P, KD, 2 * INNER], F32R) for s in ("hi", "lo")]
        wq = [sb(f"wq_{s}", [P, KD, INNER], F32R) for s in ("hi", "lo")]
        wo = [sb(f"wo_{s}", [P, H, D], F32R) for s in ("hi", "lo")]
        wg = sb("wg", [P, KD, E])
        bq = sb("bq", [P, H])
        bk = sb("bk", [P, H])
        bv = sb("bv", [P, H])
        gamma = sb("gamma", [P, 2, KD])
        beta = sb("beta", [P, 2, KD])
        bo = sb("bo", [P, TT, D])
        bg = sb("bg", [P, E])
        gate = sb("gate", [P, 2])
        tgate = sb("tgate", [P, 2])
        minus_half = sb("minus_half", [P, 4])
        x_raw = [sb(f"x_raw{i}", [P, TT, D]) for i in range(3)]
        c_raw = [sb(f"c_raw{i}", [P, TT, D]) for i in range(2)]
        xh = sb("xh", [P, TT, D])
        z = sb("z", [P, JT, D])
        zt = sb("zt", [P, KD, KEYS])
        kvt = [[sb(f"kvt{i}_{s}", [P, KD, KEYS], F32R) for s in ("hi", "lo")] for i in range(2)]
        stats = {n: sb("stats_" + n, [P, 4, 6]) for n in "abc"}
        mv_a = sb("mv_a", [P, 4, 2])
        mv_b = sb("mv_b", [P, TT, 2])
        mv_c = sb("mv_c", [P, TT, 2])
        ve = {n: sb("ve_" + n, [P, 4]) for n in "abc"}
        rs_a = sb("rs_a", [P, 4])
        rs_b = sb("rs_b", [P, TT])
        rs_c = sb("rs_c", [P, TT])
        y = sb("y", [P, TT, D])
        x2 = [sb(f"x2_{i}", [P, TT, D]) for i in range(2)]
        rows = [sb(f"rows{i}", [P, TT, ROW]) for i in range(2)]
        x2t = sb("x2t", [P, KD, T])
        gates = sb("gates", [P, TT, E])
        top8 = sb("top8", [P, TT, 8])
        arg8 = sb("arg8", [P, TT, 8], U32)
        argf = sb("argf", [P, TT, TOP])
        gap = sb("gap", [P, TT])
        egap = sb("egap", [P, TT])
        wsum = sb("wsum", [P, TT])
        w12 = sb("w12", [P, TT, TOP])
        wtmp = sb("wtmp", [P, TT, E])
        smax = sb("smax", [P, 2, TT])
        nbias = sb("nbias", [P, 2, TT])
        ssum = sb("ssum", [P, 2, TT])
        rsum = sb("rsum", [P, 2, TT])

        with ExitStack() as early:
            kv_raw = alloc(early, "kv_raw", [P, KD, 2 * INNER])
            q_raw = alloc(early, "q_raw", [P, KD, INNER])
            o_raw = alloc(early, "o_raw", [P, H, D])
        v_sb = [[sb(f"v{i}_{s}", [P, JT, HALF], F32R) for s in ("hi", "lo")] for i in range(2)]
        pt = [sb(f"pt_{s}", [P, JT, T], F32R) for s in ("hi", "lo")]
        probs = [sb(f"probs{i}", [P, TT, KEYS]) for i in range(2)]
        kt = [[sb(f"kt{i}_{s}", [P, KEYS], F32R) for s in ("hi", "lo")] for i in range(2)]
        qt = [[sb(f"qt{i}_{s}", [P, T], F32R) for s in ("hi", "lo")] for i in range(2)]
        ot = [[sb(f"ot{i}_{s}", [P, T], F32R) for s in ("hi", "lo")] for i in range(2)]

        ring = [bank(f"ring{i}") for i in range(RING)]
        score = [bank(f"score{i}") for i in range(TT)]
        turn = [bank(f"turn{i}") for i in range(2)]
        proj = bank("proj")

        s_ident0, s_ident, s_const = sem("ident0"), sem("ident_ready"), sem("const")
        s_small, s_wkv, s_wq, s_wo = sem("small"), sem("wkv_in"), sem("wq_in"), sem("wo_in")
        s_x = [sem(f"x_in{i}") for i in range(3)]
        s_c = [sem(f"c_in{i}") for i in range(2)]
        s_wg = sem("wg_in")
        s_whi, s_wlo = sem("weights_hi"), sem("weights_lo")
        s_tg = sem("tanh_gate")
        s_full = sem("unit_full")
        s_hi = sem("unit_hi")
        s_read = sem("unit_read")
        s_aread = sem("unit_read_act")
        s_score = sem("scores")
        s_max = sem("max")
        s_exp = sem("exp")
        s_rsum = sem("rsum")
        s_norm = sem("norm")
        s_turn = sem("turned")
        s_pthi, s_ptlo = sem("pt_hi"), sem("pt_lo")
        s_proj, s_projr = sem("projected"), sem("projection_read")
        s_mva, s_mvb, s_mvc = sem("mv_a"), sem("mv_b"), sem("mv_c")
        s_rsa, s_rsb, s_rsc = sem("rs_a"), sem("rs_b"), sem("rs_c")
        s_cused, s_xh, s_z = sem("media_used"), sem("xh_ready"), sem("z_ready")
        s_kvt, s_xn = sem("kvt_ready"), sem("xn_rows")
        s_x2, s_rows, s_gap, s_egap = sem("x2"), sem("rows"), sem("gap"), sem("egap")
        s_x2st = [sem(f"x2_stored{i}") for i in range(2)]
        s_rowst = [sem(f"rows_stored{i}") for i in range(2)]
        s_trash, s_trashz = sem("trash_stored"), sem("trash_zero")
        s_dve, s_pool = sem("dve_self"), sem("pool_self")

        N_SMALL = 12

        def wait_read(eng, unit):
            eng.wait_ge(s_aread if unit[0] in "zt" else s_read, read_number[unit] + 1)

        ov = A["out"][0:TOKENS, :].rearrange("(b t p) d -> b p t d", t=TT, p=P)
        rv = xhat_dram.rearrange("(b t p) d -> b p t d", t=TT, p=P)

        def split_plan():
            out = []
            for k in range(KD):
                for c in range(2):
                    s = slice(c * INNER, (c + 1) * INNER)
                    out.append((kv_raw[:, k, s], wkv[0][:, k, s], wkv[1][:, k, s], s_wkv))
            for k in range(KD):
                out.append((q_raw[:, k, :], wq[0][:, k, :], wq[1][:, k, :], s_wq))
            for c in range(2):
                s = slice(c * H // 2, (c + 1) * H // 2)
                out.append((o_raw[:, s, :], wo[0][:, s, :], wo[1][:, s, :], s_wo))
            return out

        pieces = split_plan()
        order = before + [u for s in steps for u in s]

        with nc.Block() as block:
            @block.sync
            def _(sp):
                def load(c):
                    if c >= 3:
                        sp.wait_ge(s_x2, c - 2)
                    sp.dma_start(x_raw[c % 3][:, :, :],
                                 A["x"][c].rearrange("(t p) d -> p t d", p=P)).then_inc(s_x[c % 3], 16)
                    if c >= 2:
                        sp.wait_ge(s_cused, c - 1)
                    sp.dma_start(c_raw[c % 2][:, :, :],
                                 A["ctx_1024"][c].rearrange("(t p) d -> p t d", p=P)).then_inc(s_c[c % 2], 16)

                load(0)
                with nc.allow_non_contiguous_dma(reason="bias columns"):
                    for k, (g, b_) in enumerate((("gamma_media", "beta_media"), ("gamma_lat", "beta_lat"))):
                        sp.dma_start(gamma[:, k, :], A["L0_xattn_" + g].rearrange("(k p) -> p k", p=P)).then_inc(s_small, 16)
                        sp.dma_start(beta[:, k, :], A["L0_xattn_" + b_].rearrange("(k p) -> p k", p=P)).then_inc(s_small, 16)
                    sp.dma_start(bq[:, :], A["L0_xattn_bq"].rearrange("(h p) -> p h", p=P)).then_inc(s_small, 16)
                    bkv = A["L0_xattn_bkv"]
                    sp.dma_start(bk[:, :], bkv[0:INNER].rearrange("(h p) -> p h", p=P)).then_inc(s_small, 16)
                    sp.dma_start(bv[:, :], bkv[INNER:].rearrange("(h p) -> p h", p=P)).then_inc(s_small, 16)
                sp.dma_start(kv_raw[:, :, :], A["L0_xattn_Wkv"].rearrange("(k p) n -> p k n", p=P)).then_inc(s_wkv, 16)
                sp.dma_start(q_raw[:, :, :], A["L0_xattn_Wq"].rearrange("(k p) n -> p k n", p=P)).then_inc(s_wq, 16)
                sp.dma_start(o_raw[:, :, :], A["L0_xattn_Wo"].rearrange("(h p) n -> p h n", p=P)).then_inc(s_wo, 16)
                sp.dma_start(wg[:, :, :], A["L0_ffn_Wg"].rearrange("(k p) e -> p k e", p=P)).then_inc(s_wg, 16)
                for t in range(TT):
                    sp.dma_start(bo[:, t, :], A["L0_xattn_bo"].partition_broadcast(P)).then_inc(s_small, 16)
                sp.dma_start(bg[:, :], A["L0_ffn_bg"].partition_broadcast(P)).then_inc(s_small, 16)
                sp.dma_start(gate[:, 0:1], A["g_xattn"].partition_broadcast(P)).then_inc(s_small, 16)
                sp.dma_start(gate[:, 1:2], A["g_ffn"].partition_broadcast(P)).then_inc(s_small, 16)
                load(1)
                for b in range(B):
                    if b + 2 < B:
                        load(b + 2)
                    sp.wait_ge(s_x2, b + 1)
                    sp.dma_start(ov[b], x2[b % 2][:, :, :]).then_inc(s_x2st[b % 2], 16)
                    sp.wait_ge(s_rows, b + 1)
                    sp.dma_start(rv[b], rows[b % 2][:, :, :]).then_inc(s_rowst[b % 2], 16)
                sp.wait_ge(s_trashz, 1)
                sp.dma_start(A["out"][TOKENS:TOKENS + P, :], y[:, 0, :]).then_inc(s_trash, 16)
                sp.wait_ge(s_trash, 16)
                for i in range(2):
                    sp.wait_ge(s_x2st[i], 16 * (B // 2))
                    sp.wait_ge(s_rowst[i], 16 * (B // 2))

            @block.gpsimd
            def _(pool):
                own = Later(pool, s_pool)
                pool.memset(ident[:, :], 0.0).then_inc(s_ident0, 1)
                pool.memset(minus_half[:, :], -0.5).then_inc(s_const, 1)
                pool.iota(iota8[:, :], [[1, E]], base=0, channel_multiplier=0,
                          allow_small_or_imprecise_dtypes=True).then_inc(s_const, 1)
                pool.wait_ge(s_ident0, 1)
                pool.affine_select(out=ident[:, :], in_=ident[:, :], compare_op=ALU.not_equal, fill=1.0,
                                   base=0, pattern=[[-1, P]], channel_multiplier=1).then_inc(s_ident, 1)
                pool.wait_ge(s_const, 2)

                def rstd(norm, out, mv, n, ready, count, done):
                    pool.wait_ge(ready, count)
                    own.mark(pool.tensor_scalar(ve[norm][:, 0:n], mv[:, 0:n, 1], EPS, 1.0, ALU.add, ALU.mult))
                    own.wait()
                    pool.tensor_tensor(out[:, 0:n], ve[norm][:, 0:n], minus_half[:, 0:n], ALU.pow).then_inc(done, 1)

                def negate(mv):
                    own.mark(pool.tensor_scalar(mv[:, :, 0], mv[:, :, 0], -1.0, 0.0, ALU.mult, ALU.add))

                def norm(out, src, mv, rs, n):
                    return pool.tensor_scalar(out, src, mv[:, n, 0:1], rs[:, n:n + 1], ALU.add, ALU.mult)

                def prepare_a(c):
                    rstd("a", rs_a, mv_a, 4, s_mva, c + 1, s_rsa)
                    negate(mv_a)
                    own.wait()
                    pool.wait_ge(s_rsa, c + 1)
                    if c:
                        pool.wait_ge(s_mvb, c)
                        pool.wait_ge(s_full, number["z", (c - 1, KD - 1)] + 1)
                    for t in range(TT):
                        last = norm(xh[:, t, :], x_raw[c % 3][:, t, :], mv_a, rs_a, t)
                    last.then_inc(s_xh, 1)
                    for t in range(TT):
                        last = norm(z[:, t, :], c_raw[c % 2][:, t, :], mv_a, rs_a, TT + t)
                    last.then_inc(s_cused, 1)

                def prepare_b(c):
                    rstd("b", rs_b, mv_b, TT, s_mvb, c + 1, s_rsb)
                    negate(mv_b)
                    own.wait()
                    pool.wait_ge(s_rsb, c + 1)
                    for t in range(TT):
                        last = norm(z[:, TT + t, :], xh[:, t, :], mv_b, rs_b, t)
                    last.then_inc(s_z, 1)

                def norm_rows(b):
                    rstd("c", rs_c, mv_c, TT, s_mvc, b + 1, s_rsc)
                    negate(mv_c)
                    own.wait()
                    pool.wait_ge(s_rsc, b + 1)
                    if b >= 2:
                        pool.wait_ge(s_rowst[b % 2], 16 * (b // 2))
                    for t in range(TT):
                        last = norm(rows[b % 2][:, t, 0:D], x2[b % 2][:, t, :], mv_c, rs_c, t)
                    last.then_inc(s_xn, 1)

                def split_kv(c):
                    wait_read(pool, ("z", (c, KD - 1)))
                    if c >= 2:
                        pool.wait_ge(s_full, number["q", H * (c - 1) - 1] + 1)
                        pool.wait_ge(s_full, number["v", (2 * (c - 2) + 1, JT - 1)] + 1)
                    hi, lo = kvt[c % 2]
                    own.mark(pool.tensor_copy(hi[:, :, :], zt[:, :, :]))
                    own.wait()
                    pool.tensor_tensor(lo[:, :, :], zt[:, :, :], hi[:, :, :].bitcast(F32), ALU.subtract)\
                        .then_inc(s_kvt, 1)

                def normalise(n):
                    pool.wait_ge(s_rsum, n + 1)
                    for t in range(TT):
                        last = pool.tensor_scalar(probs[n % 2][:, t, :], probs[n % 2][:, t, :],
                                                  rsum[:, n % 2, t:t + 1], 1.0, ALU.mult, ALU.mult)
                    last.then_inc(s_norm, 1)

                prepare_a(0)
                prepare_b(0)
                split_kv(0)
                prepare_a(1)
                for i in range(STEPS + H):
                    b, h = i // H, i % H
                    if i < STEPS:
                        normalise(i)
                    if h == A_STEP and b + 2 < B:
                        prepare_a(b + 2)
                    if h == B_STEP and b + 1 < B:
                        prepare_b(b + 1)
                    if h == Z_STEP and b + 1 < B:
                        split_kv(b + 1)
                    if h == R_STEP and b >= 1:
                        norm_rows(b - 1)

            @block.scalar
            def _(act):
                act.wait_ge(s_small, 16 * N_SMALL)
                act.activation(tgate[:, :], gate[:, :], ACT.Tanh).then_inc(s_tg, 1)
                for raw, hi, _, ready in pieces:
                    act.wait_ge(ready, 16)
                    act.activation(hi, raw, ACT.Copy).then_inc(s_whi, 1)

                def hi_part(kind, at):
                    n = number[kind, at]
                    src = ring[n % RING]
                    act.wait_ge(s_full, n + 1)
                    if kind == "k":
                        ins = act.activation(kt[at % 2][0][:, :], src[:, :], ACT.Identity, bias=bk[:, at % H:at % H + 1])
                    elif kind == "q":
                        ins = act.activation(qt[at % 2][0][:, :], src[:, 0:T], ACT.Identity, bias=bq[:, at % H:at % H + 1])
                    elif kind == "o":
                        ins = act.activation(ot[at % 2][0][:, :], src[:, 0:T], ACT.Identity, bias=bv[:, at % H:at % H + 1])
                    else:
                        m, w = at
                        ins = act.activation(v_sb[m % 2][0][:, w, :], src[:, :], ACT.Copy)
                    ins.then_inc(s_hi, 1)

                def exp(n, t):
                    act.wait_ge(s_max, n + 1)
                    act.activation(probs[n % 2][:, t, :], score[t][:, :], ACT.Exp, scale=SCALE,
                                   bias=nbias[:, n % 2, t:t + 1],
                                   accum_out=ssum[:, n % 2, t:t + 1]).then_inc(s_exp, 1)

                def read_unit(kind, at):
                    n = number[kind, at]
                    src = ring[n % RING]
                    act.wait_ge(s_full, n + 1)
                    if kind == "z":
                        c, k = at
                        if c:
                            act.wait_ge(s_kvt, c)
                        for s in range(2):
                            last = act.activation(zt[:, k, s * T:(s + 1) * T], src[:, s * T:(s + 1) * T], ACT.Identity,
                                                  scale=gamma[:, s, k:k + 1], bias=beta[:, s, k:k + 1])
                    else:
                        last = act.activation(x2t[:, :, :], src[:, :].rearrange("p (k t) -> p k t", k=KD), ACT.Copy)
                    last.then_inc(s_aread, 1)

                for u in before:
                    hi_part(*u) if u in hi_number else read_unit(*u)
                for i in range(STEPS + H):
                    units = [u for u in steps[i] if u in hi_number]
                    if 1 <= i <= STEPS:
                        for t in range(2):
                            act.wait_ge(s_turn, 2 * (i - 1) + t + 1)
                            act.activation(pt[0][:, 2 * t:2 * t + 2, :],
                                           turn[t][:, :].rearrange("p (j i) -> p j i", j=2), ACT.Copy).then_inc(s_pthi, 1)
                    for u in units:
                        if u[0] == "k":
                            hi_part(*u)
                    if i < STEPS:
                        exp(i, 0)
                        exp(i, 1)
                    for u in units:
                        if u[0] != "k":
                            hi_part(*u)
                    for u in steps[i]:
                        if u[0] in "zt":
                            read_unit(*u)
                    if i % H == W_STEP and i // H >= 1:
                        b = i // H - 1
                        act.wait_ge(s_gap, b + 1)
                        act.activation(egap[:, :], gap[:, :], ACT.Exp).then_inc(s_egap, 1)

            @block.tensor
            def _(pe):
                def product(out, left, right, start, stop, **kw):
                    (lh, ll), (rh, rl) = left, right
                    pe.matmul(out, ll, rh, start=start, stop=False, **kw)
                    pe.matmul(out, lh, rl, start=False, stop=False, **kw)
                    return pe.matmul(out, lh, rh, start=False, stop=stop, **kw)

                def unit(kind, at):
                    n = number[kind, at]
                    dst = ring[n % RING]
                    if n >= RING:
                        wait_read(pe, order[n - RING])
                    if kind in "kq":
                        b, h = at // H, at % H
                        pe.wait_ge(s_kvt, b + 1)
                        w, c0, width = (wkv, 0, KEYS) if kind == "k" else (wq, T, T)
                        for k in range(KD):
                            last = product(dst[:, 0:width], [s[:, k, h * DH:(h + 1) * DH] for s in w],
                                           [s[:, k, c0:c0 + width] for s in kvt[b % 2]], k == 0, k == KD - 1)
                    elif kind == "v":
                        m, w = at
                        b, half = m // 2, m % 2
                        pe.wait_ge(s_kvt, b + 1)
                        c0 = INNER + half * HALF
                        for k in range(KD):
                            last = product(dst[:, :], [s[:, k, w * P:(w + 1) * P] for s in kvt[b % 2]],
                                           [s[:, k, c0:c0 + HALF] for s in wkv], k == 0, k == KD - 1)
                    elif kind == "o":
                        m, h4 = at // JT, at % JT
                        pe.wait_ge(s_ptlo, 2 * (at + 1))
                        wait_read(pe, ("v", (m, JT - 1)))
                        for j in range(JT):
                            last = product(dst[:, 0:T], [s[:, j, h4 * DH:(h4 + 1) * DH] for s in v_sb[m % 2]],
                                           [s[:, j, :] for s in pt], j == 0, j == JT - 1)
                    elif kind == "z":
                        c, k = at
                        pe.wait_ge(s_z, c + 1)
                        for j in range(JT):
                            last = pe.transpose(dst[:, j * P:(j + 1) * P], z[:, j, k * P:(k + 1) * P], ident[:, :])
                    elif kind == "t":
                        pe.wait_ge(s_rsc, at + 1)
                        pe.wait_ge(s_xn, at + 1)
                        for k in range(KD):
                            for t in range(TT):
                                last = pe.transpose(dst[:, (k * TT + t) * P:(k * TT + t + 1) * P],
                                                    rows[at % 2][:, t, k * P:(k + 1) * P], ident[:, :])
                    else:
                        pe.wait_ge(s_wg, 16)
                        wait_read(pe, ("t", at))
                        for t in range(TT):
                            for k in range(KD):
                                last = pe.matmul(dst[:, t * E:(t + 1) * E], x2t[:, k, t * P:(t + 1) * P],
                                                 wg[:, k, :], start=k == 0, stop=k == KD - 1)
                    last.then_inc(s_full, 1)

                def scores(n):
                    wait_read(pe, ("q", n))
                    if n:
                        pe.wait_ge(s_exp, TT * n)
                    for t in range(TT):
                        product(score[t][:, :], [s[:, t * P:(t + 1) * P] for s in qt[n % 2]],
                                [s[:, :] for s in kt[n % 2]], True, True).then_inc(s_score, 1)

                def turn_probs(n):
                    pe.wait_ge(s_norm, n + 1)
                    if n:
                        pe.wait_ge(s_ptlo, 2 * n)
                    for t in range(2):
                        for j in range(2):
                            for q in range(TT):
                                last = pe.transpose(turn[t][:, j * T + q * P:j * T + (q + 1) * P],
                                                    probs[n % 2][:, q, (2 * t + j) * P:(2 * t + j + 1) * P], ident[:, :])
                        last.then_inc(s_turn, 1)

                def out_proj(n):
                    b, h = n // H, n % H
                    wait_read(pe, ("o", n))
                    if h == 0 and b:
                        pe.wait_ge(s_projr, b)
                    for t in range(TT):
                        last = product(proj[:, t * D:(t + 1) * D], [s[:, t * P:(t + 1) * P] for s in ot[n % 2]],
                                       [s[:, h, :] for s in wo], h == 0 and t == 0, h == H - 1,
                                       skip_group_check=True)
                    if h == H - 1:
                        last.then_inc(s_proj, 1)

                pe.wait_ge(s_ident, 1)
                pe.wait_ge(s_wlo, len(pieces))
                for u in before:
                    unit(*u)
                for i in range(STEPS + H):
                    if i < STEPS:
                        scores(i)
                    if 1 <= i <= STEPS:
                        turn_probs(i - 1)
                    for u in steps[i]:
                        if u[0] in "kqov":
                            unit(*u)
                    if 2 <= i <= STEPS + 1:
                        out_proj(i - 2)
                    for u in steps[i]:
                        if u[0] in "ztg":
                            unit(*u)

            @block.vector
            def _(dve):
                own = Later(dve, s_dve)

                def moments(name, tiles, mv, done, used, turn):
                    dve.wait_ge(used, turn)
                    for n, t in enumerate(tiles):
                        own.mark(dve.bn_stats(stats[name][:, n, :], t))
                    own.wait()
                    for n in range(len(tiles)):
                        last = dve.bn_aggr(mv[:, n, :], stats[name][:, n, :])
                    last.then_inc(done, 1)

                def prepare_a(c):
                    dve.wait_ge(s_x[c % 3], 16 * (c // 3 + 1))
                    dve.wait_ge(s_c[c % 2], 16 * (c // 2 + 1))
                    moments("a", [x_raw[c % 3][:, t, :] for t in range(TT)] + [c_raw[c % 2][:, t, :] for t in range(TT)],
                            mv_a, s_mva, s_cused, c)

                def prepare_b(c):
                    dve.wait_ge(s_xh, c + 1)
                    moments("b", [xh[:, t, :] for t in range(TT)], mv_b, s_mvb, s_z, c)

                def read_unit(kind, at):
                    n = number[kind, at]
                    src = ring[n % RING]
                    if (kind, at) in hi_number:
                        dve.wait_ge(s_hi, hi_number[kind, at] + 1)
                        if kind == "k":
                            hi, lo = kt[at % 2]
                            bias, part = bk[:, at % H:at % H + 1], src[:, :]
                        elif kind == "q":
                            hi, lo = qt[at % 2]
                            bias, part = bq[:, at % H:at % H + 1], src[:, 0:T]
                        elif kind == "o":
                            hi, lo = ot[at % 2]
                            bias, part = bv[:, at % H:at % H + 1], src[:, 0:T]
                        if kind == "v":
                            m, w = at
                            hi, lo = v_sb[m % 2]
                            dve.tensor_tensor(lo[:, w, :], src[:, :], hi[:, w, :].bitcast(F32), ALU.subtract)\
                                .then_inc(s_read, 1)
                        else:
                            dve.scalar_tensor_tensor(out=lo[:, :], in0=part, scalar=bias, in1=hi[:, :].bitcast(F32),
                                                     op0=ALU.add, op1=ALU.subtract).then_inc(s_read, 1)
                        return
                    dve.wait_ge(s_full, n + 1)
                    route(at, src, read_number[kind, at])

                def route(b, src, n):
                    g3 = src[:, 0:TT * E].rearrange("p (t e) -> p t e", t=TT)
                    dve.tensor_tensor(gates[:, :, :], g3, bg[:, :].unsqueeze(1).to_broadcast([P, TT, E]), ALU.add)\
                        .then_inc(s_read, 1)
                    dve.wait_ge(s_read, n + 1)
                    own.mark(dve.tensor_scalar(gates[:, :, :], gates[:, :, :], 1.0 / TEMP, None, ALU.mult))
                    own.wait()
                    for t in range(TT):
                        own.mark(dve.max(top8[:, t, :], gates[:, t, :]))
                    own.wait()
                    if b:
                        dve.wait_ge(s_egap, b)
                    dve.tensor_tensor(gap[:, :], top8[:, :, 1], top8[:, :, 0], ALU.subtract).then_inc(s_gap, 1)
                    for t in range(TT):
                        own.mark(dve.max_index(arg8[:, t, :], top8[:, t, :], gates[:, t, :]))
                    own.wait()
                    own.mark(dve.tensor_copy(argf[:, :, :], arg8[:, :, 0:TOP]))
                    own.wait()
                    for k in range(TOP):
                        for t in range(TT):
                            own.mark(dve.tensor_scalar(onehot[:, k, :, TT * b + t], iota8[:, :],
                                                       argf[:, t, k:k + 1], None, ALU.is_equal))
                    own.wait()

                def weigh(b):
                    dve.wait_ge(s_egap, b + 1)
                    own.mark(dve.tensor_scalar(wsum[:, :], egap[:, :], 1.0, None, ALU.add))
                    own.wait()
                    own.mark(dve.reciprocal(w12[:, :, 0], wsum[:, :]))
                    own.wait()
                    own.mark(dve.tensor_tensor(w12[:, :, 1], w12[:, :, 0], egap[:, :], ALU.mult))
                    own.wait()
                    own.mark(dve.tensor_scalar(w12[:, :, :], w12[:, :, :], tgate[:, 1:2], None, ALU.mult))
                    own.wait()
                    for t in range(TT):
                        own.mark(dve.tensor_scalar(wtmp[:, t, :], onehot[:, 0, :, TT * b + t], w12[:, t, 0:1], None, ALU.mult))
                    own.wait()
                    for t in range(TT):
                        last = dve.scalar_tensor_tensor(out=rows[b % 2][:, t, D:ROW], in0=onehot[:, 1, :, TT * b + t],
                                                        scalar=w12[:, t, 1:2], in1=wtmp[:, t, :],
                                                        op0=ALU.mult, op1=ALU.add)
                    last.then_inc(s_rows, 1)

                def residual(b):
                    dve.wait_ge(s_proj, b + 1)
                    dve.tensor_tensor(y[:, :, :], proj[:, :].rearrange("p (t d) -> p t d", t=TT), bo[:, :, :], ALU.add)\
                        .then_inc(s_projr, 1)
                    dve.wait_ge(s_projr, b + 1)
                    if b >= 2:
                        dve.wait_ge(s_x2st[b % 2], 16 * (b // 2))
                    dve.scalar_tensor_tensor(out=x2[b % 2][:, :, :], in0=y[:, :, :], scalar=tgate[:, 0:1],
                                             in1=x_raw[b % 3][:, :, :], op0=ALU.mult, op1=ALU.add).then_inc(s_x2, 1)
                    dve.wait_ge(s_x2, b + 1)
                    moments("c", [x2[b % 2][:, t, :] for t in range(TT)], mv_c, s_mvc, s_xn, b)

                def maximum(n):
                    for t in range(TT):
                        dve.wait_ge(s_score, TT * n + t + 1)
                        own.mark(dve.tensor_reduce(smax[:, n % 2, t:t + 1], score[t][:, :], AX_X, ALU.max))
                    own.wait()
                    dve.tensor_scalar(nbias[:, n % 2, :], smax[:, n % 2, :], -SCALE, None, ALU.mult).then_inc(s_max, 1)

                def reciprocal_sum(n):
                    dve.wait_ge(s_exp, TT * (n + 1))
                    dve.reciprocal(rsum[:, n % 2, :], ssum[:, n % 2, :]).then_inc(s_rsum, 1)

                prepare_a(0)
                for n, (raw, hi, lo, _) in enumerate(pieces):
                    dve.wait_ge(s_whi, n + 1)
                    dve.tensor_tensor(lo, raw, hi.bitcast(F32), ALU.subtract).then_inc(s_wlo, 1)
                    if n == 1:
                        prepare_b(0)
                    if n == 3:
                        prepare_a(1)
                dve.wait_ge(s_small, 16 * N_SMALL)
                dve.wait_ge(s_tg, 1)
                dve.wait_ge(s_const, 2)
                for u in before:
                    if u[0] not in "zt":
                        read_unit(*u)
                for i in range(STEPS + H):
                    b, h = i // H, i % H
                    if i < STEPS:
                        maximum(i)
                    if 1 <= i <= STEPS:
                        for t in range(2):
                            dve.wait_ge(s_pthi, 2 * (i - 1) + t + 1)
                            dve.tensor_tensor(pt[1][:, 2 * t:2 * t + 2, :],
                                              turn[t][:, :].rearrange("p (j i) -> p j i", j=2),
                                              pt[0][:, 2 * t:2 * t + 2, :].bitcast(F32), ALU.subtract)\
                                .then_inc(s_ptlo, 1)
                    for u in steps[i]:
                        if u[0] in "kq":
                            read_unit(*u)
                    if i < STEPS:
                        reciprocal_sum(i)
                    for u in steps[i]:
                        if u[0] in "vog":
                            read_unit(*u)
                    if h == A_STEP and b + 2 < B:
                        prepare_a(b + 2)
                    if h == B_STEP and b + 1 < B:
                        prepare_b(b + 1)
                    if h == R_STEP and b >= 1:
                        residual(b - 1)
                    if h == W_STEP and b >= 1:
                        weigh(b - 1)
                dve.wait_ge(s_projr, B)
                dve.memset(y[:, 0, :], 0.0).then_inc(s_trashz, 1)


def experts(nc, A, sem, alloc, ident, onehot, iota8, xhat_dram):
    with ExitStack() as ctx:
        def sb(name, shape, dt=F32):
            return alloc(ctx, name, shape, dt)

        def bank(name):
            return ctx.enter_context(nc.psum_tensor(name, [P, 512], F32))

        w1 = sb("w1", [P, KD, E * F])
        w2 = sb("w2", [P, F // P, E * D])
        b1 = sb("b1", [P, E * F], F32)
        token = sb("token", [P, N_TILES], I32)
        target = sb("target", [P, N_TILES], I32)
        expert = sb("expert", [P, N_TILES], I32)
        mine = sb("mine", [P, N_TILES, E])

        s_w1, s_w2, s_b1, s_b2 = sem("w1_in"), sem("w2_in"), sem("b1_in"), sem("b2_in")

        def load_weights(sp):
            sp.dma_start(w1[:, :, :].rearrange("p k (e f) -> p k e f", e=E)[:, 0],
                         A["L0_ffn_W1"][:, 0:P, :].rearrange("e p f -> p e f")).then_inc(s_w1, 16)
            sp.dma_start(w1[:, :, :].rearrange("p k (e f) -> p k e f", e=E)[:, 1],
                         A["L0_ffn_W1"][:, P:2 * P, :].rearrange("e p f -> p e f")).then_inc(s_w1, 16)
            for g in range(F // P):
                sp.dma_start(w2[:, g, :].rearrange("p (e d) -> p e d", e=E),
                             A["L0_ffn_W2"][:, g * P:(g + 1) * P, :].rearrange("e p d -> p e d")).then_inc(s_w2, 16)
            sp.dma_start(b1[:, :], A["L0_ffn_b1"].rearrange("e f -> (e f)").partition_broadcast(P)).then_inc(s_b1, 16)

        routing(nc, alloc, sem, onehot, iota8, token, target, expert, mine, load_weights)

        b2 = sb("b2", [P, E * D], F32)
        NX, NO = 4, 2
        xg = [sb(f"xg{i}", [P, ROW]) for i in range(NX)]
        xt = [sb(f"xt{i}", [P, KD, P]) for i in range(2)]
        hb = sb("hb", [P, F])
        ha = sb("ha", [P, F])
        ht = sb("ht", [P, F // P, P])
        yb = sb("yb", [P, D])
        yo = [sb(f"yo{i}", [P, D]) for i in range(NO)]
        wcol = sb("wcol", [P, 2])
        wjunk = sb("wjunk", [P, E])
        ph = [bank(f"ph{i}") for i in range(2)]
        pht = [bank(f"pht{i}") for i in range(2)]
        px = bank("px")
        py = bank("py")

        s_g = [sem(f"gathered{i}") for i in range(NX)]
        s_px, s_xt = sem("x_turned"), sem("xt_ready")
        s_ph, s_hb, s_ha = sem("hidden"), sem("hidden_bias"), sem("hidden_act")
        s_pht, s_htd, s_hta = sem("hidden_turned"), sem("ht_dve"), sem("ht_act")
        s_py, s_pyr, s_w, s_yo = sem("y_sum"), sem("y_read"), sem("w_ready"), sem("y_out")
        s_add = sem("added")
        GH = F // 512

        with nc.Block() as block:
            @block.sync
            def _(sp):
                sp.dma_start(b2[:, :], A["L0_ffn_b2"].rearrange("e d -> (e d)").partition_broadcast(P)).then_inc(s_b2, 16)
                sp.wait_ge(s_b2, 16)

            @block.gpsimd
            def _(pool):
                def gather(t):
                    if t >= NX:
                        pool.wait_ge(s_px, t - NX + 1)
                        pool.wait_ge(s_w, t - NX + 1)
                    pool.indirect_dma_start(
                        out=xg[t % NX][:, :], out_offset=None, in_=xhat_dram,
                        in_offset=bass.IndirectOffsetOnAxis(ap=token[:, t:t + 1].bitcast(U32), axis=0),
                    ).then_inc(s_g[t % NX], 16)

                for t in range(NX - 1):
                    gather(t)
                for t in range(N_TILES):
                    if t + NX - 1 < N_TILES:
                        gather(t + NX - 1)
                    pool.wait_ge(s_yo, t + 1)
                    if t:
                        pool.wait_ge(s_add, 16 * t)
                    pool.indirect_dma_start(
                        out=A["out"], out_offset=bass.IndirectOffsetOnAxis(ap=target[:, t:t + 1].bitcast(U32), axis=0),
                        in_=yo[t % NO][:, :], in_offset=None, compute_op=ALU.add,
                    ).then_inc(s_add, 16)
                pool.wait_ge(s_add, 16 * N_TILES)

            @block.tensor
            def _(pe):
                def turn_x(t):
                    pe.wait_ge(s_g[t % NX], 16 * (t // NX + 1))
                    if t:
                        pe.wait_ge(s_xt, t)
                    for k in range(KD):
                        last = pe.transpose(px[:, k * P:(k + 1) * P], xg[t % NX][:, k * P:(k + 1) * P], ident[:, :])
                    last.then_inc(s_px, 1)

                def hidden(t, e):
                    pe.wait_ge(s_xt, t + 1)
                    if t:
                        pe.wait_ge(s_hb, GH * t)
                    for c in range(GH):
                        for k in range(KD):
                            last = pe.matmul(ph[c][:, :], xt[t % 2][:, k, :], w1[:, k, bass.ds(e * F + c * 512, 512)],
                                             start=k == 0, stop=k == KD - 1)
                        last.then_inc(s_ph, 1)

                def turn_h(t):
                    pe.wait_ge(s_ha, GH * (t + 1))
                    if t:
                        pe.wait_ge(s_htd, t)
                        pe.wait_ge(s_hta, t)
                    for c in range(GH):
                        for j in range(4):
                            last = pe.transpose(pht[c][:, j * P:(j + 1) * P], ha[:, (4 * c + j) * P:(4 * c + j + 1) * P],
                                                ident[:, :])
                        last.then_inc(s_pht, 1)

                def out(t, e):
                    pe.wait_ge(s_htd, t + 1)
                    pe.wait_ge(s_hta, t + 1)
                    if t:
                        pe.wait_ge(s_pyr, t)
                    for g in range(F // P):
                        last = pe.matmul(py[:, 0:D], ht[:, g, :], w2[:, g, bass.ds(e * D, D)],
                                         start=g == 0, stop=g == F // P - 1)
                    last.then_inc(s_py, 1)

                pe.wait_ge(s_w1, 32)
                turn_x(0)
                pe.wait_ge(s_w2, 16 * (F // P))
                before_e = None
                for t in range(N_TILES + 1):
                    if t < N_TILES:
                        e = pe.value_load(expert[0:1, t:t + 1], min_val=0, max_val=E - 1)
                    if t:
                        turn_h(t - 1)
                    if t < N_TILES:
                        hidden(t, e)
                    if t + 1 < N_TILES:
                        turn_x(t + 1)
                    if t:
                        out(t - 1, before_e)
                    before_e = e

            @block.vector
            def _(dve):
                def copy_x(t):
                    dve.wait_ge(s_px, t + 1)
                    if t >= 2:
                        dve.wait_ge(s_ph, GH * (t - 1))
                    dve.tensor_copy(xt[t % 2][:, :, :], px[:, 0:D].rearrange("p (k t) -> p k t", k=KD)).then_inc(s_xt, 1)

                dve.wait_ge(s_b1, 16)
                dve.wait_ge(s_b2, 16)
                copy_x(0)
                before_e = None
                for t in range(N_TILES + 1):
                    if t < N_TILES:
                        e = dve.value_load(expert[0:1, t:t + 1], min_val=0, max_val=E - 1)
                    if t:
                        dve.wait_ge(s_pht, GH * (t - 1) + 1)
                        if t > 1:
                            dve.wait_ge(s_py, t - 1)
                        dve.tensor_copy(ht[:, 0:4, :], pht[0][:, :].rearrange("p (g t) -> p g t", g=4)).then_inc(s_htd, 1)
                    if t < N_TILES:
                        for c in range(GH):
                            dve.wait_ge(s_ph, GH * t + c + 1)
                            if t:
                                dve.wait_ge(s_ha, GH * (t - 1) + c + 1)
                            dve.tensor_tensor(hb[:, c * 512:(c + 1) * 512], ph[c][:, :],
                                              b1[:, bass.ds(e * F + c * 512, 512)], ALU.add).then_inc(s_hb, 1)
                        dve.wait_ge(s_g[t % NX], 16 * (t // NX + 1))
                        if t >= 2:
                            dve.wait_ge(s_yo, t - 1)
                        dve.scalar_tensor_tensor(out=wjunk[:, :], in0=xg[t % NX][:, D:ROW], scalar=1.0, in1=mine[:, t, :],
                                                 op0=ALU.mult, op1=ALU.mult, accum_out=wcol[:, t % 2:t % 2 + 1])\
                            .then_inc(s_w, 1)
                    if t + 1 < N_TILES:
                        copy_x(t + 1)
                    if t:
                        dve.wait_ge(s_py, t)
                        dve.tensor_tensor(yb[:, :], py[:, 0:D], b2[:, bass.ds(before_e * D, D)], ALU.add).then_inc(s_pyr, 1)
                        dve.wait_ge(s_pyr, t)
                        dve.wait_ge(s_w, t)
                        if t > NO:
                            dve.wait_ge(s_add, 16 * (t - NO))
                        dve.tensor_scalar(yo[(t - 1) % NO][:, :], yb[:, :], wcol[:, (t - 1) % 2:(t - 1) % 2 + 1], None,
                                          ALU.mult).then_inc(s_yo, 1)
                    before_e = e

            @block.scalar
            def _(act):
                for t in range(N_TILES + 1):
                    if t:
                        act.wait_ge(s_pht, GH * t)
                        if t > 1:
                            act.wait_ge(s_py, t - 1)
                        act.activation(ht[:, 4:8, :], pht[1][:, :].rearrange("p (g t) -> p g t", g=4), ACT.Copy)\
                            .then_inc(s_hta, 1)
                    if t < N_TILES:
                        for c in range(GH):
                            act.wait_ge(s_hb, GH * t + c + 1)
                            if t:
                                act.wait_ge(s_pht, GH * (t - 1) + c + 1)
                            act.activation(ha[:, c * 512:(c + 1) * 512], hb[:, c * 512:(c + 1) * 512], ACT.Silu)\
                                .then_inc(s_ha, 1)


def routing(nc, alloc, sem, onehot, iota8, token, target, expert, mine, load_weights):
    EC = E * TOK_TILES
    NP = TOP * TOK_TILES
    with ExitStack() as ctx:
        def sb(name, shape, dt=F32):
            return alloc(ctx, name, shape, dt)

        def bank(name):
            return ctx.enter_context(nc.psum_tensor(name, [P, 512], F32))

        chosen = sb("chosen", [P, E, TOK_TILES])
        below = sb("below", [P, P])
        ones = sb("ones", [P, P])
        lane = sb("lane", [P, 1])
        iota_p = sb("iota_p", [P, P])
        totals = sb("totals", [P, E, TOK_TILES])
        run = sb("run", [P, E, TOK_TILES])
        zero = sb("zero", [P, EC])
        count = sb("count", [P, E])
        counti = sb("counti", [P, E], I32)
        tiles = sb("tiles", [P, E])
        first = sb("first", [P, E])
        shift = sb("shift", [P, E])
        place = sb("place", [P, E, TOK_TILES])
        mult = sb("mult", [P, E, TOK_TILES])
        slot = sb("slot", [P, TOP, TOK_TILES])
        sloti = sb("sloti", [P, NP], I32)
        part = sb("part", [P, 2, NP], I32)
        slot_tile = sb("slot_tile", [P, NP])
        slot_row = sb("slot_row", [P, NP])
        GRP = 16
        left = [sb(f"left{i}", [P, GRP, P], BF16) for i in range(2)]
        tile_eq = [sb(f"tile_eq{i}", [P, GRP, N_TILES], BF16) for i in range(2)]
        right = [sb(f"right{i}", [P, GRP, 3, N_TILES], BF16) for i in range(2)]
        tokf = sb("tokf", [P, N_TILES])
        tgtf = sb("tgtf", [P, N_TILES])
        pad = sb("pad", [P, N_TILES])
        trash = sb("trash", [P, 1])
        ge = sb("ge", [P, E, N_TILES])
        expf = sb("expf", [P, N_TILES])
        pc0, pc1, inv = bank("prefix"), bank("sums"), bank("inverse")

        s_k0, s_k1, s_ch, s_pre = sem("consts0"), sem("consts1"), sem("chosen"), sem("prefix")
        s_oh, s_inv, s_dve = sem("rows_cols"), sem("inverse_part"), sem("route_self")

        with nc.Block() as block:
            @block.sync
            def _(sp):
                load_weights(sp)

            @block.gpsimd
            def _(pool):
                pool.memset(below[:, :], 1.0).then_inc(s_k0, 1)
                pool.memset(ones[:, :], 1.0).then_inc(s_k1, 1)
                pool.iota(iota_p[:, :], [[1, P]], base=0, channel_multiplier=0,
                          allow_small_or_imprecise_dtypes=True).then_inc(s_k1, 1)
                pool.iota(lane[:, :], [[1, 1]], base=0, channel_multiplier=1,
                          allow_small_or_imprecise_dtypes=True).then_inc(s_k1, 1)
                pool.wait_ge(s_k0, 1)
                pool.affine_select(out=below[:, :], in_=below[:, :], compare_op=ALU.is_gt, fill=0.0,
                                   base=0, pattern=[[1, P]], channel_multiplier=-1).then_inc(s_k1, 1)

            @block.tensor
            def _(pe):
                pe.wait_ge(s_k1, 4)
                pe.wait_ge(s_ch, 1)
                ch = chosen[:, :, :].rearrange("p e t -> p (e t)")
                pe.matmul(pc0[:, 0:EC], below[:, :], ch, start=True, stop=True)
                pe.matmul(pc1[:, 0:EC], ones[:, :], ch, start=True, stop=True).then_inc(s_pre, 1)
                for g in range(NP // GRP):
                    pe.wait_ge(s_oh, g + 1)
                    for j in range(GRP):
                        last = pe.matmul(inv[:, 0:3 * N_TILES], left[g % 2][:, j, :],
                                         right[g % 2][:, j, :, :].rearrange("p a t -> p (a t)"),
                                         start=g == 0 and j == 0, stop=g == NP // GRP - 1 and j == GRP - 1)
                    last.then_inc(s_inv, 1)

            @block.vector
            def _(dve):
                own = Later(dve, s_dve)

                def do(instruction):
                    own.mark(instruction)
                    own.wait()

                dve.tensor_tensor(chosen[:, :, :], onehot[:, 0], onehot[:, 1], ALU.add).then_inc(s_ch, 1)
                own.mark(dve.memset(zero[:, :], 0.0))
                dve.wait_ge(s_k1, 4)
                dve.wait_ge(s_pre, 1)
                flat = lambda a: a[:, :, :].rearrange("p e t -> p (e t)")
                do(dve.tensor_copy(flat(totals), pc1[:, 0:EC]))
                own.mark(dve.tensor_reduce(count[:, :], totals[:, :, :], AX_X, ALU.add))
                do(dve.tensor_tensor_scan(flat(run), flat(totals), zero[:, :], 0.0, ALU.add, ALU.add))
                do(dve.tensor_tensor(flat(run), flat(run), flat(totals), ALU.subtract))
                do(dve.tensor_scalar(counti[:, :], count[:, :], float(P - 1), None, ALU.add))
                do(dve.tensor_scalar(counti[:, :], counti[:, :], 7, None, ALU.logical_shift_right))
                do(dve.tensor_copy(tiles[:, :], counti[:, :]))
                do(dve.tensor_tensor_scan(first[:, :], tiles[:, :], zero[:, 0:E], 0.0, ALU.add, ALU.add))
                do(dve.tensor_tensor(first[:, :], first[:, :], tiles[:, :], ALU.subtract))
                do(dve.scalar_tensor_tensor(out=shift[:, :], in0=first[:, :], scalar=float(P), in1=run[:, :, 0],
                                            op0=ALU.mult, op1=ALU.subtract))
                do(dve.tensor_tensor(flat(place), pc0[:, 0:EC], flat(run), ALU.add))
                do(dve.tensor_tensor(place[:, :, :], place[:, :, :],
                                     shift[:, :].unsqueeze(2).to_broadcast([P, E, TOK_TILES]), ALU.add))
                for k in range(TOP):
                    do(dve.tensor_tensor(mult[:, :, :], place[:, :, :], onehot[:, k], ALU.mult))
                    do(dve.tensor_reduce(slot[:, k, :], mult[:, :, :].rearrange("p e t -> p t e"), AX_X, ALU.add))
                do(dve.tensor_copy(sloti[:, :], slot[:, :, :].rearrange("p k t -> p (k t)")))
                do(dve.tensor_scalar(part[:, 0, :], sloti[:, :], 7, None, ALU.logical_shift_right))
                do(dve.tensor_scalar(part[:, 1, :], sloti[:, :], P - 1, None, ALU.bitwise_and))
                own.mark(dve.tensor_copy(slot_tile[:, :], part[:, 0, :]))
                do(dve.tensor_copy(slot_row[:, :], part[:, 1, :]))
                for g in range(NP // GRP):
                    if g >= 2:
                        dve.wait_ge(s_inv, g - 1)
                    s = slice(g * GRP, (g + 1) * GRP)
                    r = right[g % 2]
                    own.mark(dve.tensor_tensor(left[g % 2][:, :, :], iota_p[:, :].unsqueeze(1).to_broadcast([P, GRP, P]),
                                               slot_row[:, s].unsqueeze(2).to_broadcast([P, GRP, P]), ALU.is_equal))
                    do(dve.tensor_tensor(tile_eq[g % 2][:, :, :],
                                         iota_p[:, 0:N_TILES].unsqueeze(1).to_broadcast([P, GRP, N_TILES]),
                                         slot_tile[:, s].unsqueeze(2).to_broadcast([P, GRP, N_TILES]), ALU.is_equal))
                    own.mark(dve.tensor_copy(r[:, :, 0, :], tile_eq[g % 2][:, :, :]))
                    own.mark(dve.tensor_scalar(r[:, :, 1, :], tile_eq[g % 2][:, :, :], lane[:, 0:1], None, ALU.mult))
                    t0 = g * GRP % TOK_TILES
                    dve.tensor_tensor(r[:, :, 2, :], tile_eq[g % 2][:, :, :],
                                      iota_p[:, t0:t0 + GRP].unsqueeze(2).to_broadcast([P, GRP, N_TILES]), ALU.mult)\
                        .then_inc(s_oh, 1)
                own.wait()
                do(dve.tensor_tensor(ge[:, :, :], iota_p[:, 0:N_TILES].unsqueeze(1).to_broadcast([P, E, N_TILES]),
                                     first[:, :].unsqueeze(2).to_broadcast([P, E, N_TILES]), ALU.is_ge))
                do(dve.tensor_reduce(expf[:, :], ge[:, 1:E, :].rearrange("p e t -> p t e"), AX_X, ALU.add))
                own.mark(dve.tensor_copy(expert[:, :], expf[:, :]))
                own.mark(dve.tensor_tensor(mine[:, :, :], iota8[:, :].unsqueeze(1).to_broadcast([P, N_TILES, E]),
                                           expf[:, :].unsqueeze(2).to_broadcast([P, N_TILES, E]), ALU.is_equal))
                own.mark(dve.tensor_scalar(trash[:, :], lane[:, :], float(TOKENS), None, ALU.add))
                dve.wait_ge(s_inv, NP // GRP)
                own.mark(dve.tensor_scalar(pad[:, :], inv[:, 0:N_TILES], -1.0, 1.0, ALU.mult, ALU.add))
                do(dve.tensor_scalar(tokf[:, :], inv[:, 2 * N_TILES:3 * N_TILES], float(P), None, ALU.mult))
                do(dve.tensor_tensor(tokf[:, :], inv[:, N_TILES:2 * N_TILES], tokf[:, :], ALU.add))
                own.mark(dve.tensor_copy(token[:, :], tokf[:, :]))
                do(dve.scalar_tensor_tensor(out=tgtf[:, :], in0=pad[:, :], scalar=trash[:, 0:1], in1=tokf[:, :],
                                            op0=ALU.mult, op1=ALU.add))
                do(dve.tensor_copy(target[:, :], tgtf[:, :]))


_INS = ['x', 'ctx_1024', 'g_xattn', 'g_ffn', 'L0_xattn_gamma_media', 'L0_xattn_beta_media', 'L0_xattn_gamma_lat',
        'L0_xattn_beta_lat', 'L0_xattn_Wq', 'L0_xattn_bq', 'L0_xattn_Wkv', 'L0_xattn_bkv', 'L0_xattn_Wo',
        'L0_xattn_bo', 'L0_ffn_Wg', 'L0_ffn_bg', 'L0_ffn_W1', 'L0_ffn_b1', 'L0_ffn_W2', 'L0_ffn_b2']


def kernel(**inputs):
    import numpy as np
    import concourse.bacc as bacc
    from concourse.bass_utils import run_bass_kernel_spmd

    nc = bacc.Bacc("TRN2", target_bir_lowering=False, num_devices=1)
    arrays, aps = {}, {}
    for name in _INS:
        a = np.ascontiguousarray(inputs[name])
        arrays["in_" + name] = a
        aps[name] = nc.dram_tensor("in_" + name, a.shape, mybir.dt.from_np(a.dtype), kind="ExternalInput").ap()
    aps["out"] = nc.dram_tensor("out_rows", (TOKENS + P, D), F32, kind="ExternalOutput").ap()
    build(nc, aps)
    got = run_bass_kernel_spmd(nc, [arrays], core_ids=[0]).results[0]["out_rows"]
    return got[0:TOKENS].reshape(B, T, D)
```

```python
from contextlib import ExitStack

import concourse.bass as bass
from concourse import mybir

F32 = mybir.dt.float32
F32R = mybir.dt.float32r
BF16 = mybir.dt.bfloat16
I32 = mybir.dt.int32
U32 = mybir.dt.uint32
ALU = mybir.AluOpType
ACT = mybir.ActivationFunctionType
AX_X = mybir.AxisListType.X

P = 128
B, T, D = 16, 256, 256
H, DH = 8, 128
INNER = H * DH
KEYS = 2 * T
E, F, TOP = 8, 1024, 2
TEMP = 1.0 + 1e-06
EPS = 1e-5
SCALE = float(DH) ** -0.5
KD = D // P
TT = T // P
JT = KEYS // P
STEPS = B * H
TOKENS = B * T
TOK_TILES = TOKENS // P
PAIRS = TOKENS * TOP
N_TILES = (PAIRS + E * (P - 1)) // P
ROW = D + E
HALF = INNER // 2
FH = F // 2
PIECE = 1024
PIECES = (KD * E * FH + FH // P * E * D) // PIECE
NX, NY, NO, NW, NSTAGE = 4, 3, 2, 4, 6
RING = 3

A_STEP = 6
B_STEP = 0
Z_STEP = 2
R_STEP = 1
T_STEP = 3
G_STEP = 4
W_STEP = 5


def plan_units():
    before = [("z", (0, k)) for k in range(KD)] + [("k", 0), ("q", 0)] + [("v", (0, w)) for w in range(JT)]
    steps = []
    for i in range(STEPS + H):
        units = []
        if i + 1 < STEPS:
            units += [("k", i + 1), ("q", i + 1)]
        m, w = (i - 1) // JT + 1, (i - 1) % JT
        if i and m < 2 * B:
            units.append(("v", (m, w)))
        if 1 <= i <= STEPS:
            units.append(("o", i - 1))
        b, h = i // H, i % H
        if h == Z_STEP and b + 1 < B:
            units += [("z", (b + 1, k)) for k in range(KD)]
        if h == T_STEP and b >= 1:
            units.append(("t", b - 1))
        if h == G_STEP and b >= 1:
            units.append(("g", b - 1))
        steps.append(units)
    return before, steps


class Later:

    def __init__(self, eng, sem):
        self.eng, self.sem, self.n = eng, sem, 0

    def mark(self, instruction):
        self.n += 1
        instruction.then_inc(self.sem, 1)

    def wait(self):
        self.eng.wait_ge(self.sem, self.n)


def product(pe, out, left, right, start, stop, **kw):
    (lh, ll), (rh, rl) = left, right
    pe.matmul(out, ll, rh, start=start, stop=False, **kw)
    pe.matmul(out, lh, rl, start=False, stop=False, **kw)
    return pe.matmul(out, lh, rh, start=False, stop=stop, **kw)


def build(nc, A):
    before, steps = plan_units()
    order = before + [u for s in steps for u in s]
    number = {u: n for n, u in enumerate(order)}
    hi_order = [u for u in order if u[0] in "kqvo"]
    hi_number = {u: n for n, u in enumerate(hi_order)}
    read_number = {u: n for group in ("zt", "kqvog")
                   for n, u in enumerate(u for u in order if u[0] in group)}

    with ExitStack() as top:
        def sem(name):
            return top.enter_context(nc.semaphore(name))

        def alloc(stack, name, shape, dt=F32):
            return stack.enter_context(nc.sbuf_tensor(name, shape, dt))

        ident = alloc(top, "ident", [P, P])
        onehot = alloc(top, "onehot", [P, TOP, E, TOK_TILES])
        iota8 = alloc(top, "iota8", [P, E])

        with ExitStack() as first:
            early = dict(
                wkv=[alloc(first, f"wkv_{s}", [P, KD, 2 * INNER], F32R) for s in ("hi", "lo")],
                wq=[alloc(first, f"wq_{s}", [P, KD, INNER], F32R) for s in ("hi", "lo")],
                kvt=[[alloc(first, f"kvt{i}_{s}", [P, KD, KEYS], F32R) for s in ("hi", "lo")] for i in range(2)],
                zt=alloc(first, "zt", [P, KD, KEYS]),
                z=alloc(first, "z", [P, JT, D]),
            )
        with ExitStack() as second:
            raw = alloc(second, "w_raw", [P, PIECES, PIECE])
        work = dict(
            b1=alloc(top, "b1", [P, E * FH]),
            b2=alloc(top, "b2", [P, E * D]),
            xg=[alloc(top, f"xg{i}", [P, ROW]) for i in range(NX)],
            xt=[[alloc(top, f"xt{i}_{s}", [P, KD, P], F32R) for s in ("hi", "lo")] for i in range(2)],
            hb=alloc(top, "hb", [P, FH]),
            ha=alloc(top, "ha", [P, FH]),
            ht=[[alloc(top, f"ht{i}_{s}", [P, FH // P, P], F32R) for s in ("hi", "lo")] for i in range(2)],
            y1=[alloc(top, f"y1_{i}", [P, D]) for i in range(NY)],
            ysum=alloc(top, "ysum", [P, D]),
            yo=[alloc(top, f"yo{i}", [P, D]) for i in range(NO)],
            stage=[alloc(top, f"stage{i}", [P, PIECE]) for i in range(NSTAGE)],
            wcol=alloc(top, "wcol", [P, NW]),
            wjunk=alloc(top, "wjunk", [P, E]),
            token=alloc(top, "token", [P, N_TILES], I32),
            target=alloc(top, "target", [P, N_TILES], I32),
            expert=alloc(top, "expert", [P, N_TILES], I32),
            mine=alloc(top, "mine", [P, N_TILES, E]),
        )
        xhat_dram = nc.dram_tensor("xhat_rows", (TOKENS, ROW), F32, kind="Internal").ap()
        half_dram = nc.dram_tensor("half_sums", (N_TILES, P, D), F32, kind="Internal").ap()
        sems = dict(
            w=[sem(f"piece_in{i}") for i in range(PIECES)],
            x2st=[sem(f"x2_stored{i}") for i in range(2)],
            rowst=[sem(f"rows_stored{i}") for i in range(2)],
            trash=sem("trash_stored"),
        )
        attention(nc, A, sem, sems, alloc, early, raw, ident, onehot, iota8, xhat_dram,
                  before, steps, number, hi_number, read_number)
        experts(nc, A, sem, sems, alloc, work, raw, ident, onehot, iota8, xhat_dram, half_dram)


def piece_views(A, half, j):
    if j < PIECES // 2:
        per = PIECE // FH
        k, c = divmod(j, E // per)
        src = A["L0_ffn_W1"][c * per:(c + 1) * per, k * P:(k + 1) * P, half * FH:(half + 1) * FH]
        return src.rearrange("e p f -> p e f"), 0, (k, slice(c * PIECE, (c + 1) * PIECE)), per
    per = PIECE // D
    g, c = divmod(j - PIECES // 2, E // per)
    src = A["L0_ffn_W2"][c * per:(c + 1) * per, half * FH + g * P:half * FH + (g + 1) * P, :]
    return src.rearrange("e p d -> p e d"), 1, (g, slice(c * PIECE, (c + 1) * PIECE)), per


def load_piece(sp, A, half, j, dst, done):
    src, _, _, per = piece_views(A, half, j)
    sp.dma_start(dst.rearrange("p (e n) -> p e n", e=per), src).then_inc(done, 16)


def attention(nc, A, sem, sems, alloc, early, raw, ident, onehot, iota8, xhat_dram, before, steps, number, hi_number, read_number):
    with ExitStack() as ctx:
        def sb(name, shape, dt=F32):
            return alloc(ctx, name, shape, dt)

        def bank(name):
            return ctx.enter_context(nc.psum_tensor(name, [P, 512], F32))

        wkv, wq, kvt, zt, z = (early[n] for n in ("wkv", "wq", "kvt", "zt", "z"))
        wo = [sb(f"wo_{s}", [P, H, D], F32R) for s in ("hi", "lo")]
        wg = sb("wg", [P, KD, E])
        bq = sb("bq", [P, H])
        bk = sb("bk", [P, H])
        bv = sb("bv", [P, H])
        gamma = sb("gamma", [P, 2, KD])
        beta = sb("beta", [P, 2, KD])
        bo = sb("bo", [P, TT, D])
        bg = sb("bg", [P, E])
        gate = sb("gate", [P, 2])
        tgate = sb("tgate", [P, 2])
        minus_half = sb("minus_half", [P, 4])
        x_raw = [sb(f"x_raw{i}", [P, TT, D]) for i in range(3)]
        c_raw = [sb(f"c_raw{i}", [P, TT, D]) for i in range(2)]
        xh = sb("xh", [P, TT, D])
        stats = {n: sb("stats_" + n, [P, 4, 6]) for n in "abc"}
        mv_a = sb("mv_a", [P, 4, 2])
        mv_b = sb("mv_b", [P, TT, 2])
        mv_c = sb("mv_c", [P, TT, 2])
        ve = {n: sb("ve_" + n, [P, 4]) for n in "abc"}
        rs_a = sb("rs_a", [P, 4])
        rs_b = sb("rs_b", [P, TT])
        rs_c = sb("rs_c", [P, TT])
        y = sb("y", [P, TT, D])
        x2 = [sb(f"x2_{i}", [P, TT, D]) for i in range(2)]
        rows = [sb(f"rows{i}", [P, TT, ROW]) for i in range(2)]
        x2t = sb("x2t", [P, KD, T])
        gates = sb("gates", [P, TT, E])
        top8 = sb("top8", [P, TT, 8])
        arg8 = sb("arg8", [P, TT, 8], U32)
        argf = sb("argf", [P, TT, TOP])
        gap = sb("gap", [P, TT])
        egap = sb("egap", [P, TT])
        wsum = sb("wsum", [P, TT])
        w12 = sb("w12", [P, TT, TOP])
        wtmp = sb("wtmp", [P, TT, E])
        smax = sb("smax", [P, 2, TT])
        nbias = sb("nbias", [P, 2, TT])
        ssum = sb("ssum", [P, 2, TT])
        rsum = sb("rsum", [P, 2, TT])

        with ExitStack() as raws:
            kv_raw = alloc(raws, "kv_raw", [P, KD, 2 * INNER])
            q_raw = alloc(raws, "q_raw", [P, KD, INNER])
            o_raw = alloc(raws, "o_raw", [P, H, D])
        v_sb = [[sb(f"v{i}_{s}", [P, JT, HALF], F32R) for s in ("hi", "lo")] for i in range(2)]
        pt = [sb(f"pt_{s}", [P, JT, T], F32R) for s in ("hi", "lo")]
        probs = [sb(f"probs{i}", [P, TT, KEYS]) for i in range(2)]
        kt = [[sb(f"kt{i}_{s}", [P, KEYS], F32R) for s in ("hi", "lo")] for i in range(2)]
        qt = [[sb(f"qt{i}_{s}", [P, T], F32R) for s in ("hi", "lo")] for i in range(2)]
        ot = [[sb(f"ot{i}_{s}", [P, T], F32R) for s in ("hi", "lo")] for i in range(2)]

        ring = [bank(f"ring{i}") for i in range(RING)]
        score = [bank(f"score{i}") for i in range(TT)]
        turn = [bank(f"turn{i}") for i in range(2)]
        proj = bank("proj")

        s_ident0, s_ident, s_const = sem("ident0"), sem("ident_ready"), sem("const")
        s_affine, s_bias, s_small = sem("affine_in"), sem("bias_in"), sem("small_in")
        s_win = {name: sem(name + "_in") for name in ("k0", "k1", "q0", "q1", "v0", "v1", "o0", "o1")}
        s_x = [sem(f"x_in{i}") for i in range(3)]
        s_c = [sem(f"c_in{i}") for i in range(2)]
        s_wg = sem("wg_in")
        s_whi = sem("weights_hi")
        s_wlo = {"dve": sem("weights_lo_dve"), "pool": sem("weights_lo_pool")}
        s_kvt0 = sem("kvt0_hi")
        s_tg = sem("tanh_gate")
        s_full = sem("unit_full")
        s_hi = sem("unit_hi")
        s_read = sem("unit_read")
        s_aread = sem("unit_read_act")
        s_score = sem("scores")
        s_max = sem("max")
        s_exp = sem("exp")
        s_rsum = sem("rsum")
        s_norm = sem("norm")
        s_turn = sem("turned")
        s_pthi, s_ptlo = sem("pt_hi"), sem("pt_lo")
        s_proj, s_projr = sem("projected"), sem("projection_read")
        s_mva, s_mvb, s_mvc = sem("mv_a"), sem("mv_b"), sem("mv_c")
        s_rsa, s_rsb, s_rsc = sem("rs_a"), sem("rs_b"), sem("rs_c")
        s_cused, s_xh, s_z = sem("media_used"), sem("xh_ready"), sem("z_ready")
        s_kvt, s_xn = sem("kvt_ready"), sem("xn_rows")
        s_x2, s_rows, s_gap, s_egap = sem("x2"), sem("rows"), sem("gap"), sem("egap")
        s_x2st, s_rowst, s_trash = sems["x2st"], sems["rowst"], sems["trash"]
        s_trashz = sem("trash_zero")
        s_dve, s_pool = sem("dve_self"), sem("pool_self")

        N_AFFINE, N_BIAS, N_SMALL = 4, 3, TT + 3

        def wait_read(eng, unit):
            eng.wait_ge(s_aread if unit[0] in "zt" else s_read, read_number[unit] + 1)

        ov = A["out"][0:TOKENS, :].rearrange("(b t p) d -> b p t d", t=TT, p=P)
        rv = xhat_dram.rearrange("(b t p) d -> b p t d", t=TT, p=P)

        pieces = []
        for c, name in enumerate("kv"):
            cols = slice(c * INNER, (c + 1) * INNER)
            for k in range(KD):
                pieces.append((name + str(k), A["L0_xattn_Wkv"][k * P:(k + 1) * P, cols], kv_raw[:, k, cols],
                               [w[:, k, cols] for w in wkv], "dve" if name == "k" else "pool"))
        for k in range(KD):
            pieces.insert(KD + k, ("q" + str(k), A["L0_xattn_Wq"][k * P:(k + 1) * P, :], q_raw[:, k, :],
                                   [w[:, k, :] for w in wq], "dve"))
        for c in range(2):
            heads = slice(c * H // 2, (c + 1) * H // 2)
            pieces.append(("o" + str(c), A["L0_xattn_Wo"][c * INNER // 2:(c + 1) * INNER // 2, :]
                           .rearrange("(h p) n -> p h n", p=P), o_raw[:, heads, :], [w[:, heads, :] for w in wo], "dve"))

        def hi_weights(act, kinds):
            for name, _, raw, (hi, _), _ in pieces:
                if name[0] in kinds:
                    act.wait_ge(s_win[name], 16)
                    act.activation(hi, raw, ACT.Copy).then_inc(s_whi, 1)

        def lo_weights(eng, who, kind):
            for n, (name, _, raw, (hi, lo), by) in enumerate(pieces):
                if name[0] == kind and by == who:
                    eng.wait_ge(s_whi, n + 1)
                    eng.tensor_tensor(lo, raw, hi.bitcast(F32), ALU.subtract).then_inc(s_wlo[who], 1)

        def weights_split(eng, kind):
            by = [p[4] for p in pieces]
            last = max(n for n, p in enumerate(pieces) if p[0][0] == kind)
            eng.wait_ge(s_wlo[by[last]], by[:last + 1].count(by[last]))

        order = before + [u for s in steps for u in s]

        with nc.Block() as block:
            @block.sync
            def _(sp):
                def load(c):
                    if c >= 3:
                        sp.wait_ge(s_x2, c - 2)
                    sp.dma_start(x_raw[c % 3][:, :, :],
                                 A["x"][c].rearrange("(t p) d -> p t d", p=P)).then_inc(s_x[c % 3], 16)
                    if c >= 2:
                        sp.wait_ge(s_cused, c - 1)
                    sp.dma_start(c_raw[c % 2][:, :, :],
                                 A["ctx_1024"][c].rearrange("(t p) d -> p t d", p=P)).then_inc(s_c[c % 2], 16)

                def load_weights(kinds):
                    for name, src, raw, _, _ in pieces:
                        if name[0] in kinds:
                            sp.dma_start(raw, src).then_inc(s_win[name], 16)

                load(0)
                load_weights("k")
                with nc.allow_non_contiguous_dma(reason="columns of vectors"):
                    for k, (g, b_) in enumerate((("gamma_media", "beta_media"), ("gamma_lat", "beta_lat"))):
                        sp.dma_start(gamma[:, k, :], A["L0_xattn_" + g].rearrange("(k p) -> p k", p=P)).then_inc(s_affine, 16)
                        sp.dma_start(beta[:, k, :], A["L0_xattn_" + b_].rearrange("(k p) -> p k", p=P)).then_inc(s_affine, 16)
                load_weights("q")
                with nc.allow_non_contiguous_dma(reason="columns of vectors"):
                    bkv = A["L0_xattn_bkv"]
                    sp.dma_start(bk[:, :], bkv[0:INNER].rearrange("(h p) -> p h", p=P)).then_inc(s_bias, 16)
                    sp.dma_start(bq[:, :], A["L0_xattn_bq"].rearrange("(h p) -> p h", p=P)).then_inc(s_bias, 16)
                    sp.dma_start(bv[:, :], bkv[INNER:].rearrange("(h p) -> p h", p=P)).then_inc(s_bias, 16)
                load_weights("v")
                load(1)
                load_weights("o")
                sp.dma_start(wg[:, :, :], A["L0_ffn_Wg"].rearrange("(k p) e -> p k e", p=P)).then_inc(s_wg, 16)
                for t in range(TT):
                    sp.dma_start(bo[:, t, :], A["L0_xattn_bo"].partition_broadcast(P)).then_inc(s_small, 16)
                sp.dma_start(bg[:, :], A["L0_ffn_bg"].partition_broadcast(P)).then_inc(s_small, 16)
                sp.dma_start(gate[:, 0:1], A["g_xattn"].partition_broadcast(P)).then_inc(s_small, 16)
                sp.dma_start(gate[:, 1:2], A["g_ffn"].partition_broadcast(P)).then_inc(s_small, 16)
                for b in range(B):
                    if b + 2 < B:
                        load(b + 2)
                    if b == B - 1:
                        for kind in "kqv":
                            sp.wait_ge(s_full, max(number[u] for u in number if u[0] == kind) + 1)
                        for j in range(PIECES):
                            load_piece(sp, A, 0, j, raw[:, j, :], sems["w"][j])
                    sp.wait_ge(s_x2, b + 1)
                    sp.dma_start(ov[b], x2[b % 2][:, :, :]).then_inc(s_x2st[b % 2], 16)
                    sp.wait_ge(s_rows, b + 1)
                    sp.dma_start(rv[b], rows[b % 2][:, :, :]).then_inc(s_rowst[b % 2], 16)
                sp.wait_ge(s_trashz, 1)
                sp.dma_start(A["out"][TOKENS:TOKENS + P, :], y[:, 0, :]).then_inc(s_trash, 16)
                sp.wait_ge(s_trash, 16)

            @block.gpsimd
            def _(pool):
                own = Later(pool, s_pool)
                pool.memset(ident[:, :], 0.0).then_inc(s_ident0, 1)
                pool.memset(minus_half[:, :], -0.5).then_inc(s_const, 1)
                pool.iota(iota8[:, :], [[1, E]], base=0, channel_multiplier=0,
                          allow_small_or_imprecise_dtypes=True).then_inc(s_const, 1)
                pool.wait_ge(s_ident0, 1)
                pool.affine_select(out=ident[:, :], in_=ident[:, :], compare_op=ALU.not_equal, fill=1.0,
                                   base=0, pattern=[[-1, P]], channel_multiplier=1).then_inc(s_ident, 1)
                pool.wait_ge(s_const, 2)

                def rstd(norm, out, mv, n, ready, count, done):
                    pool.wait_ge(ready, count)
                    own.mark(pool.tensor_scalar(ve[norm][:, 0:n], mv[:, 0:n, 1], EPS, 1.0, ALU.add, ALU.mult))
                    own.wait()
                    pool.tensor_tensor(out[:, 0:n], ve[norm][:, 0:n], minus_half[:, 0:n], ALU.pow).then_inc(done, 1)

                def negate(mv):
                    own.mark(pool.tensor_scalar(mv[:, :, 0], mv[:, :, 0], -1.0, 0.0, ALU.mult, ALU.add))

                def norm(out, src, mv, rs, n):
                    return pool.tensor_scalar(out, src, mv[:, n, 0:1], rs[:, n:n + 1], ALU.add, ALU.mult)

                def prepare_a(c):
                    rstd("a", rs_a, mv_a, 4, s_mva, c + 1, s_rsa)
                    negate(mv_a)
                    own.wait()
                    pool.wait_ge(s_rsa, c + 1)
                    if c:
                        pool.wait_ge(s_mvb, c)
                        pool.wait_ge(s_full, number["z", (c - 1, KD - 1)] + 1)
                    for t in range(TT):
                        last = norm(xh[:, t, :], x_raw[c % 3][:, t, :], mv_a, rs_a, t)
                    last.then_inc(s_xh, 1)
                    for t in range(TT):
                        last = norm(z[:, t, :], c_raw[c % 2][:, t, :], mv_a, rs_a, TT + t)
                    last.then_inc(s_cused, 1)

                def prepare_b(c):
                    rstd("b", rs_b, mv_b, TT, s_mvb, c + 1, s_rsb)
                    negate(mv_b)
                    own.wait()
                    pool.wait_ge(s_rsb, c + 1)
                    for t in range(TT):
                        last = norm(z[:, TT + t, :], xh[:, t, :], mv_b, rs_b, t)
                    last.then_inc(s_z, 1)

                def norm_rows(b):
                    rstd("c", rs_c, mv_c, TT, s_mvc, b + 1, s_rsc)
                    negate(mv_c)
                    own.wait()
                    pool.wait_ge(s_rsc, b + 1)
                    if b >= 2:
                        pool.wait_ge(s_rowst[b % 2], 16 * (b // 2))
                    for t in range(TT):
                        last = norm(rows[b % 2][:, t, 0:D], x2[b % 2][:, t, :], mv_c, rs_c, t)
                    last.then_inc(s_xn, 1)

                def split_kv(c):
                    wait_read(pool, ("z", (c, KD - 1)))
                    if c >= 2:
                        pool.wait_ge(s_full, number["q", H * (c - 1) - 1] + 1)
                        pool.wait_ge(s_full, number["v", (2 * (c - 2) + 1, JT - 1)] + 1)
                    hi, lo = kvt[c % 2]
                    own.mark(pool.tensor_copy(hi[:, :, :], zt[:, :, :]))
                    own.wait()
                    pool.tensor_tensor(lo[:, :, :], zt[:, :, :], hi[:, :, :].bitcast(F32), ALU.subtract)\
                        .then_inc(s_kvt, 1)

                def normalise(n):
                    pool.wait_ge(s_rsum, n + 1)
                    for t in range(TT):
                        last = pool.tensor_scalar(probs[n % 2][:, t, :], probs[n % 2][:, t, :],
                                                  rsum[:, n % 2, t:t + 1], 1.0, ALU.mult, ALU.mult)
                    last.then_inc(s_norm, 1)

                prepare_a(0)
                prepare_b(0)
                lo_weights(pool, "pool", "v")
                prepare_a(1)
                for i in range(STEPS + H):
                    b, h = i // H, i % H
                    if i < STEPS:
                        normalise(i)
                    if h == A_STEP and b + 2 < B:
                        prepare_a(b + 2)
                    if h == B_STEP and b + 1 < B:
                        prepare_b(b + 1)
                    if h == Z_STEP and b + 1 < B:
                        split_kv(b + 1)
                    if h == R_STEP and b >= 1:
                        norm_rows(b - 1)

            @block.scalar
            def _(act):
                hi_weights(act, "kqv")
                act.wait_ge(s_affine, 16 * N_AFFINE)

                def hi_part(kind, at):
                    n = number[kind, at]
                    src = ring[n % RING]
                    act.wait_ge(s_full, n + 1)
                    if kind == "k":
                        ins = act.activation(kt[at % 2][0][:, :], src[:, :], ACT.Identity, bias=bk[:, at % H:at % H + 1])
                    elif kind == "q":
                        ins = act.activation(qt[at % 2][0][:, :], src[:, 0:T], ACT.Identity, bias=bq[:, at % H:at % H + 1])
                    elif kind == "o":
                        ins = act.activation(ot[at % 2][0][:, :], src[:, 0:T], ACT.Identity, bias=bv[:, at % H:at % H + 1])
                    else:
                        m, w = at
                        ins = act.activation(v_sb[m % 2][0][:, w, :], src[:, :], ACT.Copy)
                    ins.then_inc(s_hi, 1)

                def exp(n, t):
                    act.wait_ge(s_max, n + 1)
                    act.activation(probs[n % 2][:, t, :], score[t][:, :], ACT.Exp, scale=SCALE,
                                   bias=nbias[:, n % 2, t:t + 1],
                                   accum_out=ssum[:, n % 2, t:t + 1]).then_inc(s_exp, 1)

                def read_unit(kind, at):
                    n = number[kind, at]
                    src = ring[n % RING]
                    act.wait_ge(s_full, n + 1)
                    if kind == "z":
                        c, k = at
                        if c:
                            act.wait_ge(s_kvt, c)
                        for s in range(2):
                            last = act.activation(zt[:, k, s * T:(s + 1) * T], src[:, s * T:(s + 1) * T], ACT.Identity,
                                                  scale=gamma[:, s, k:k + 1], bias=beta[:, s, k:k + 1])
                    else:
                        last = act.activation(x2t[:, :, :], src[:, :].rearrange("p (k t) -> p k t", k=KD), ACT.Copy)
                    last.then_inc(s_aread, 1)

                for n, u in enumerate(before):
                    if n == KD:
                        act.wait_ge(s_aread, KD)
                        act.activation(kvt[0][0][:, :, :], zt[:, :, :], ACT.Copy).then_inc(s_kvt0, 1)
                        hi_weights(act, "o")
                        act.wait_ge(s_bias, 16 * N_BIAS)
                    hi_part(*u) if u in hi_number else read_unit(*u)
                act.wait_ge(s_small, 16 * N_SMALL)
                act.activation(tgate[:, :], gate[:, :], ACT.Tanh).then_inc(s_tg, 1)
                for i in range(STEPS + H):
                    units = [u for u in steps[i] if u in hi_number]
                    if 1 <= i <= STEPS:
                        for t in range(2):
                            act.wait_ge(s_turn, 2 * (i - 1) + t + 1)
                            act.activation(pt[0][:, 2 * t:2 * t + 2, :],
                                           turn[t][:, :].rearrange("p (j i) -> p j i", j=2), ACT.Copy).then_inc(s_pthi, 1)
                    for u in units:
                        if u[0] == "k":
                            hi_part(*u)
                    if i < STEPS:
                        exp(i, 0)
                        exp(i, 1)
                    for u in units:
                        if u[0] != "k":
                            hi_part(*u)
                    for u in steps[i]:
                        if u[0] in "zt":
                            read_unit(*u)
                    if i % H == W_STEP and i // H >= 1:
                        b = i // H - 1
                        act.wait_ge(s_gap, b + 1)
                        act.activation(egap[:, :], gap[:, :], ACT.Exp).then_inc(s_egap, 1)

            @block.tensor
            def _(pe):
                def unit(kind, at):
                    n = number[kind, at]
                    dst = ring[n % RING]
                    if n >= RING:
                        wait_read(pe, order[n - RING])
                    if kind in "kq":
                        b, h = at // H, at % H
                        pe.wait_ge(s_kvt, b + 1)
                        w, c0, width = (wkv, 0, KEYS) if kind == "k" else (wq, T, T)
                        for k in range(KD):
                            last = product(pe, dst[:, 0:width], [s[:, k, h * DH:(h + 1) * DH] for s in w],
                                           [s[:, k, c0:c0 + width] for s in kvt[b % 2]], k == 0, k == KD - 1)
                    elif kind == "v":
                        m, w = at
                        b, half = m // 2, m % 2
                        pe.wait_ge(s_kvt, b + 1)
                        c0 = INNER + half * HALF
                        for k in range(KD):
                            last = product(pe, dst[:, :], [s[:, k, w * P:(w + 1) * P] for s in kvt[b % 2]],
                                           [s[:, k, c0:c0 + HALF] for s in wkv], k == 0, k == KD - 1)
                    elif kind == "o":
                        m, h4 = at // JT, at % JT
                        pe.wait_ge(s_ptlo, 2 * (at + 1))
                        wait_read(pe, ("v", (m, JT - 1)))
                        for j in range(JT):
                            last = product(pe, dst[:, 0:T], [s[:, j, h4 * DH:(h4 + 1) * DH] for s in v_sb[m % 2]],
                                           [s[:, j, :] for s in pt], j == 0, j == JT - 1)
                    elif kind == "z":
                        c, k = at
                        pe.wait_ge(s_z, c + 1)
                        for j in range(JT):
                            last = pe.transpose(dst[:, j * P:(j + 1) * P], z[:, j, k * P:(k + 1) * P], ident[:, :])
                    elif kind == "t":
                        pe.wait_ge(s_rsc, at + 1)
                        pe.wait_ge(s_xn, at + 1)
                        for k in range(KD):
                            for t in range(TT):
                                last = pe.transpose(dst[:, (k * TT + t) * P:(k * TT + t + 1) * P],
                                                    rows[at % 2][:, t, k * P:(k + 1) * P], ident[:, :])
                    else:
                        pe.wait_ge(s_wg, 16)
                        wait_read(pe, ("t", at))
                        for t in range(TT):
                            for k in range(KD):
                                last = pe.matmul(dst[:, t * E:(t + 1) * E], x2t[:, k, t * P:(t + 1) * P],
                                                 wg[:, k, :], start=k == 0, stop=k == KD - 1)
                    last.then_inc(s_full, 1)

                def scores(n):
                    wait_read(pe, ("q", n))
                    if n:
                        pe.wait_ge(s_exp, TT * n)
                    for t in range(TT):
                        product(pe, score[t][:, :], [s[:, t * P:(t + 1) * P] for s in qt[n % 2]],
                                [s[:, :] for s in kt[n % 2]], True, True).then_inc(s_score, 1)

                def turn_probs(n):
                    pe.wait_ge(s_norm, n + 1)
                    if n:
                        pe.wait_ge(s_ptlo, 2 * n)
                    for t in range(2):
                        for j in range(2):
                            for q in range(TT):
                                last = pe.transpose(turn[t][:, j * T + q * P:j * T + (q + 1) * P],
                                                    probs[n % 2][:, q, (2 * t + j) * P:(2 * t + j + 1) * P], ident[:, :])
                        last.then_inc(s_turn, 1)

                def out_proj(n):
                    b, h = n // H, n % H
                    wait_read(pe, ("o", n))
                    if h == 0 and b:
                        pe.wait_ge(s_projr, b)
                    for t in range(TT):
                        last = product(pe, proj[:, t * D:(t + 1) * D], [s[:, t * P:(t + 1) * P] for s in ot[n % 2]],
                                       [s[:, h, :] for s in wo], h == 0 and t == 0, h == H - 1,
                                       skip_group_check=True)
                    if h == H - 1:
                        last.then_inc(s_proj, 1)

                pe.wait_ge(s_ident, 1)
                for u in before:
                    if u[0] != "z":
                        weights_split(pe, u[0])
                    unit(*u)
                for i in range(STEPS + H):
                    if i == 1:
                        weights_split(pe, "o")
                    if i < STEPS:
                        scores(i)
                    if 1 <= i <= STEPS:
                        turn_probs(i - 1)
                    for u in steps[i]:
                        if u[0] in "kqov":
                            unit(*u)
                    if 2 <= i <= STEPS + 1:
                        out_proj(i - 2)
                    for u in steps[i]:
                        if u[0] in "ztg":
                            unit(*u)

            @block.vector
            def _(dve):
                own = Later(dve, s_dve)

                def moments(name, tiles, mv, done, used, turn):
                    dve.wait_ge(used, turn)
                    for n, t in enumerate(tiles):
                        own.mark(dve.bn_stats(stats[name][:, n, :], t))
                    own.wait()
                    for n in range(len(tiles)):
                        last = dve.bn_aggr(mv[:, n, :], stats[name][:, n, :])
                    last.then_inc(done, 1)

                def prepare_a(c):
                    dve.wait_ge(s_x[c % 3], 16 * (c // 3 + 1))
                    dve.wait_ge(s_c[c % 2], 16 * (c // 2 + 1))
                    moments("a", [x_raw[c % 3][:, t, :] for t in range(TT)] + [c_raw[c % 2][:, t, :] for t in range(TT)],
                            mv_a, s_mva, s_cused, c)

                def prepare_b(c):
                    dve.wait_ge(s_xh, c + 1)
                    moments("b", [xh[:, t, :] for t in range(TT)], mv_b, s_mvb, s_z, c)

                def read_unit(kind, at):
                    n = number[kind, at]
                    src = ring[n % RING]
                    if (kind, at) in hi_number:
                        dve.wait_ge(s_hi, hi_number[kind, at] + 1)
                        if kind == "k":
                            hi, lo = kt[at % 2]
                            bias, part = bk[:, at % H:at % H + 1], src[:, :]
                        elif kind == "q":
                            hi, lo = qt[at % 2]
                            bias, part = bq[:, at % H:at % H + 1], src[:, 0:T]
                        elif kind == "o":
                            hi, lo = ot[at % 2]
                            bias, part = bv[:, at % H:at % H + 1], src[:, 0:T]
                        if kind == "v":
                            m, w = at
                            hi, lo = v_sb[m % 2]
                            dve.tensor_tensor(lo[:, w, :], src[:, :], hi[:, w, :].bitcast(F32), ALU.subtract)\
                                .then_inc(s_read, 1)
                        else:
                            dve.scalar_tensor_tensor(out=lo[:, :], in0=part, scalar=bias, in1=hi[:, :].bitcast(F32),
                                                     op0=ALU.add, op1=ALU.subtract).then_inc(s_read, 1)
                        return
                    dve.wait_ge(s_full, n + 1)
                    route(at, src, read_number[kind, at])

                def route(b, src, n):
                    g3 = src[:, 0:TT * E].rearrange("p (t e) -> p t e", t=TT)
                    dve.tensor_tensor(gates[:, :, :], g3, bg[:, :].unsqueeze(1).to_broadcast([P, TT, E]), ALU.add)\
                        .then_inc(s_read, 1)
                    dve.wait_ge(s_read, n + 1)
                    own.mark(dve.tensor_scalar(gates[:, :, :], gates[:, :, :], 1.0 / TEMP, None, ALU.mult))
                    own.wait()
                    for t in range(TT):
                        own.mark(dve.max(top8[:, t, :], gates[:, t, :]))
                    own.wait()
                    if b:
                        dve.wait_ge(s_egap, b)
                    dve.tensor_tensor(gap[:, :], top8[:, :, 1], top8[:, :, 0], ALU.subtract).then_inc(s_gap, 1)
                    for t in range(TT):
                        own.mark(dve.max_index(arg8[:, t, :], top8[:, t, :], gates[:, t, :]))
                    own.wait()
                    own.mark(dve.tensor_copy(argf[:, :, :], arg8[:, :, 0:TOP]))
                    own.wait()
                    for k in range(TOP):
                        for t in range(TT):
                            own.mark(dve.tensor_scalar(onehot[:, k, :, TT * b + t], iota8[:, :],
                                                       argf[:, t, k:k + 1], None, ALU.is_equal))
                    own.wait()

                def weigh(b):
                    dve.wait_ge(s_egap, b + 1)
                    own.mark(dve.tensor_scalar(wsum[:, :], egap[:, :], 1.0, None, ALU.add))
                    own.wait()
                    own.mark(dve.reciprocal(w12[:, :, 0], wsum[:, :]))
                    own.wait()
                    own.mark(dve.tensor_tensor(w12[:, :, 1], w12[:, :, 0], egap[:, :], ALU.mult))
                    own.wait()
                    own.mark(dve.tensor_scalar(w12[:, :, :], w12[:, :, :], tgate[:, 1:2], None, ALU.mult))
                    own.wait()
                    for t in range(TT):
                        own.mark(dve.tensor_scalar(wtmp[:, t, :], onehot[:, 0, :, TT * b + t], w12[:, t, 0:1], None, ALU.mult))
                    own.wait()
                    for t in range(TT):
                        last = dve.scalar_tensor_tensor(out=rows[b % 2][:, t, D:ROW], in0=onehot[:, 1, :, TT * b + t],
                                                        scalar=w12[:, t, 1:2], in1=wtmp[:, t, :],
                                                        op0=ALU.mult, op1=ALU.add)
                    last.then_inc(s_rows, 1)

                def residual(b):
                    dve.wait_ge(s_proj, b + 1)
                    dve.tensor_tensor(y[:, :, :], proj[:, :].rearrange("p (t d) -> p t d", t=TT), bo[:, :, :], ALU.add)\
                        .then_inc(s_projr, 1)
                    dve.wait_ge(s_projr, b + 1)
                    if b >= 2:
                        dve.wait_ge(s_x2st[b % 2], 16 * (b // 2))
                    dve.scalar_tensor_tensor(out=x2[b % 2][:, :, :], in0=y[:, :, :], scalar=tgate[:, 0:1],
                                             in1=x_raw[b % 3][:, :, :], op0=ALU.mult, op1=ALU.add).then_inc(s_x2, 1)
                    dve.wait_ge(s_x2, b + 1)
                    moments("c", [x2[b % 2][:, t, :] for t in range(TT)], mv_c, s_mvc, s_xn, b)

                def maximum(n):
                    for t in range(TT):
                        dve.wait_ge(s_score, TT * n + t + 1)
                        own.mark(dve.tensor_reduce(smax[:, n % 2, t:t + 1], score[t][:, :], AX_X, ALU.max))
                    own.wait()
                    dve.tensor_scalar(nbias[:, n % 2, :], smax[:, n % 2, :], -SCALE, None, ALU.mult).then_inc(s_max, 1)

                def reciprocal_sum(n):
                    dve.wait_ge(s_exp, TT * (n + 1))
                    dve.reciprocal(rsum[:, n % 2, :], ssum[:, n % 2, :]).then_inc(s_rsum, 1)

                prepare_a(0)
                lo_weights(dve, "dve", "k")
                prepare_b(0)
                lo_weights(dve, "dve", "q")
                dve.wait_ge(s_kvt0, 1)
                dve.tensor_tensor(kvt[0][1][:, :, :], zt[:, :, :], kvt[0][0][:, :, :].bitcast(F32), ALU.subtract)\
                    .then_inc(s_kvt, 1)
                prepare_a(1)
                lo_weights(dve, "dve", "o")
                dve.wait_ge(s_bias, 16 * N_BIAS)
                for u in before:
                    if u[0] not in "zt":
                        read_unit(*u)
                dve.wait_ge(s_small, 16 * N_SMALL)
                dve.wait_ge(s_tg, 1)
                dve.wait_ge(s_const, 2)
                for i in range(STEPS + H):
                    b, h = i // H, i % H
                    if i < STEPS:
                        maximum(i)
                    if 1 <= i <= STEPS:
                        for t in range(2):
                            dve.wait_ge(s_pthi, 2 * (i - 1) + t + 1)
                            dve.tensor_tensor(pt[1][:, 2 * t:2 * t + 2, :],
                                              turn[t][:, :].rearrange("p (j i) -> p j i", j=2),
                                              pt[0][:, 2 * t:2 * t + 2, :].bitcast(F32), ALU.subtract)\
                                .then_inc(s_ptlo, 1)
                    for u in steps[i]:
                        if u[0] in "kq":
                            read_unit(*u)
                    if i < STEPS:
                        reciprocal_sum(i)
                    for u in steps[i]:
                        if u[0] in "vog":
                            read_unit(*u)
                    if h == A_STEP and b + 2 < B:
                        prepare_a(b + 2)
                    if h == B_STEP and b + 1 < B:
                        prepare_b(b + 1)
                    if h == R_STEP and b >= 1:
                        residual(b - 1)
                    if h == W_STEP and b >= 1:
                        weigh(b - 1)
                dve.wait_ge(s_projr, B)
                dve.memset(y[:, 0, :], 0.0).then_inc(s_trashz, 1)


def experts(nc, A, sem, sems, alloc, work, raw, ident, onehot, iota8, xhat_dram, half_dram):
    with ExitStack() as ctx:
        def sb(name, shape, dt=F32):
            return alloc(ctx, name, shape, dt)

        def bank(name):
            return ctx.enter_context(nc.psum_tensor(name, [P, 512], F32))

        w1 = [sb(f"w1_{s}", [P, KD, E * FH], F32R) for s in ("hi", "lo")]
        w2_hi = sb("w2_hi", [P, FH // P, E * D], F32R)
        s_b1, s_b2 = sem("b1_in"), sem("b2_in")
        s_whi = sem("w_hi")
        s_wlo = {"pool": sem("w_lo_pool"), "dve": sem("w_lo_dve")}
        b1, b2 = work["b1"], work["b2"]

        def load_b1(sp, half):
            sp.dma_start(b1[:, :].rearrange("p (e f) -> p e f", e=E),
                         A["L0_ffn_b1"][:, half * FH:(half + 1) * FH].partition_broadcast(P)).then_inc(s_b1, 16)

        lo_of = [w1[1]]
        lo_by = [["pool" if j < PIECES // 2 or j in (10, 13) else "dve" for j in range(PIECES)],
                 ["pool" if j in (1, 4, 8, 11) else "dve" for j in range(PIECES)]]
        lo_count = {}
        made = {"pool": 0, "dve": 0}
        for half in range(2):
            for j in range(PIECES):
                made[lo_by[half][j]] += 1
                lo_count[half, j] = made[lo_by[half][j]]

        def staged(j):
            return j % (PIECES // 2) < NSTAGE

        def source(half, j):
            if half == 0:
                return raw[:, j, :]
            if staged(j):
                return work["stage"][j % (PIECES // 2)][:, :]
            _, which, (k, cols), _ = piece_views(A, half, j)
            return lo_of[which][:, k, cols].bitcast(F32)

        def arrived(half, j):
            return 16 * (half + 1)

        def hi_piece(act, half, j):
            _, which, (k, cols), _ = piece_views(A, half, j)
            act.wait_ge(sems["w"][j], arrived(half, j))
            act.activation((w1[0], w2_hi)[which][:, k, cols], source(half, j), ACT.Copy).then_inc(s_whi, 1)

        def lo_piece(eng, name, half, j, w2_lo=None):
            _, which, (k, cols), _ = piece_views(A, half, j)
            eng.wait_ge(s_whi, PIECES * half + j + 1)
            eng.tensor_tensor((w1[1], w2_lo)[which][:, k, cols], source(half, j),
                              (w1[0], w2_hi)[which][:, k, cols].bitcast(F32), ALU.subtract).then_inc(s_wlo[name], 1)

        def lo_made(eng, half, j):
            eng.wait_ge(s_wlo[lo_by[half][j]], lo_count[half, j])

        def raw_split(eng):
            for j in range(PIECES):
                lo_made(eng, 0, j)

        def routing_sync(sp):
            for j in range(4):
                lo_made(sp, 0, j)
            load_b1(sp, 0)
            for j in range(4, 6):
                lo_made(sp, 0, j)
            sp.dma_start(b2[:, :], A["L0_ffn_b2"].rearrange("e d -> (e d)").partition_broadcast(P)).then_inc(s_b2, 16)

        routing(nc, alloc, sem, onehot, iota8, work, routing_sync,
                [lambda act, j=j: hi_piece(act, 0, j) for j in range(PIECES)],
                [lambda pool, j=j: lo_piece(pool, "pool", 0, j) for j in range(PIECES // 2)])

        w2_lo = sb("w2_lo", [P, FH // P, E * D], F32R)
        lo_of.append(w2_lo)
        w2 = [w2_hi, w2_lo]
        xg, xt, hb, ha, ht, y1, ysum, yo, stage, wcol, wjunk = (
            work[n] for n in ("xg", "xt", "hb", "ha", "ht", "y1", "ysum", "yo", "stage", "wcol", "wjunk"))
        token, target, expert, mine = (work[n] for n in ("token", "target", "expert", "mine"))
        ph = [bank(f"ph{i}") for i in range(2)]
        pht = [bank(f"pht{i}") for i in range(2)]
        px = [bank(f"px{i}") for i in range(2)]
        py = [bank(f"py{i}") for i in range(2)]

        TURNS = 2 * N_TILES

        def expert_of(eng, u):
            return eng.value_load(expert[0:1, u % N_TILES:u % N_TILES + 1], min_val=0, max_val=E - 1)

        SOON = PIECES // 2 + 2
        LAG = 2
        s_g = [sem(f"gathered{i}") for i in range(NX)]
        s_y1st = [sem(f"y1_stored{i}") for i in range(NY)]
        s_y1ld = [sem(f"y1_loaded{i}") for i in range(NY)]
        s_px, s_xhi, s_xlo = sem("x_turned"), sem("xt_hi"), sem("xt_lo")
        s_ph, s_hb, s_ha = sem("hidden"), sem("hidden_bias"), sem("hidden_act")
        s_pht, s_hhi, s_hlo = sem("hidden_turned"), sem("ht_hi"), sem("ht_lo")
        s_py, s_pyr, s_w, s_yo = sem("y_sum"), sem("y_read"), sem("w_ready"), sem("y_out")
        s_add = sem("added")

        with nc.Block() as block:
            @block.sync
            def _(sp):
                def load(j):
                    load_piece(sp, A, 1, j, source(1, j), sems["w"][j])

                for u in range(TURNS):
                    t = u % N_TILES
                    if u == 0:
                        raw_split(sp)
                        for j in range(NSTAGE):
                            load(j)
                    if u == N_TILES - LAG:
                        sp.wait_ge(s_hb, N_TILES)
                        for j in range(NSTAGE, PIECES // 2):
                            load(j)
                        load_b1(sp, 1)
                    if u < N_TILES:
                        sp.wait_ge(s_pyr, u + 1)
                        sp.dma_start(half_dram[t], y1[u % NY][:, :]).then_inc(s_y1st[u % NY], 16)
                    if u == N_TILES - 1:
                        for j in range(PIECES // 2, PIECES):
                            if staged(j):
                                lo_made(sp, 1, j - PIECES // 2)
                            load(j)
                        for i in range(NY):
                            sp.wait_ge(s_y1st[i], 16 * len(range(i, N_TILES, NY)))
                    v = u + 2
                    if u >= N_TILES - 1 and v < TURNS + 1:
                        ahead = range(N_TILES, v + 1) if u == N_TILES - 1 else [v]
                        for r in ahead:
                            if r >= TURNS:
                                continue
                            n = r - N_TILES
                            if n >= NY:
                                sp.wait_ge(s_pyr, r - NY + 1)
                            sp.dma_start(y1[n % NY][:, :], half_dram[n]).then_inc(s_y1ld[n % NY], 16)

            @block.gpsimd
            def _(pool):
                def gather(u):
                    t = u % N_TILES
                    if u >= NX:
                        pool.wait_ge(s_px, u - NX + 1)
                        pool.wait_ge(s_w, u - NX + 1)
                    pool.indirect_dma_start(
                        out=xg[u % NX][:, :], out_offset=None, in_=xhat_dram,
                        in_offset=bass.IndirectOffsetOnAxis(ap=token[:, t:t + 1].bitcast(U32), axis=0),
                    ).then_inc(s_g[u % NX], 16)

                for i in range(2):
                    pool.wait_ge(sems["x2st"][i], 16 * (B // 2))
                    pool.wait_ge(sems["rowst"][i], 16 * (B // 2))
                pool.wait_ge(sems["trash"], 16)
                for u in range(NX - 1):
                    gather(u)
                for j in range(PIECES // 2, PIECES):
                    if lo_by[0][j] == "pool":
                        lo_piece(pool, "pool", 0, j, w2_lo)
                for u in range(TURNS + LAG):
                    if u == N_TILES:
                        for j in range(PIECES):
                            if j == 0:
                                pool.wait_ge(s_ph, N_TILES)
                            if j == PIECES // 2:
                                pool.wait_ge(s_py, N_TILES)
                            if lo_by[1][j] == "pool":
                                lo_piece(pool, "pool", 1, j, w2_lo)
                    if u + NX - 1 < TURNS:
                        gather(u + NX - 1)
                    t = u - LAG - N_TILES
                    if t >= 0:
                        pool.wait_ge(s_yo, t + 1)
                        if t:
                            pool.wait_ge(s_add, 16 * t)
                        pool.indirect_dma_start(
                            out=A["out"], out_offset=bass.IndirectOffsetOnAxis(ap=target[:, t:t + 1].bitcast(U32), axis=0),
                            in_=yo[t % NO][:, :], in_offset=None, compute_op=ALU.add,
                        ).then_inc(s_add, 16)
                pool.wait_ge(s_add, 16 * N_TILES)

            @block.tensor
            def _(pe):
                def turn_x(u):
                    pe.wait_ge(s_g[u % NX], 16 * (u // NX + 1))
                    if u >= 2:
                        pe.wait_ge(s_xlo, u - 1)
                    for k in range(KD):
                        last = pe.transpose(px[u % 2][:, k * P:(k + 1) * P], xg[u % NX][:, k * P:(k + 1) * P], ident[:, :])
                    last.then_inc(s_px, 1)

                def hidden(u, e):
                    pe.wait_ge(s_xlo, u + 1)
                    if u >= 2:
                        pe.wait_ge(s_hb, u - 1)
                    for k in range(KD):
                        last = product(pe, ph[u % 2][:, :], [s[:, k, :] for s in xt[u % 2]],
                                       [s[:, k, bass.ds(e * FH, FH)] for s in w1], k == 0, k == KD - 1)
                    last.then_inc(s_ph, 1)

                def turn_h(u):
                    pe.wait_ge(s_ha, u + 1)
                    if u >= 2:
                        pe.wait_ge(s_hlo, u - 1)
                    for g in range(FH // P):
                        last = pe.transpose(pht[u % 2][:, g * P:(g + 1) * P], ha[:, g * P:(g + 1) * P], ident[:, :])
                    last.then_inc(s_pht, 1)

                def out(u, e):
                    pe.wait_ge(s_hlo, u + 1)
                    if u >= 2:
                        pe.wait_ge(s_pyr, u - 1)
                    if u % N_TILES == 0:
                        for j in range(PIECES // 2, PIECES):
                            lo_made(pe, u // N_TILES, j)
                    for g in range(FH // P):
                        last = product(pe, py[u % 2][:, 0:D], [s[:, g, :] for s in ht[u % 2]],
                                       [s[:, g, bass.ds(e * D, D)] for s in w2], g == 0, g == FH // P - 1)
                    last.then_inc(s_py, 1)

                turn_x(0)
                e = {}
                for u in range(TURNS + LAG):
                    if u == N_TILES:
                        turn_x(u + 1)
                        turn_h(u - 1)
                        for v in range(u - LAG, u):
                            out(v, e[v])
                    if u < TURNS:
                        e[u] = expert_of(pe, u)
                        if u % N_TILES == 0:
                            for j in range(PIECES // 2):
                                lo_made(pe, u // N_TILES, j)
                        hidden(u, e[u])
                    if u == N_TILES:
                        continue
                    if u + 1 < TURNS:
                        turn_x(u + 1)
                    if 1 <= u <= TURNS:
                        turn_h(u - 1)
                    if u >= LAG and not N_TILES <= u < N_TILES + LAG:
                        out(u - LAG, e[u - LAG])

            @block.vector
            def _(dve):
                def lo_x(u):
                    dve.wait_ge(s_xhi, u + 1)
                    dve.tensor_tensor(xt[u % 2][1][:, :, :], px[u % 2][:, 0:D].rearrange("p (k t) -> p k t", k=KD),
                                      xt[u % 2][0][:, :, :].bitcast(F32), ALU.subtract).then_inc(s_xlo, 1)

                def finish(u, e):
                    t = u % N_TILES
                    dve.wait_ge(s_py, u + 1)
                    if u < N_TILES:
                        if u >= NY:
                            dve.wait_ge(s_y1st[u % NY], 16 * (u // NY))
                        dve.tensor_tensor(y1[u % NY][:, :], py[u % 2][:, 0:D], b2[:, bass.ds(e * D, D)], ALU.add)\
                            .then_inc(s_pyr, 1)
                        return
                    dve.wait_ge(s_y1ld[t % NY], 16 * (t // NY + 1))
                    if t:
                        dve.wait_ge(s_yo, t)
                    dve.tensor_tensor(ysum[:, :], py[u % 2][:, 0:D], y1[t % NY][:, :], ALU.add).then_inc(s_pyr, 1)
                    dve.wait_ge(s_pyr, u + 1)
                    if t >= NO:
                        dve.wait_ge(s_add, 16 * (t - NO + 1))
                    dve.tensor_scalar(yo[t % NO][:, :], ysum[:, :], wcol[:, u % NW:u % NW + 1], None, ALU.mult)\
                        .then_inc(s_yo, 1)

                for j in range(PIECES // 2, PIECES):
                    if lo_by[0][j] == "dve":
                        lo_piece(dve, "dve", 0, j, w2_lo)
                lo_x(0)
                dve.wait_ge(s_b1, 16)
                dve.wait_ge(s_b2, 16)
                def add_bias(u, e):
                    dve.wait_ge(s_ph, u + 1)
                    if u:
                        dve.wait_ge(s_ha, u)
                    dve.tensor_tensor(hb[:, :], ph[u % 2][:, :], b1[:, bass.ds(e * FH, FH)], ALU.add).then_inc(s_hb, 1)

                def take_weights(u):
                    dve.wait_ge(s_g[u % NX], 16 * (u // NX + 1))
                    if u:
                        dve.wait_ge(s_w, u)
                    if u >= N_TILES + NW:
                        dve.wait_ge(s_yo, u - N_TILES - NW + 1)
                    dve.scalar_tensor_tensor(out=wjunk[:, :], in0=xg[u % NX][:, D:ROW], scalar=1.0,
                                             in1=mine[:, u % N_TILES, :], op0=ALU.mult, op1=ALU.mult,
                                             accum_out=wcol[:, u % NW:u % NW + 1]).then_inc(s_w, 1)

                def lo_h(u):
                    if u == 0:
                        raw_split(dve)
                    dve.wait_ge(s_hhi, u + 1)
                    dve.tensor_tensor(ht[u % 2][1][:, :, :], pht[u % 2][:, :].rearrange("p (g t) -> p g t", g=FH // P),
                                      ht[u % 2][0][:, :, :].bitcast(F32), ALU.subtract).then_inc(s_hlo, 1)

                def second_lo(js):
                    for j in js:
                        if lo_by[1][j] == "dve":
                            lo_piece(dve, "dve", 1, j, w2_lo)

                e = {}
                for u in range(TURNS + LAG):
                    if u < TURNS:
                        e[u] = expert_of(dve, u)
                    if u == N_TILES:
                        lo_x(u + 1)
                        take_weights(u)
                        lo_h(u - 1)
                        for v in range(u - LAG, u):
                            finish(v, e[v])
                        second_lo(range(PIECES // 2))
                        dve.wait_ge(s_b1, 32)
                        add_bias(u, e[u])
                        continue
                    if u < TURNS:
                        add_bias(u, e[u])
                    if u + 1 < TURNS:
                        lo_x(u + 1)
                    if u < TURNS:
                        take_weights(u)
                    if 1 <= u <= TURNS:
                        lo_h(u - 1)
                    if u == N_TILES + 1:
                        second_lo(range(PIECES // 2, PIECES))
                    if u >= LAG and not N_TILES <= u < N_TILES + LAG:
                        finish(u - LAG, e[u - LAG])

            @block.scalar
            def _(act):
                def hi_x(u):
                    act.wait_ge(s_px, u + 1)
                    if u >= 2:
                        act.wait_ge(s_ph, u - 1)
                    act.activation(xt[u % 2][0][:, :, :], px[u % 2][:, 0:D].rearrange("p (k t) -> p k t", k=KD), ACT.Copy)\
                        .then_inc(s_xhi, 1)

                hi_x(0)
                for u in range(TURNS + 1):
                    if u + 1 < TURNS:
                        hi_x(u + 1)
                    if u:
                        v = u - 1
                        if v == 0:
                            raw_split(act)
                        act.wait_ge(s_pht, v + 1)
                        if v >= 2:
                            act.wait_ge(s_py, v - 1)
                        act.activation(ht[v % 2][0][:, :, :], pht[v % 2][:, :].rearrange("p (g t) -> p g t", g=FH // P),
                                       ACT.Copy).then_inc(s_hhi, 1)
                    if u == N_TILES:
                        for j in range(SOON):
                            if j == PIECES // 2:
                                act.wait_ge(s_py, N_TILES)
                            hi_piece(act, 1, j)
                    if u < TURNS:
                        act.wait_ge(s_hb, u + 1)
                        if u:
                            act.wait_ge(s_pht, u)
                        act.activation(ha[:, :], hb[:, :], ACT.Silu).then_inc(s_ha, 1)
                    if u == N_TILES + 1:
                        for j in range(SOON, PIECES):
                            hi_piece(act, 1, j)


def routing(nc, alloc, sem, onehot, iota8, work, sync_part, act_pieces, pool_pieces):
    token, target, expert, mine = (work[n] for n in ("token", "target", "expert", "mine"))
    EC = E * TOK_TILES
    NP = TOP * TOK_TILES
    with ExitStack() as ctx:
        def sb(name, shape, dt=F32):
            return alloc(ctx, name, shape, dt)

        def bank(name):
            return ctx.enter_context(nc.psum_tensor(name, [P, 512], F32))

        chosen = sb("chosen", [P, E, TOK_TILES])
        below = sb("below", [P, P])
        ones = sb("ones", [P, P])
        lane = sb("lane", [P, 1])
        iota_p = sb("iota_p", [P, P])
        totals = sb("totals", [P, E, TOK_TILES])
        run = sb("run", [P, E, TOK_TILES])
        zero = sb("zero", [P, EC])
        count = sb("count", [P, E])
        counti = sb("counti", [P, E], I32)
        tiles = sb("tiles", [P, E])
        first = sb("first", [P, E])
        shift = sb("shift", [P, E])
        place = sb("place", [P, E, TOK_TILES])
        mult = sb("mult", [P, E, TOK_TILES])
        slot = sb("slot", [P, TOP, TOK_TILES])
        sloti = sb("sloti", [P, NP], I32)
        part = sb("part", [P, 2, NP], I32)
        slot_tile = sb("slot_tile", [P, NP])
        slot_row = sb("slot_row", [P, NP])
        GRP = 8
        left = [sb(f"left{i}", [P, GRP, P], BF16) for i in range(2)]
        tile_eq = [sb(f"tile_eq{i}", [P, GRP, N_TILES], BF16) for i in range(2)]
        right = [sb(f"right{i}", [P, GRP, 3, N_TILES], BF16) for i in range(2)]
        tokf = sb("tokf", [P, N_TILES])
        tgtf = sb("tgtf", [P, N_TILES])
        pad = sb("pad", [P, N_TILES])
        trash = sb("trash", [P, 1])
        ge = sb("ge", [P, E, N_TILES])
        expf = sb("expf", [P, N_TILES])
        pc0, pc1, inv = bank("prefix"), bank("sums"), bank("inverse")

        s_k0, s_k1, s_ch, s_pre = sem("consts0"), sem("consts1"), sem("chosen"), sem("prefix")
        s_oh, s_inv, s_dve = sem("rows_cols"), sem("inverse_part"), sem("route_self")
        s_eq, s_cols = sem("tile_eq"), sem("cols")

        with nc.Block() as block:
            @block.sync
            def _(sp):
                sync_part(sp)

            @block.gpsimd
            def _(pool):
                pool.memset(below[:, :], 1.0).then_inc(s_k0, 1)
                pool.memset(ones[:, :], 1.0).then_inc(s_k1, 1)
                pool.iota(iota_p[:, :], [[1, P]], base=0, channel_multiplier=0,
                          allow_small_or_imprecise_dtypes=True).then_inc(s_k1, 1)
                pool.iota(lane[:, :], [[1, 1]], base=0, channel_multiplier=1,
                          allow_small_or_imprecise_dtypes=True).then_inc(s_k1, 1)
                pool.wait_ge(s_k0, 1)
                pool.affine_select(out=below[:, :], in_=below[:, :], compare_op=ALU.is_gt, fill=0.0,
                                   base=0, pattern=[[1, P]], channel_multiplier=-1).then_inc(s_k1, 1)
                for piece in pool_pieces:
                    piece(pool)

            @block.scalar
            def _(act):
                act.wait_ge(s_k1, 4)
                todo = list(act_pieces)
                for g in range(NP // GRP):
                    while todo and len(todo) > PIECES - 2 * (g + 1):
                        todo.pop(0)(act)
                    act.wait_ge(s_eq, g + 1)
                    if g >= 2:
                        act.wait_ge(s_inv, g - 1)
                    r = right[g % 2]
                    act.activation(r[:, :, 0, :], tile_eq[g % 2][:, :, :], ACT.Copy)
                    act.activation(r[:, :, 1, :], tile_eq[g % 2][:, :, :], ACT.Copy, scale=lane[:, 0:1])\
                        .then_inc(s_cols, 1)

            @block.tensor
            def _(pe):
                pe.wait_ge(s_k1, 4)
                pe.wait_ge(s_ch, 1)
                ch = chosen[:, :, :].rearrange("p e t -> p (e t)")
                pe.matmul(pc0[:, 0:EC], below[:, :], ch, start=True, stop=True)
                pe.matmul(pc1[:, 0:EC], ones[:, :], ch, start=True, stop=True).then_inc(s_pre, 1)
                for g in range(NP // GRP):
                    pe.wait_ge(s_oh, g + 1)
                    pe.wait_ge(s_cols, g + 1)
                    for j in range(GRP):
                        last = pe.matmul(inv[:, 0:3 * N_TILES], left[g % 2][:, j, :],
                                         right[g % 2][:, j, :, :].rearrange("p a t -> p (a t)"),
                                         start=g == 0 and j == 0, stop=g == NP // GRP - 1 and j == GRP - 1)
                    last.then_inc(s_inv, 1)

            @block.vector
            def _(dve):
                own = Later(dve, s_dve)

                def do(instruction):
                    own.mark(instruction)
                    own.wait()

                dve.tensor_tensor(chosen[:, :, :], onehot[:, 0], onehot[:, 1], ALU.add).then_inc(s_ch, 1)
                own.mark(dve.memset(zero[:, :], 0.0))
                dve.wait_ge(s_k1, 4)
                dve.wait_ge(s_pre, 1)
                flat = lambda a: a[:, :, :].rearrange("p e t -> p (e t)")
                do(dve.tensor_copy(flat(totals), pc1[:, 0:EC]))
                own.mark(dve.tensor_reduce(count[:, :], totals[:, :, :], AX_X, ALU.add))
                do(dve.tensor_tensor_scan(flat(run), flat(totals), zero[:, :], 0.0, ALU.add, ALU.add))
                do(dve.tensor_tensor(flat(run), flat(run), flat(totals), ALU.subtract))
                do(dve.tensor_scalar(counti[:, :], count[:, :], float(P - 1), None, ALU.add))
                do(dve.tensor_scalar(counti[:, :], counti[:, :], 7, None, ALU.logical_shift_right))
                do(dve.tensor_copy(tiles[:, :], counti[:, :]))
                do(dve.tensor_tensor_scan(first[:, :], tiles[:, :], zero[:, 0:E], 0.0, ALU.add, ALU.add))
                do(dve.tensor_tensor(first[:, :], first[:, :], tiles[:, :], ALU.subtract))
                do(dve.scalar_tensor_tensor(out=shift[:, :], in0=first[:, :], scalar=float(P), in1=run[:, :, 0],
                                            op0=ALU.mult, op1=ALU.subtract))
                do(dve.tensor_tensor(flat(place), pc0[:, 0:EC], flat(run), ALU.add))
                do(dve.tensor_tensor(place[:, :, :], place[:, :, :],
                                     shift[:, :].unsqueeze(2).to_broadcast([P, E, TOK_TILES]), ALU.add))
                for k in range(TOP):
                    do(dve.tensor_tensor(mult[:, :, :], place[:, :, :], onehot[:, k], ALU.mult))
                    do(dve.tensor_reduce(slot[:, k, :], mult[:, :, :].rearrange("p e t -> p t e"), AX_X, ALU.add))
                do(dve.tensor_copy(sloti[:, :], slot[:, :, :].rearrange("p k t -> p (k t)")))
                do(dve.tensor_scalar(part[:, 0, :], sloti[:, :], 7, None, ALU.logical_shift_right))
                do(dve.tensor_scalar(part[:, 1, :], sloti[:, :], P - 1, None, ALU.bitwise_and))
                own.mark(dve.tensor_copy(slot_tile[:, :], part[:, 0, :]))
                do(dve.tensor_copy(slot_row[:, :], part[:, 1, :]))
                for g in range(NP // GRP):
                    if g >= 2:
                        dve.wait_ge(s_inv, g - 1)
                    s = slice(g * GRP, (g + 1) * GRP)
                    r = right[g % 2]
                    own.mark(dve.tensor_tensor(left[g % 2][:, :, :], iota_p[:, :].unsqueeze(1).to_broadcast([P, GRP, P]),
                                               slot_row[:, s].unsqueeze(2).to_broadcast([P, GRP, P]), ALU.is_equal))
                    if g >= 2:
                        dve.wait_ge(s_cols, g - 1)
                    dve.tensor_tensor(tile_eq[g % 2][:, :, :],
                                      iota_p[:, 0:N_TILES].unsqueeze(1).to_broadcast([P, GRP, N_TILES]),
                                      slot_tile[:, s].unsqueeze(2).to_broadcast([P, GRP, N_TILES]), ALU.is_equal)\
                        .then_inc(s_eq, 1)
                    dve.wait_ge(s_eq, g + 1)
                    t0 = g * GRP % TOK_TILES
                    dve.tensor_tensor(r[:, :, 2, :], tile_eq[g % 2][:, :, :],
                                      iota_p[:, t0:t0 + GRP].unsqueeze(2).to_broadcast([P, GRP, N_TILES]), ALU.mult)\
                        .then_inc(s_oh, 1)
                own.wait()
                do(dve.tensor_tensor(ge[:, :, :], iota_p[:, 0:N_TILES].unsqueeze(1).to_broadcast([P, E, N_TILES]),
                                     first[:, :].unsqueeze(2).to_broadcast([P, E, N_TILES]), ALU.is_ge))
                do(dve.tensor_reduce(expf[:, :], ge[:, 1:E, :].rearrange("p e t -> p t e"), AX_X, ALU.add))
                own.mark(dve.tensor_copy(expert[:, :], expf[:, :]))
                own.mark(dve.tensor_tensor(mine[:, :, :], iota8[:, :].unsqueeze(1).to_broadcast([P, N_TILES, E]),
                                           expf[:, :].unsqueeze(2).to_broadcast([P, N_TILES, E]), ALU.is_equal))
                own.mark(dve.tensor_scalar(trash[:, :], lane[:, :], float(TOKENS), None, ALU.add))
                dve.wait_ge(s_inv, NP // GRP)
                own.mark(dve.tensor_scalar(pad[:, :], inv[:, 0:N_TILES], -1.0, 1.0, ALU.mult, ALU.add))
                do(dve.tensor_scalar(tokf[:, :], inv[:, 2 * N_TILES:3 * N_TILES], float(P), None, ALU.mult))
                do(dve.tensor_tensor(tokf[:, :], inv[:, N_TILES:2 * N_TILES], tokf[:, :], ALU.add))
                own.mark(dve.tensor_copy(token[:, :], tokf[:, :]))
                do(dve.scalar_tensor_tensor(out=tgtf[:, :], in0=pad[:, :], scalar=trash[:, 0:1], in1=tokf[:, :],
                                            op0=ALU.mult, op1=ALU.add))
                do(dve.tensor_copy(target[:, :], tgtf[:, :]))


_INS = ['x', 'ctx_1024', 'g_xattn', 'g_ffn', 'L0_xattn_gamma_media', 'L0_xattn_beta_media', 'L0_xattn_gamma_lat',
        'L0_xattn_beta_lat', 'L0_xattn_Wq', 'L0_xattn_bq', 'L0_xattn_Wkv', 'L0_xattn_bkv', 'L0_xattn_Wo',
        'L0_xattn_bo', 'L0_ffn_Wg', 'L0_ffn_bg', 'L0_ffn_W1', 'L0_ffn_b1', 'L0_ffn_W2', 'L0_ffn_b2']


def kernel(**inputs):
    import numpy as np
    import concourse.bacc as bacc
    from concourse.bass_utils import run_bass_kernel_spmd

    nc = bacc.Bacc("TRN2", target_bir_lowering=False, num_devices=1)
    arrays, aps = {}, {}
    for name in _INS:
        a = np.ascontiguousarray(inputs[name])
        arrays["in_" + name] = a
        aps[name] = nc.dram_tensor("in_" + name, a.shape, mybir.dt.from_np(a.dtype), kind="ExternalInput").ap()
    aps["out"] = nc.dram_tensor("out_rows", (TOKENS + P, D), F32, kind="ExternalOutput").ap()
    build(nc, aps)
    got = run_bass_kernel_spmd(nc, [arrays], core_ids=[0]).results[0]["out_rows"]
    return got[0:TOKENS].reshape(B, T, D)
```

```python
from contextlib import ExitStack

import concourse.bass as bass
from concourse import mybir

F32 = mybir.dt.float32
F32R = mybir.dt.float32r
I32 = mybir.dt.int32
U32 = mybir.dt.uint32
ALU = mybir.AluOpType
ACT = mybir.ActivationFunctionType
AX_X = mybir.AxisListType.X

P = 128
B, T, D = 16, 256, 256
H, DH = 8, 128
INNER = H * DH
KEYS = 2 * T
E, F, TOP = 8, 1024, 2
TEMP = 1.0 + 1e-06
EPS = 1e-5
SCALE = float(DH) ** -0.5
KD = D // P
TT = T // P
JT = KEYS // P
STEPS = B * H
TOKENS = B * T
TOK_TILES = TOKENS // P
PAIRS = TOKENS * TOP
N_TILES = (PAIRS + E * (P - 1)) // P
ROW = D + E
LIST_TILES = TOKENS // P
LISTS = (E - 1) * LIST_TILES + N_TILES
HALF = INNER // 2
FH = F // 2
PIECE = 1024
PIECES = (KD * E * FH + FH // P * E * D) // PIECE
NX, NT, NY, NO, NSTAGE = 4, 2, 3, 2, 6
RING = 3

A_STEP = 3
B_STEP = 0
Z_STEP = 2
R_STEP = 1
T_STEP = 3
G_STEP = 4
E_STEP = 5
W_STEP = 6
L_STEP = 7


def plan_units():
    before = [("z", (0, k)) for k in range(KD)] + [("k", 0), ("q", 0)] + [("v", (0, w)) for w in range(JT)]
    steps = []
    for i in range(STEPS + H):
        units = []
        if i + 1 < STEPS:
            units += [("k", i + 1), ("q", i + 1)]
        m, w = (i - 1) // JT + 1, (i - 1) % JT
        if i and m < 2 * B:
            units.append(("v", (m, w)))
        if 1 <= i <= STEPS:
            units.append(("o", i - 1))
        b, h = i // H, i % H
        if h == Z_STEP and b + 1 < B:
            units += [("z", (b + 1, k)) for k in range(KD)]
        if h == T_STEP and b >= 1:
            units.append(("t", b - 1))
        if h == G_STEP and b >= 1:
            units.append(("g", b - 1))
        if h == W_STEP and b >= 1:
            units.append(("r", b - 1))
        steps.append(units)
    return before, steps


class Later:

    def __init__(self, eng, sem):
        self.eng, self.sem, self.n = eng, sem, 0

    def mark(self, instruction):
        self.n += 1
        instruction.then_inc(self.sem, 1)

    def wait(self):
        self.eng.wait_ge(self.sem, self.n)


def product(pe, out, left, right, start, stop, **kw):
    (lh, ll), (rh, rl) = left, right
    pe.matmul(out, ll, rh, start=start, stop=False, **kw)
    pe.matmul(out, lh, rl, start=False, stop=False, **kw)
    return pe.matmul(out, lh, rh, start=False, stop=stop, **kw)


def build(nc, A):
    before, steps = plan_units()
    order = before + [u for s in steps for u in s]
    number = {u: n for n, u in enumerate(order)}
    hi_order = [u for u in order if u[0] in "kqvo"]
    hi_number = {u: n for n, u in enumerate(hi_order)}
    read_number = {u: n for group in ("zt", "kqvogr")
                   for n, u in enumerate(u for u in order if u[0] in group)}

    with ExitStack() as top:
        def sem(name):
            return top.enter_context(nc.semaphore(name))

        def alloc(stack, name, shape, dt=F32):
            return stack.enter_context(nc.sbuf_tensor(name, shape, dt))

        ident = alloc(top, "ident", [P, P])
        iota8 = alloc(top, "iota8", [P, E])
        lane = alloc(top, "lane", [P, 1])
        lists = dict(
            iota_t=alloc(top, "iota_t", [P, N_TILES]),
            ids=alloc(top, "ids", [P, TOK_TILES]),
            place=alloc(top, "place", [P, TOP * TT], I32),
            first=alloc(top, "first", [P, E]),
            row=alloc(top, "row", [P, 1], I32),
            token=alloc(top, "token", [P, N_TILES], I32),
            expert=alloc(top, "expert", [P, N_TILES], I32),
            mine=alloc(top, "mine", [P, N_TILES, E]),
        )

        with ExitStack() as first:
            early = dict(
                wkv=[alloc(first, f"wkv_{s}", [P, KD, 2 * INNER], F32R) for s in ("hi", "lo")],
                wq=[alloc(first, f"wq_{s}", [P, KD, INNER], F32R) for s in ("hi", "lo")],
                kvt=[[alloc(first, f"kvt{i}_{s}", [P, KD, KEYS], F32R) for s in ("hi", "lo")] for i in range(2)],
                zt=alloc(first, "zt", [P, KD, KEYS]),
                z=alloc(first, "z", [P, JT, D]),
            )
        with ExitStack() as second:
            raw = alloc(second, "w_raw", [P, PIECES, PIECE])
        work = dict(
            b1=alloc(top, "b1", [P, E * FH]),
            b2=alloc(top, "b2", [P, E * D]),
            xg=[alloc(top, f"xg{i}", [P, ROW]) for i in range(NX)],
            xt=[alloc(top, f"xt{i}", [P, 2, KD, P], F32R) for i in range(NT)],
            hb=alloc(top, "hb", [P, FH]),
            ha=alloc(top, "ha", [P, FH]),
            ht=[[alloc(top, f"ht{i}_{s}", [P, FH // P, P], F32R) for s in ("hi", "lo")] for i in range(2)],
            y1=[alloc(top, f"y1_{i}", [P, D]) for i in range(NY)],
            yo=[alloc(top, f"yo{i}", [P, D]) for i in range(NO)],
            stage=[alloc(top, f"stage{i}", [P, PIECE]) for i in range(NSTAGE)],
            wcol=alloc(top, "wcol", [P, N_TILES]),
            wjunk=alloc(top, "wjunk", [P, E]),
        )
        with ExitStack() as heads:
            with ExitStack() as raws:
                step = dict(
                    kv_raw=alloc(raws, "kv_raw", [P, KD, 2 * INNER]),
                    q_raw=alloc(raws, "q_raw", [P, KD, INNER]),
                    o_raw=alloc(raws, "o_raw", [P, H, D]),
                )
            pair = ("hi", "lo")
            step.update(
                v_sb=[[alloc(heads, f"v{i}_{s}", [P, JT, HALF], F32R) for s in pair] for i in range(2)],
                pt=[alloc(heads, f"pt_{s}", [P, JT, T], F32R) for s in pair],
                probs=[alloc(heads, f"probs{i}", [P, TT, KEYS]) for i in range(2)],
                kt=[[alloc(heads, f"kt{i}_{s}", [P, KEYS], F32R) for s in pair] for i in range(2)],
                qt=[[alloc(heads, f"qt{i}_{s}", [P, T], F32R) for s in pair] for i in range(2)],
                ot=[[alloc(heads, f"ot{i}_{s}", [P, T], F32R) for s in pair] for i in range(2)],
            )
        w1, w1_in = weight_pair(alloc, top, "w1", [P, KD, E * FH])

        dram = dict(
            xhat=nc.dram_tensor("xhat_rows", (TOKENS + P, ROW), F32, kind="Internal").ap(),
            half=nc.dram_tensor("half_sums", (N_TILES, P, D), F32, kind="Internal").ap(),
            xt=nc.dram_tensor("turned_rows", (N_TILES, P, 2, KD, P), F32, kind="Internal").ap(),
            lists=nc.dram_tensor("expert_lists", (LISTS, P), F32, kind="Internal").ap(),
        )
        sems = dict(
            w=[sem(f"piece_in{i}") for i in range(PIECES)],
            x2st=[sem(f"x2_stored{i}") for i in range(2)],
            rowst=[sem(f"rows_stored{i}") for i in range(2)],
            pad=sem("padding_rows"),
            listed=sem("listed"),
            row=sem("row_ready"),
            b1=sem("b1_in"),
        )

        def load_b1(sp, half):
            sp.dma_start(work["b1"][:, :].rearrange("p (e f) -> p e f", e=E),
                         A["L0_ffn_b1"][:, half * FH:(half + 1) * FH].partition_broadcast(P)).then_inc(sems["b1"], 16)

        split = Splitter(A, sems["w"], sem("w_hi"), {"pool": sem("w_lo_pool"), "dve": sem("w_lo_dve")},
                         raw, work["stage"])
        split.add(w1, w1_in)
        programs = {name: [] for name in ("sync", "gpsimd", "scalar", "tensor", "vector")}

        def program(name):
            return programs[name].append

        attention(nc, program, A, sem, sems, alloc, early, step, split, load_b1, lists, ident, iota8, lane, dram,
                  before, steps, number, hi_number, read_number)
        experts(nc, program, A, sem, sems, alloc, work, split, load_b1, lists, ident, iota8, dram)

        with nc.Block() as block:
            @block.sync
            def _(sp):
                for part in programs["sync"]:
                    part(sp)

            @block.gpsimd
            def _(pool):
                for part in programs["gpsimd"]:
                    part(pool)

            @block.scalar
            def _(act):
                for part in programs["scalar"]:
                    part(act)

            @block.tensor
            def _(pe):
                for part in programs["tensor"]:
                    part(pe)

            @block.vector
            def _(dve):
                for part in programs["vector"]:
                    part(dve)


def weight_pair(alloc, stack, name, shape):
    with ExitStack() as before:
        alloc(before, name + "_room", shape)
        arriving = alloc(before, name + "_in", shape)
    return [alloc(stack, f"{name}_{s}", shape, F32R) for s in ("hi", "lo")], arriving


class Splitter:

    def __init__(self, A, arrived, s_hi, s_lo, raw, stage):
        self.A, self.arrived, self.s_hi, self.s_lo = A, arrived, s_hi, s_lo
        self.raw, self.stage = raw, stage
        self.w, self.w_in = [], []
        self.by = [["pool" if j in (3, 5, 7) else "dve" for j in range(PIECES)],
                   ["pool" if j in (1, 4, 8, 11) else "dve" for j in range(PIECES)]]

    def add(self, pair, w_in):
        self.w.append(pair)
        self.w_in.append(w_in)

    def staged(self, j):
        return j % (PIECES // 2) < NSTAGE

    def parts(self, half, j):
        _, which, (k, cols), _ = piece_views(self.A, half, j)
        hi, lo = (w[:, k, cols] for w in self.w[which])
        if half == 0:
            return self.raw[:, j, :], hi, lo
        return (self.stage[j % (PIECES // 2)][:, :] if self.staged(j) else self.w_in[which][:, k, cols]), hi, lo

    def load(self, sp, half, j):
        src, _, _, per = piece_views(self.A, half, j)
        dst = self.raw[:, j, :] if half == 0 else self.parts(half, j)[0]
        sp.dma_start(dst.rearrange("p (e n) -> p e n", e=per), src).then_inc(self.arrived[j], 16)

    def make_hi(self, act, half, js):
        for j in js:
            raw, hi, _ = self.parts(half, j)
            act.wait_ge(self.arrived[j], 16 * (half + 1))
            act.activation(hi, raw, ACT.Copy).then_inc(self.s_hi, 1)

    def make_lo(self, eng, name, half, js):
        for j in js:
            if self.by[half][j] == name:
                raw, hi, lo = self.parts(half, j)
                eng.wait_ge(self.s_hi, PIECES * half + j + 1)
                eng.tensor_tensor(lo, raw, hi.bitcast(F32), ALU.subtract).then_inc(self.s_lo[name], 1)

    def wait_lo(self, eng, half, js):
        for j in js:
            name = self.by[half][j]
            count = sum(self.by[h][i] == name for h in range(half + 1) for i in range(PIECES)
                        if (h, i) <= (half, j))
            eng.wait_ge(self.s_lo[name], count)


def piece_views(A, half, j):
    if j < PIECES // 2:
        per = PIECE // FH
        k, c = divmod(j, E // per)
        src = A["L0_ffn_W1"][c * per:(c + 1) * per, k * P:(k + 1) * P, half * FH:(half + 1) * FH]
        return src.rearrange("e p f -> p e f"), 0, (k, slice(c * PIECE, (c + 1) * PIECE)), per
    per = PIECE // D
    g, c = divmod(j - PIECES // 2, E // per)
    src = A["L0_ffn_W2"][c * per:(c + 1) * per, half * FH + g * P:half * FH + (g + 1) * P, :]
    return src.rearrange("e p d -> p e d"), 1, (g, slice(c * PIECE, (c + 1) * PIECE)), per


def attention(nc, program, A, sem, sems, alloc, early, step, split, load_b1, lists, ident, iota8, lane, dram,
              before, steps, number, hi_number, read_number):
    with ExitStack() as ctx:
        def sb(name, shape, dt=F32):
            return alloc(ctx, name, shape, dt)

        def bank(name):
            return ctx.enter_context(nc.psum_tensor(name, [P, 512], F32))

        wkv, wq, kvt, zt, z = (early[n] for n in ("wkv", "wq", "kvt", "zt", "z"))
        wo = [sb(f"wo_{s}", [P, H, D], F32R) for s in ("hi", "lo")]
        wg = sb("wg", [P, KD, E])
        bq = sb("bq", [P, H])
        bk = sb("bk", [P, H])
        bv = sb("bv", [P, H])
        gamma = sb("gamma", [P, 2, KD])
        beta = sb("beta", [P, 2, KD])
        bo = sb("bo", [P, TT, D])
        bg = sb("bg", [P, E])
        gate = sb("gate", [P, 2])
        tgate = sb("tgate", [P, 2])
        minus_half = sb("minus_half", [P, 4])
        x_raw = [sb(f"x_raw{i}", [P, TT, D]) for i in range(3)]
        c_raw = [sb(f"c_raw{i}", [P, TT, D]) for i in range(2)]
        xh = sb("xh", [P, TT, D])
        stats = {n: sb("stats_" + n, [P, 4, 6]) for n in "abc"}
        mv_a = sb("mv_a", [P, 4, 2])
        mv_b = sb("mv_b", [P, TT, 2])
        mv_c = sb("mv_c", [P, TT, 2])
        ve = {n: sb("ve_" + n, [P, 4]) for n in "abc"}
        rs_a = sb("rs_a", [P, 4])
        rs_b = sb("rs_b", [P, TT])
        rs_c = sb("rs_c", [P, TT])
        y = sb("y", [P, TT, D])
        x2 = [sb(f"x2_{i}", [P, TT, D]) for i in range(2)]
        rows = [sb(f"rows{i}", [P, TT, ROW]) for i in range(2)]
        x2t = sb("x2t", [P, KD, T])
        gates = sb("gates", [P, TT, E])
        top8 = sb("top8", [P, TT, 8])
        arg8 = sb("arg8", [P, TT, 8], U32)
        argf = sb("argf", [P, TT, TOP])
        gap = sb("gap", [P, TT])
        egap = sb("egap", [P, TT])
        wsum = sb("wsum", [P, TT])
        w12 = sb("w12", [P, TT, TOP])
        wtmp = sb("wtmp", [P, TT, E])
        smax = sb("smax", [P, 2, TT])
        nbias = sb("nbias", [P, 2, TT])
        ssum = sb("ssum", [P, 2, TT])
        rsum = sb("rsum", [P, 2, TT])

        kv_raw, q_raw, o_raw, v_sb, pt, probs, kt, qt, ot = (
            step[n] for n in ("kv_raw", "q_raw", "o_raw", "v_sb", "pt", "probs", "kt", "qt", "ot"))
        iota_t, ids, place, first, row = (lists[n] for n in ("iota_t", "ids", "place", "first", "row"))
        onehot = sb("onehot", [P, TOP, E, TT])
        chosen = sb("chosen", [P, E, TT])
        below = sb("below", [P, P])
        ones = sb("ones", [P, P])
        pad_ids = sb("pad_ids", [P, P])
        start = sb("start", [P, E])
        counts = sb("counts", [P, 2, E, TT])
        total = sb("total", [P, E])
        rank = sb("rank", [P, E, TT])
        ranked = sb("ranked", [P, TOP, E, TT])
        placef = sb("placef", [P, TOP, TT])
        tiles_i = sb("tiles_i", [P, E], I32)
        tiles = sb("tiles", [P, E])
        zero = sb("zero", [P, E])
        gone = sb("gone", [P, E - 1])
        extra = sb("extra", [P, E - 1])
        skipped = sb("skipped", [P, 1])

        ring = [bank(f"ring{i}") for i in range(RING)]
        score = [bank(f"score{i}") for i in range(TT)]
        turn = [bank(f"turn{i}") for i in range(2)]
        proj = bank("proj")

        s_ident0, s_ident, s_const = sem("ident0"), sem("ident_ready"), sem("const")
        s_affine, s_bias, s_small = sem("affine_in"), sem("bias_in"), sem("small_in")
        s_win = {name: sem(name + "_in") for name in ("k0", "k1", "q0", "q1", "v0", "v1", "o0", "o1")}
        s_x = [sem(f"x_in{i}") for i in range(3)]
        s_c = [sem(f"c_in{i}") for i in range(2)]
        s_wg = sem("wg_in")
        s_whi = sem("weights_hi")
        s_wlo = {"dve": sem("weights_lo_dve"), "pool": sem("weights_lo_pool")}
        s_kvt0 = sem("kvt0_hi")
        s_tg = sem("tanh_gate")
        s_full = sem("unit_full")
        s_hi = sem("unit_hi")
        s_read = sem("unit_read")
        s_aread = sem("unit_read_act")
        s_score = sem("scores")
        s_max = sem("max")
        s_exp = sem("exp")
        s_rsum = sem("rsum")
        s_norm = sem("norm")
        s_turn = sem("turned")
        s_pthi, s_ptlo = sem("pt_hi"), sem("pt_lo")
        s_proj, s_projr = sem("projected"), sem("projection_read")
        s_mva, s_mvb, s_mvc = sem("mv_a"), sem("mv_b"), sem("mv_c")
        s_rsa, s_rsb, s_rsc = sem("rs_a"), sem("rs_b"), sem("rs_c")
        s_cused, s_xh, s_z = sem("media_used"), sem("xh_ready"), sem("z_ready")
        s_kvt, s_xn = sem("kvt_ready"), sem("xn_rows")
        s_x2, s_rows, s_gap, s_egap = sem("x2"), sem("rows"), sem("gap"), sem("egap")
        s_x2st, s_rowst, s_pad, s_listed, s_row = (sems[n] for n in ("x2st", "rowst", "pad", "listed", "row"))
        s_padz, s_chosen, s_place, s_routing = sem("padding_zero"), sem("chosen"), sem("places"), sem("routing_consts")
        s_dve, s_pool = sem("dve_self"), sem("pool_self")

        N_ROUTING = 6
        N_PAD = 2 + -(-LISTS // P)
        N_AFFINE, N_BIAS, N_SMALL = 4, 3, TT + 3

        def wait_read(eng, unit):
            eng.wait_ge(s_aread if unit[0] in "zt" else s_read, read_number[unit] + 1)

        ov = A["out"][0:TOKENS, :].rearrange("(b t p) d -> b p t d", t=TT, p=P)
        rv = dram["xhat"][0:TOKENS, :].rearrange("(b t p) d -> b p t d", t=TT, p=P)

        pieces = []
        for c, name in enumerate("kv"):
            cols = slice(c * INNER, (c + 1) * INNER)
            for k in range(KD):
                pieces.append((name + str(k), A["L0_xattn_Wkv"][k * P:(k + 1) * P, cols], kv_raw[:, k, cols],
                               [w[:, k, cols] for w in wkv], "dve" if name == "k" else "pool"))
        for k in range(KD):
            pieces.insert(KD + k, ("q" + str(k), A["L0_xattn_Wq"][k * P:(k + 1) * P, :], q_raw[:, k, :],
                                   [w[:, k, :] for w in wq], "dve"))
        for c in range(2):
            heads = slice(c * H // 2, (c + 1) * H // 2)
            pieces.append(("o" + str(c), A["L0_xattn_Wo"][c * INNER // 2:(c + 1) * INNER // 2, :]
                           .rearrange("(h p) n -> p h n", p=P), o_raw[:, heads, :], [w[:, heads, :] for w in wo], "dve"))

        def hi_weights(act, kinds):
            for name, _, raw, (hi, _), _ in pieces:
                if name[0] in kinds:
                    act.wait_ge(s_win[name], 16)
                    act.activation(hi, raw, ACT.Copy).then_inc(s_whi, 1)

        def lo_weights(eng, who, kind):
            for n, (name, _, raw, (hi, lo), by) in enumerate(pieces):
                if name[0] == kind and by == who:
                    eng.wait_ge(s_whi, n + 1)
                    eng.tensor_tensor(lo, raw, hi.bitcast(F32), ALU.subtract).then_inc(s_wlo[who], 1)

        def weights_split(eng, kind):
            by = [p[4] for p in pieces]
            last = max(n for n, p in enumerate(pieces) if p[0][0] == kind)
            eng.wait_ge(s_wlo[by[last]], by[:last + 1].count(by[last]))

        order = before + [u for s in steps for u in s]

        @program("sync")
        def _(sp):
            def load(c):
                if c >= 3:
                    sp.wait_ge(s_x2, c - 2)
                sp.dma_start(x_raw[c % 3][:, :, :],
                             A["x"][c].rearrange("(t p) d -> p t d", p=P)).then_inc(s_x[c % 3], 16)
                if c >= 2:
                    sp.wait_ge(s_cused, c - 1)
                sp.dma_start(c_raw[c % 2][:, :, :],
                             A["ctx_1024"][c].rearrange("(t p) d -> p t d", p=P)).then_inc(s_c[c % 2], 16)

            def load_weights(kinds):
                for name, src, raw, _, _ in pieces:
                    if name[0] in kinds:
                        sp.dma_start(raw, src).then_inc(s_win[name], 16)

            load(0)
            load_weights("k")
            with nc.allow_non_contiguous_dma(reason="columns of vectors"):
                for k, (g, b_) in enumerate((("gamma_media", "beta_media"), ("gamma_lat", "beta_lat"))):
                    sp.dma_start(gamma[:, k, :], A["L0_xattn_" + g].rearrange("(k p) -> p k", p=P)).then_inc(s_affine, 16)
                    sp.dma_start(beta[:, k, :], A["L0_xattn_" + b_].rearrange("(k p) -> p k", p=P)).then_inc(s_affine, 16)
            load_weights("q")
            with nc.allow_non_contiguous_dma(reason="columns of vectors"):
                bkv = A["L0_xattn_bkv"]
                sp.dma_start(bk[:, :], bkv[0:INNER].rearrange("(h p) -> p h", p=P)).then_inc(s_bias, 16)
                sp.dma_start(bq[:, :], A["L0_xattn_bq"].rearrange("(h p) -> p h", p=P)).then_inc(s_bias, 16)
                sp.dma_start(bv[:, :], bkv[INNER:].rearrange("(h p) -> p h", p=P)).then_inc(s_bias, 16)
            load_weights("v")
            load(1)
            load_weights("o")
            sp.dma_start(wg[:, :, :], A["L0_ffn_Wg"].rearrange("(k p) e -> p k e", p=P)).then_inc(s_wg, 16)
            for t in range(TT):
                sp.dma_start(bo[:, t, :], A["L0_xattn_bo"].partition_broadcast(P)).then_inc(s_small, 16)
            sp.dma_start(bg[:, :], A["L0_ffn_bg"].partition_broadcast(P)).then_inc(s_small, 16)
            sp.dma_start(gate[:, 0:1], A["g_xattn"].partition_broadcast(P)).then_inc(s_small, 16)
            sp.dma_start(gate[:, 1:2], A["g_ffn"].partition_broadcast(P)).then_inc(s_small, 16)
            def load_raw(kinds, js):
                for kind in kinds:
                    sp.wait_ge(s_full, max(number[u] for u in number if u[0] == kind) + 1)
                for j in js:
                    split.load(sp, 0, j)

            sp.wait_ge(s_padz, 1)
            sp.dma_start(dram["xhat"][TOKENS:, :], rows[0][:, 0, :]).then_inc(s_pad, 16)
            sp.dma_start(A["out"][TOKENS:, :], rows[0][:, 0, 0:D]).then_inc(s_pad, 16)
            sp.wait_ge(s_routing, N_ROUTING)
            for r in range(0, LISTS, P):
                n = min(P, LISTS - r)
                sp.dma_start(dram["lists"][r:r + n, :], pad_ids[0:n, :]).then_inc(s_pad, 16)
            load(2)
            for b in range(B):
                if b == B - 1:
                    load_raw("kq", (0, 2, 4, 6, 8, 9, 10, 11, 14, 15))
                sp.wait_ge(s_x2, b + 1)
                sp.dma_start(ov[b], x2[b % 2][:, :, :]).then_inc(s_x2st[b % 2], 16)
                if b + 3 < B:
                    load(b + 3)
                if b == B - 1:
                    split.wait_lo(sp, 0, range(PIECES // 4))
                    load_b1(sp, 0)
                if b == B - 2:
                    load_raw("v", (1, 3, 5, 7, 12, 13))
                sp.wait_ge(s_rows, b + 1)
                sp.dma_start(rv[b], rows[b % 2][:, :, :]).then_inc(s_rowst[b % 2], 16)
        @program("gpsimd")
        def _(pool):
            own = Later(pool, s_pool)
            pool.memset(ident[:, :], 0.0).then_inc(s_ident0, 1)
            pool.memset(minus_half[:, :], -0.5).then_inc(s_const, 1)
            pool.iota(iota8[:, :], [[1, E]], base=0, channel_multiplier=0,
                      allow_small_or_imprecise_dtypes=True).then_inc(s_const, 1)
            pool.wait_ge(s_ident0, 1)
            pool.affine_select(out=ident[:, :], in_=ident[:, :], compare_op=ALU.not_equal, fill=1.0,
                               base=0, pattern=[[-1, P]], channel_multiplier=1).then_inc(s_ident, 1)
            pool.wait_ge(s_const, 2)
            pool.memset(rows[0][:, 0, :], 0.0).then_inc(s_padz, 1)

            def rstd(norm, out, mv, n, ready, count, done):
                pool.wait_ge(ready, count)
                own.mark(pool.tensor_scalar(ve[norm][:, 0:n], mv[:, 0:n, 1], EPS, 1.0, ALU.add, ALU.mult))
                own.wait()
                pool.tensor_tensor(out[:, 0:n], ve[norm][:, 0:n], minus_half[:, 0:n], ALU.pow).then_inc(done, 1)

            def negate(mv):
                own.mark(pool.tensor_scalar(mv[:, :, 0], mv[:, :, 0], -1.0, 0.0, ALU.mult, ALU.add))

            def norm(out, src, mv, rs, n):
                return pool.tensor_scalar(out, src, mv[:, n, 0:1], rs[:, n:n + 1], ALU.add, ALU.mult)

            def prepare_a(c):
                rstd("a", rs_a, mv_a, 4, s_mva, 2 * (c + 1), s_rsa)
                negate(mv_a)
                own.wait()
                pool.wait_ge(s_rsa, c + 1)
                if c:
                    pool.wait_ge(s_mvb, c)
                    pool.wait_ge(s_full, number["z", (c - 1, KD - 1)] + 1)
                for t in range(TT):
                    last = norm(xh[:, t, :], x_raw[c % 3][:, t, :], mv_a, rs_a, t)
                last.then_inc(s_xh, 1)
                for t in range(TT):
                    last = norm(z[:, t, :], c_raw[c % 2][:, t, :], mv_a, rs_a, TT + t)
                last.then_inc(s_cused, 1)

            def prepare_b(c):
                rstd("b", rs_b, mv_b, TT, s_mvb, c + 1, s_rsb)
                negate(mv_b)
                own.wait()
                pool.wait_ge(s_rsb, c + 1)
                for t in range(TT):
                    last = norm(z[:, TT + t, :], xh[:, t, :], mv_b, rs_b, t)
                last.then_inc(s_z, 1)

            def norm_rows(b):
                rstd("c", rs_c, mv_c, TT, s_mvc, b + 1, s_rsc)
                negate(mv_c)
                own.wait()
                pool.wait_ge(s_rsc, b + 1)
                if b >= 2:
                    pool.wait_ge(s_rowst[b % 2], 16 * (b // 2))
                elif b == 0:
                    pool.wait_ge(s_pad, 16 * N_PAD)
                for t in range(TT):
                    last = norm(rows[b % 2][:, t, 0:D], x2[b % 2][:, t, :], mv_c, rs_c, t)
                last.then_inc(s_xn, 1)

            def routing_constants():
                def iota(out, base, pattern, per_partition):
                    pool.iota(out, pattern, base=base, channel_multiplier=per_partition,
                              allow_small_or_imprecise_dtypes=True).then_inc(s_routing, 1)

                own.mark(pool.memset(below[:, :], 1.0))
                pool.memset(ones[:, :], 1.0).then_inc(s_routing, 1)
                iota(iota_t[:, :], 0, [[1, N_TILES]], 0)
                iota(lane[:, :], 0, [[1, 1]], 1)
                iota(pad_ids[:, :], TOKENS, [[1, P]], 0)
                iota(ids[:, :], 0, [[P, TOK_TILES]], 1)
                own.wait()
                pool.affine_select(out=below[:, :], in_=below[:, :], compare_op=ALU.is_gt, fill=0.0,
                                   base=0, pattern=[[1, P]], channel_multiplier=-1).then_inc(s_routing, 1)

            def list_tokens(b):
                pool.wait_ge(s_place, b + 1)
                pool.wait_ge(s_pad, 16 * N_PAD)
                for k in range(TOP):
                    for t in range(TT):
                        q = k * TT + t
                        pool.indirect_dma_start(
                            out=dram["lists"].rearrange("l (p o) -> (l p) o", o=1),
                            out_offset=bass.IndirectOffsetOnAxis(ap=place[:, q:q + 1].bitcast(U32), axis=0),
                            in_=ids[:, TT * b + t:TT * b + t + 1], in_offset=None,
                        ).then_inc(s_listed, 16)

            def split_kv(c):
                wait_read(pool, ("z", (c, KD - 1)))
                if c >= 2:
                    pool.wait_ge(s_full, number["q", H * (c - 1) - 1] + 1)
                    pool.wait_ge(s_full, number["v", (2 * (c - 2) + 1, JT - 1)] + 1)
                hi, lo = kvt[c % 2]
                own.mark(pool.tensor_copy(hi[:, :, :], zt[:, :, :]))
                own.wait()
                pool.tensor_tensor(lo[:, :, :], zt[:, :, :], hi[:, :, :].bitcast(F32), ALU.subtract)\
                    .then_inc(s_kvt, 1)

            def normalise(n):
                pool.wait_ge(s_rsum, n + 1)
                for t in range(TT):
                    last = pool.tensor_scalar(probs[n % 2][:, t, :], probs[n % 2][:, t, :],
                                              rsum[:, n % 2, t:t + 1], 1.0, ALU.mult, ALU.mult)
                last.then_inc(s_norm, 1)

            prepare_a(0)
            prepare_b(0)
            lo_weights(pool, "pool", "v")
            routing_constants()
            prepare_a(1)
            for i in range(STEPS + H):
                b, h = i // H, i % H
                if i < STEPS:
                    normalise(i)
                if h == A_STEP and b + 2 < B:
                    prepare_a(b + 2)
                if h == B_STEP and b + 1 < B:
                    prepare_b(b + 1)
                if h == Z_STEP and b + 1 < B:
                    split_kv(b + 1)
                if h == R_STEP and b >= 1:
                    norm_rows(b - 1)
                if h == L_STEP and b >= 1:
                    list_tokens(b - 1)
                if i == STEPS + 2:
                    pool.wait_ge(s_proj, B)
                    split.make_lo(pool, "pool", 0, range(PIECES // 2))

        @program("scalar")
        def _(act):
            hi_weights(act, "kqv")
            act.wait_ge(s_affine, 16 * N_AFFINE)

            def hi_part(kind, at):
                n = number[kind, at]
                src = ring[n % RING]
                act.wait_ge(s_full, n + 1)
                if kind == "k":
                    ins = act.activation(kt[at % 2][0][:, :], src[:, :], ACT.Identity, bias=bk[:, at % H:at % H + 1])
                elif kind == "q":
                    ins = act.activation(qt[at % 2][0][:, :], src[:, 0:T], ACT.Identity, bias=bq[:, at % H:at % H + 1])
                elif kind == "o":
                    ins = act.activation(ot[at % 2][0][:, :], src[:, 0:T], ACT.Identity, bias=bv[:, at % H:at % H + 1])
                else:
                    m, w = at
                    ins = act.activation(v_sb[m % 2][0][:, w, :], src[:, :], ACT.Copy)
                ins.then_inc(s_hi, 1)

            def exp(n, t):
                act.wait_ge(s_max, n + 1)
                act.activation(probs[n % 2][:, t, :], score[t][:, :], ACT.Exp, scale=SCALE,
                               bias=nbias[:, n % 2, t:t + 1],
                               accum_out=ssum[:, n % 2, t:t + 1]).then_inc(s_exp, 1)

            def read_unit(kind, at):
                n = number[kind, at]
                src = ring[n % RING]
                act.wait_ge(s_full, n + 1)
                if kind == "z":
                    c, k = at
                    if c:
                        act.wait_ge(s_kvt, c)
                    for s in range(2):
                        last = act.activation(zt[:, k, s * T:(s + 1) * T], src[:, s * T:(s + 1) * T], ACT.Identity,
                                              scale=gamma[:, s, k:k + 1], bias=beta[:, s, k:k + 1])
                else:
                    last = act.activation(x2t[:, :, :], src[:, :].rearrange("p (k t) -> p k t", k=KD), ACT.Copy)
                last.then_inc(s_aread, 1)

            for n, u in enumerate(before):
                if n == KD:
                    act.wait_ge(s_aread, KD)
                    act.activation(kvt[0][0][:, :, :], zt[:, :, :], ACT.Copy).then_inc(s_kvt0, 1)
                    hi_weights(act, "o")
                    act.wait_ge(s_bias, 16 * N_BIAS)
                hi_part(*u) if u in hi_number else read_unit(*u)
            act.wait_ge(s_small, 16 * N_SMALL)
            act.activation(tgate[:, :], gate[:, :], ACT.Tanh).then_inc(s_tg, 1)
            for i in range(STEPS + H):
                units = [u for u in steps[i] if u in hi_number]
                if 1 <= i <= STEPS:
                    for t in range(2):
                        act.wait_ge(s_turn, 2 * (i - 1) + t + 1)
                        act.activation(pt[0][:, 2 * t:2 * t + 2, :],
                                       turn[t][:, :].rearrange("p (j i) -> p j i", j=2), ACT.Copy).then_inc(s_pthi, 1)
                for u in units:
                    if u[0] == "k":
                        hi_part(*u)
                if i < STEPS:
                    exp(i, 0)
                    exp(i, 1)
                for u in units:
                    if u[0] != "k":
                        hi_part(*u)
                if i == STEPS + 2:
                    act.wait_ge(s_proj, B)
                    split.make_hi(act, 0, range(PIECES // 2 - 2))
                for u in steps[i]:
                    if u[0] in "zt":
                        read_unit(*u)
                if i == STEPS + T_STEP:
                    split.make_hi(act, 0, range(PIECES // 2 - 2, PIECES // 2))
                if i % H == E_STEP and i // H >= 1:
                    b = i // H - 1
                    act.wait_ge(s_gap, b + 1)
                    act.activation(egap[:, :], gap[:, :], ACT.Exp).then_inc(s_egap, 1)

        @program("tensor")
        def _(pe):
            def unit(kind, at):
                n = number[kind, at]
                dst = ring[n % RING]
                if n >= RING:
                    wait_read(pe, order[n - RING])
                if kind in "kq":
                    b, h = at // H, at % H
                    pe.wait_ge(s_kvt, b + 1)
                    w, c0, width = (wkv, 0, KEYS) if kind == "k" else (wq, T, T)
                    for k in range(KD):
                        last = product(pe, dst[:, 0:width], [s[:, k, h * DH:(h + 1) * DH] for s in w],
                                       [s[:, k, c0:c0 + width] for s in kvt[b % 2]], k == 0, k == KD - 1)
                elif kind == "v":
                    m, w = at
                    b, half = m // 2, m % 2
                    pe.wait_ge(s_kvt, b + 1)
                    c0 = INNER + half * HALF
                    for k in range(KD):
                        last = product(pe, dst[:, :], [s[:, k, w * P:(w + 1) * P] for s in kvt[b % 2]],
                                       [s[:, k, c0:c0 + HALF] for s in wkv], k == 0, k == KD - 1)
                elif kind == "o":
                    m, h4 = at // JT, at % JT
                    pe.wait_ge(s_ptlo, 2 * (at + 1))
                    wait_read(pe, ("v", (m, JT - 1)))
                    for j in range(JT):
                        last = product(pe, dst[:, 0:T], [s[:, j, h4 * DH:(h4 + 1) * DH] for s in v_sb[m % 2]],
                                       [s[:, j, :] for s in pt], j == 0, j == JT - 1)
                elif kind == "z":
                    c, k = at
                    pe.wait_ge(s_z, c + 1)
                    for j in range(JT):
                        last = pe.transpose(dst[:, j * P:(j + 1) * P], z[:, j, k * P:(k + 1) * P], ident[:, :])
                elif kind == "t":
                    pe.wait_ge(s_rsc, at + 1)
                    pe.wait_ge(s_xn, at + 1)
                    for k in range(KD):
                        for t in range(TT):
                            last = pe.transpose(dst[:, (k * TT + t) * P:(k * TT + t + 1) * P],
                                                rows[at % 2][:, t, k * P:(k + 1) * P], ident[:, :])
                elif kind == "r":
                    pe.wait_ge(s_routing, N_ROUTING)
                    pe.wait_ge(s_chosen, at + 1)
                    ch = chosen[:, :, :].rearrange("p e t -> p (e t)")
                    pe.matmul(dst[:, 0:E * TT], below[:, :], ch, start=True, stop=True)
                    last = pe.matmul(dst[:, E * TT:2 * E * TT], ones[:, :], ch, start=True, stop=True)
                else:
                    pe.wait_ge(s_wg, 16)
                    wait_read(pe, ("t", at))
                    for t in range(TT):
                        for k in range(KD):
                            last = pe.matmul(dst[:, t * E:(t + 1) * E], x2t[:, k, t * P:(t + 1) * P],
                                             wg[:, k, :], start=k == 0, stop=k == KD - 1)
                last.then_inc(s_full, 1)

            def scores(n):
                wait_read(pe, ("q", n))
                if n:
                    pe.wait_ge(s_exp, TT * n)
                for t in range(TT):
                    product(pe, score[t][:, :], [s[:, t * P:(t + 1) * P] for s in qt[n % 2]],
                            [s[:, :] for s in kt[n % 2]], True, True).then_inc(s_score, 1)

            def turn_probs(n):
                pe.wait_ge(s_norm, n + 1)
                if n:
                    pe.wait_ge(s_ptlo, 2 * n)
                for t in range(2):
                    for j in range(2):
                        for q in range(TT):
                            last = pe.transpose(turn[t][:, j * T + q * P:j * T + (q + 1) * P],
                                                probs[n % 2][:, q, (2 * t + j) * P:(2 * t + j + 1) * P], ident[:, :])
                    last.then_inc(s_turn, 1)

            def out_proj(n):
                b, h = n // H, n % H
                wait_read(pe, ("o", n))
                if h == 0 and b:
                    pe.wait_ge(s_projr, b)
                for t in range(TT):
                    last = product(pe, proj[:, t * D:(t + 1) * D], [s[:, t * P:(t + 1) * P] for s in ot[n % 2]],
                                   [s[:, h, :] for s in wo], h == 0 and t == 0, h == H - 1,
                                   skip_group_check=True)
                if h == H - 1:
                    last.then_inc(s_proj, 1)

            pe.wait_ge(s_ident, 1)
            for u in before:
                if u[0] != "z":
                    weights_split(pe, u[0])
                unit(*u)
            for i in range(STEPS + H):
                if i == 1:
                    weights_split(pe, "o")
                if i < STEPS:
                    scores(i)
                if 1 <= i <= STEPS:
                    turn_probs(i - 1)
                for u in steps[i]:
                    if u[0] in "kqov":
                        unit(*u)
                if 2 <= i <= STEPS + 1:
                    out_proj(i - 2)
                for u in steps[i]:
                    if u[0] in "ztgr":
                        unit(*u)

        @program("vector")
        def _(dve):
            own = Later(dve, s_dve)

            def moments(name, tiles, mv, done, used, turn, at=0):
                dve.wait_ge(used, turn)
                for n, t in enumerate(tiles, at):
                    own.mark(dve.bn_stats(stats[name][:, n, :], t))
                own.wait()
                for n in range(at, at + len(tiles)):
                    last = dve.bn_aggr(mv[:, n, :], stats[name][:, n, :])
                last.then_inc(done, 1)

            def prepare_a(c, only=None):
                if only != 1:
                    dve.wait_ge(s_x[c % 3], 16 * (c // 3 + 1))
                    moments("a", [x_raw[c % 3][:, t, :] for t in range(TT)], mv_a, s_mva, s_cused, c)
                if only != 0:
                    dve.wait_ge(s_c[c % 2], 16 * (c // 2 + 1))
                    moments("a", [c_raw[c % 2][:, t, :] for t in range(TT)], mv_a, s_mva, s_cused, c, TT)

            def prepare_b(c):
                dve.wait_ge(s_xh, c + 1)
                moments("b", [xh[:, t, :] for t in range(TT)], mv_b, s_mvb, s_z, c)

            def read_unit(kind, at):
                n = number[kind, at]
                src = ring[n % RING]
                if (kind, at) in hi_number:
                    dve.wait_ge(s_hi, hi_number[kind, at] + 1)
                    if kind == "k":
                        hi, lo = kt[at % 2]
                        bias, part = bk[:, at % H:at % H + 1], src[:, :]
                    elif kind == "q":
                        hi, lo = qt[at % 2]
                        bias, part = bq[:, at % H:at % H + 1], src[:, 0:T]
                    elif kind == "o":
                        hi, lo = ot[at % 2]
                        bias, part = bv[:, at % H:at % H + 1], src[:, 0:T]
                    if kind == "v":
                        m, w = at
                        hi, lo = v_sb[m % 2]
                        dve.tensor_tensor(lo[:, w, :], src[:, :], hi[:, w, :].bitcast(F32), ALU.subtract)\
                            .then_inc(s_read, 1)
                    else:
                        dve.scalar_tensor_tensor(out=lo[:, :], in0=part, scalar=bias, in1=hi[:, :].bitcast(F32),
                                                 op0=ALU.add, op1=ALU.subtract).then_inc(s_read, 1)
                    return
                dve.wait_ge(s_full, n + 1)
                if kind == "g":
                    dve.tensor_tensor(gates[:, :, :], src[:, 0:TT * E].rearrange("p (t e) -> p t e", t=TT),
                                      bg[:, :].unsqueeze(1).to_broadcast([P, TT, E]), ALU.add).then_inc(s_read, 1)
                else:
                    dve.tensor_copy(counts[:, :, :, :], src[:, 0:2 * E * TT].rearrange("p (c e t) -> p c e t", c=2, t=TT))\
                        .then_inc(s_read, 1)

            def largest(b):
                dve.wait_ge(s_read, read_number["g", b] + 1)
                own.mark(dve.tensor_scalar(gates[:, :, :], gates[:, :, :], 1.0 / TEMP, None, ALU.mult))
                own.wait()
                for t in range(TT):
                    own.mark(dve.max(top8[:, t, :], gates[:, t, :]))
                own.wait()
                if b:
                    dve.wait_ge(s_egap, b)
                dve.tensor_tensor(gap[:, :], top8[:, :, 1], top8[:, :, 0], ALU.subtract).then_inc(s_gap, 1)

            def choose(b):
                for t in range(TT):
                    own.mark(dve.max_index(arg8[:, t, :], top8[:, t, :], gates[:, t, :]))
                own.wait()
                own.mark(dve.tensor_copy(argf[:, :, :], arg8[:, :, 0:TOP]))
                own.wait()
                for k in range(TOP):
                    for t in range(TT):
                        own.mark(dve.tensor_scalar(onehot[:, k, :, t], iota8[:, :],
                                                   argf[:, t, k:k + 1], None, ALU.is_equal))
                own.wait()
                dve.tensor_tensor(chosen[:, :, :], onehot[:, 0], onehot[:, 1], ALU.add).then_inc(s_chosen, 1)

            def find_places(b):
                inside, whole = counts[:, 0], counts[:, 1]
                dve.wait_ge(s_read, read_number["r", b] + 1)
                own.mark(dve.tensor_tensor(rank[:, :, :], inside,
                                           start[:, :].unsqueeze(2).to_broadcast([P, E, TT]), ALU.add))
                own.mark(dve.tensor_reduce(total[:, :], whole, AX_X, ALU.add))
                own.wait()
                own.mark(dve.tensor_tensor(rank[:, :, 1], rank[:, :, 1], whole[:, :, 0], ALU.add))
                own.mark(dve.tensor_tensor(start[:, :], start[:, :], total[:, :], ALU.add))
                own.wait()
                own.mark(dve.tensor_tensor(ranked[:, :, :, :], onehot[:, :, :, :],
                                           rank[:, :, :].unsqueeze(1).to_broadcast([P, TOP, E, TT]), ALU.mult))
                own.wait()
                own.mark(dve.tensor_reduce(placef[:, :, :], ranked[:, :, :, :].rearrange("p k e t -> p k t e"),
                                           AX_X, ALU.add))
                own.wait()
                if b:
                    dve.wait_ge(s_listed, 16 * TOP * TT * b)
                dve.tensor_copy(place[:, :], placef[:, :, :].rearrange("p k t -> p (k t)")).then_inc(s_place, 1)

            def find_rows():
                def do(instruction):
                    own.mark(instruction)
                    own.wait()

                own.wait()
                do(dve.tensor_scalar(tiles_i[:, :], start[:, :], float(P - 1), None, ALU.add))
                do(dve.tensor_scalar(tiles_i[:, :], tiles_i[:, :], P.bit_length() - 1, None, ALU.logical_shift_right))
                do(dve.tensor_copy(tiles[:, :], tiles_i[:, :]))
                do(dve.scalar_tensor_tensor(out=tiles[:, :], in0=iota8[:, :], scalar=-float(LIST_TILES),
                                            in1=tiles[:, :], op0=ALU.mult, op1=ALU.add))
                own.mark(dve.tensor_scalar(extra[:, :], tiles[:, 0:E - 1], -1.0, float(LIST_TILES), ALU.mult, ALU.add))
                do(dve.tensor_tensor_scan(first[:, :], tiles[:, :], zero[:, :], 0.0, ALU.add, ALU.add))
                do(dve.tensor_scalar(gone[:, :], first[:, 0:E - 1], lane[:, 0:1], None, ALU.is_le))
                do(dve.scalar_tensor_tensor(out=gone[:, :], in0=gone[:, :], scalar=1.0, in1=extra[:, :],
                                            op0=ALU.mult, op1=ALU.mult, accum_out=skipped[:, :]))
                dve.tensor_tensor(row[:, :], lane[:, :], skipped[:, :], ALU.add).then_inc(s_row, 1)

            def weigh(b):
                dve.wait_ge(s_egap, b + 1)
                own.mark(dve.tensor_scalar(wsum[:, :], egap[:, :], 1.0, None, ALU.add))
                own.wait()
                own.mark(dve.reciprocal(w12[:, :, 0], wsum[:, :]))
                own.wait()
                own.mark(dve.tensor_tensor(w12[:, :, 1], w12[:, :, 0], egap[:, :], ALU.mult))
                own.wait()
                own.mark(dve.tensor_scalar(w12[:, :, :], w12[:, :, :], tgate[:, 1:2], None, ALU.mult))
                own.wait()
                for t in range(TT):
                    own.mark(dve.tensor_scalar(wtmp[:, t, :], onehot[:, 0, :, t], w12[:, t, 0:1], None, ALU.mult))
                own.wait()
                for t in range(TT):
                    last = dve.scalar_tensor_tensor(out=rows[b % 2][:, t, D:ROW], in0=onehot[:, 1, :, t],
                                                    scalar=w12[:, t, 1:2], in1=wtmp[:, t, :],
                                                    op0=ALU.mult, op1=ALU.add)
                last.then_inc(s_rows, 1)

            def residual(b):
                dve.wait_ge(s_proj, b + 1)
                dve.tensor_tensor(y[:, :, :], proj[:, :].rearrange("p (t d) -> p t d", t=TT), bo[:, :, :], ALU.add)\
                    .then_inc(s_projr, 1)
                dve.wait_ge(s_projr, b + 1)
                if b >= 2:
                    dve.wait_ge(s_x2st[b % 2], 16 * (b // 2))
                dve.scalar_tensor_tensor(out=x2[b % 2][:, :, :], in0=y[:, :, :], scalar=tgate[:, 0:1],
                                         in1=x_raw[b % 3][:, :, :], op0=ALU.mult, op1=ALU.add).then_inc(s_x2, 1)
                dve.wait_ge(s_x2, b + 1)
                moments("c", [x2[b % 2][:, t, :] for t in range(TT)], mv_c, s_mvc, s_xn, b)

            def maximum(n):
                for t in range(TT):
                    dve.wait_ge(s_score, TT * n + t + 1)
                    own.mark(dve.tensor_reduce(smax[:, n % 2, t:t + 1], score[t][:, :], AX_X, ALU.max))
                own.wait()
                dve.tensor_scalar(nbias[:, n % 2, :], smax[:, n % 2, :], -SCALE, None, ALU.mult).then_inc(s_max, 1)

            def reciprocal_sum(n):
                dve.wait_ge(s_exp, TT * (n + 1))
                dve.reciprocal(rsum[:, n % 2, :], ssum[:, n % 2, :]).then_inc(s_rsum, 1)

            prepare_a(0)
            lo_weights(dve, "dve", "k")
            prepare_b(0)
            lo_weights(dve, "dve", "q")
            dve.wait_ge(s_kvt0, 1)
            dve.tensor_tensor(kvt[0][1][:, :, :], zt[:, :, :], kvt[0][0][:, :, :].bitcast(F32), ALU.subtract)\
                .then_inc(s_kvt, 1)
            prepare_a(1)
            lo_weights(dve, "dve", "o")
            dve.wait_ge(s_bias, 16 * N_BIAS)
            for u in before:
                if u[0] not in "zt":
                    read_unit(*u)
            dve.wait_ge(s_small, 16 * N_SMALL)
            dve.wait_ge(s_tg, 1)
            dve.wait_ge(s_const, 2)
            dve.wait_ge(s_routing, N_ROUTING)
            own.mark(dve.memset(zero[:, :], 0.0))
            own.mark(dve.tensor_scalar(start[:, :], iota8[:, :], float(LIST_TILES * P), None, ALU.mult))
            own.wait()
            for i in range(STEPS + H):
                b, h = i // H, i % H
                if i < STEPS:
                    maximum(i)
                if 1 <= i <= STEPS:
                    for t in range(2):
                        dve.wait_ge(s_pthi, 2 * (i - 1) + t + 1)
                        dve.tensor_tensor(pt[1][:, 2 * t:2 * t + 2, :],
                                          turn[t][:, :].rearrange("p (j i) -> p j i", j=2),
                                          pt[0][:, 2 * t:2 * t + 2, :].bitcast(F32), ALU.subtract)\
                            .then_inc(s_ptlo, 1)
                for u in steps[i]:
                    if u[0] in "kq":
                        read_unit(*u)
                if i < STEPS:
                    reciprocal_sum(i)
                for u in steps[i]:
                    if u[0] in "vogr":
                        read_unit(*u)
                if h in (A_STEP - 1, A_STEP) and b + 2 < B:
                    prepare_a(b + 2, h - A_STEP + 1)
                if h == B_STEP and b + 1 < B:
                    prepare_b(b + 1)
                if b >= 1:
                    for at, part in ((R_STEP, residual), (G_STEP, largest), (E_STEP, choose), (W_STEP, weigh),
                                     (L_STEP, find_places)):
                        if h == at:
                            part(b - 1)
                if i == STEPS + 2:
                    split.make_lo(dve, "dve", 0, range(PIECES // 2))
            find_rows()


def experts(nc, program, A, sem, sems, alloc, work, split, load_b1, lists, ident, iota8, dram):
    with ExitStack() as ctx:
        def sb(name, shape, dt=F32):
            return alloc(ctx, name, shape, dt)

        def bank(name):
            return ctx.enter_context(nc.psum_tensor(name, [P, 512], F32))

        w1 = split.w[0]
        w2, w2_in = weight_pair(alloc, ctx, "w2", [P, FH // P, E * D])
        split.add(w2, w2_in)
        ge = sb("ge", [P, E - 1, N_TILES])
        expf = sb("expf", [P, N_TILES])
        W1S, W2S = range(PIECES // 2), range(PIECES // 2, PIECES)
        s_b1, s_b2 = sems["b1"], sem("b2_in")
        b1, b2 = work["b1"], work["b2"]

        def raw_split(eng):
            split.wait_lo(eng, 0, range(PIECES))

        xg, xt, hb, ha, ht, y1, yo, wcol, wjunk = (
            work[n] for n in ("xg", "xt", "hb", "ha", "ht", "y1", "yo", "wcol", "wjunk"))
        names = xg[NX - 1]
        token, expert, mine, first, iota_t, row = (
            lists[n] for n in ("token", "expert", "mine", "first", "iota_t", "row"))
        ph = [bank(f"ph{i}") for i in range(2)]
        pht = [bank(f"pht{i}") for i in range(2)]
        px = [bank(f"px{i}") for i in range(2)]
        py = [bank(f"py{i}") for i in range(2)]

        TURNS = 2 * N_TILES

        def expert_of(eng, u):
            return eng.value_load(expert[0:1, u % N_TILES:u % N_TILES + 1], min_val=0, max_val=E - 1)

        SOON = 2
        LAG = 2
        s_g = [sem(f"gathered{i}") for i in range(NX)]
        s_xst = [sem(f"xt_stored{i}") for i in range(NT)]
        s_xld = [sem(f"xt_loaded{i}") for i in range(NT)]
        s_y1st = [sem(f"y1_stored{i}") for i in range(NY)]
        s_y1ld = [sem(f"y1_loaded{i}") for i in range(NY)]
        s_px, s_xhi, s_xlo = sem("x_turned"), sem("xt_hi"), sem("xt_lo")
        s_ph, s_hb, s_ha = sem("hidden"), sem("hidden_bias"), sem("hidden_act")
        s_pht, s_hhi, s_hlo = sem("hidden_turned"), sem("ht_hi"), sem("ht_lo")
        s_py, s_pyr, s_w, s_yo = sem("y_sum"), sem("y_read"), sem("w_ready"), sem("y_out")
        s_add = sem("added")
        s_names, s_turned, s_token, s_tables = sem("names_in"), sem("names_turned"), sem("token_ready"), sem("tables")

        @program("sync")
        def _(sp):
            def load_x(u):
                sp.dma_start(xt[u % NT][:, :, :, :].bitcast(F32), dram["xt"][u - N_TILES]).then_inc(s_xld[u % NT], 16)

            def load_y1(u):
                n = u - N_TILES
                if n >= NY:
                    sp.wait_ge(s_pyr, u - NY + 1)
                sp.dma_start(y1[n % NY][:, :], dram["half"][n]).then_inc(s_y1ld[n % NY], 16)

            sp.wait_ge(s_g[NX - 2], 16)
            split.wait_lo(sp, 0, W1S)
            sp.dma_start(b2[:, :], A["L0_ffn_b2"].rearrange("e d -> (e d)").partition_broadcast(P)).then_inc(s_b2, 16)
            for u in range(N_TILES + LAG):
                if u < N_TILES:
                    sp.wait_ge(s_xlo, u + 1)
                    sp.dma_start(dram["xt"][u], xt[u % NT][:, :, :, :].bitcast(F32)).then_inc(s_xst[u % NT], 16)
                if u == NSTAGE:
                    raw_split(sp)
                if NSTAGE <= u < 2 * NSTAGE:
                    split.load(sp, 1, u - NSTAGE)
                if u == N_TILES:
                    sp.wait_ge(s_hb, N_TILES)
                    for i in range(NT):
                        sp.wait_ge(s_xst[i], 16 * len(range(i, N_TILES, NT)))
                    for j in range(NSTAGE, PIECES // 2):
                        split.load(sp, 1, j)
                    for v in range(NT):
                        load_x(N_TILES + v)
                    load_b1(sp, 1)
                if u >= LAG:
                    v = u - LAG
                    sp.wait_ge(s_pyr, v + 1)
                    sp.dma_start(dram["half"][v], y1[v % NY][:, :]).then_inc(s_y1st[v % NY], 16)
            for j in range(PIECES // 2, PIECES):
                if split.staged(j):
                    split.wait_lo(sp, 1, [j - PIECES // 2])
                split.load(sp, 1, j)
            for i in range(NY):
                sp.wait_ge(s_y1st[i], 16 * len(range(i, N_TILES, NY)))
            load_y1(N_TILES)
            for u in range(N_TILES, TURNS):
                if u + NT < TURNS:
                    sp.wait_ge(s_ph, u + 1)
                    load_x(u + NT)
                if u + 1 < TURNS:
                    load_y1(u + 1)

        @program("gpsimd")
        def _(pool):
            def gather(u):
                if u >= NX:
                    pool.wait_ge(s_px, u - NX + 1)
                    pool.wait_ge(s_w, u - NX + 1)
                pool.indirect_dma_start(
                    out=xg[u % NX][:, :], out_offset=None, in_=dram["xhat"],
                    in_offset=bass.IndirectOffsetOnAxis(ap=token[:, u:u + 1].bitcast(U32), axis=0),
                ).then_inc(s_g[u % NX], 16)

            split.wait_lo(pool, 0, W1S)
            pool.wait_ge(sems["row"], 1)
            pool.wait_ge(sems["listed"], 16 * TOP * TT * B)
            pool.indirect_dma_start(
                out=names[0:N_TILES, 0:P], out_offset=None, in_=dram["lists"],
                in_offset=bass.IndirectOffsetOnAxis(ap=row[0:N_TILES, :].bitcast(U32), axis=0),
            ).then_inc(s_names, 16)
            for i in range(2):
                pool.wait_ge(sems["x2st"][i], 16 * (B // 2))
                pool.wait_ge(sems["rowst"][i], 16 * (B // 2))
            pool.wait_ge(s_token, 1)
            for u in range(NX - 1):
                gather(u)
            for u in range(TURNS + LAG):
                if u == N_TILES:
                    pool.wait_ge(s_ph, N_TILES)
                    split.make_lo(pool, "pool", 1, W1S)
                    pool.wait_ge(s_py, N_TILES)
                    split.make_lo(pool, "pool", 1, W2S)
                if u + NX - 1 < N_TILES:
                    gather(u + NX - 1)
                t = u - LAG - N_TILES
                if t >= 0:
                    pool.wait_ge(s_yo, t + 1)
                    if t:
                        pool.wait_ge(s_add, 16 * t)
                    pool.indirect_dma_start(
                        out=A["out"], out_offset=bass.IndirectOffsetOnAxis(ap=token[:, t:t + 1].bitcast(U32), axis=0),
                        in_=yo[t % NO][:, :], in_offset=None, compute_op=ALU.add,
                    ).then_inc(s_add, 16)
            pool.wait_ge(s_add, 16 * N_TILES)

        @program("tensor")
        def _(pe):
            def turn_x(u):
                pe.wait_ge(s_g[u % NX], 16 * (u // NX + 1))
                if u >= 2:
                    pe.wait_ge(s_xlo, u - 1)
                for k in range(KD):
                    last = pe.transpose(px[u % 2][:, k * P:(k + 1) * P], xg[u % NX][:, k * P:(k + 1) * P], ident[:, :])
                last.then_inc(s_px, 1)

            def hidden(u, e):
                if u < N_TILES:
                    pe.wait_ge(s_xlo, u + 1)
                else:
                    pe.wait_ge(s_xld[u % NT], 16 * sum(v % NT == u % NT for v in range(N_TILES, u + 1)))
                if u >= 2:
                    pe.wait_ge(s_hb, u - 1)
                for k in range(KD):
                    last = product(pe, ph[u % 2][:, :], [xt[u % NT][:, s, k, :] for s in range(2)],
                                   [s[:, k, bass.ds(e * FH, FH)] for s in w1], k == 0, k == KD - 1)
                last.then_inc(s_ph, 1)

            def turn_h(u):
                pe.wait_ge(s_ha, u + 1)
                if u >= 2:
                    pe.wait_ge(s_hlo, u - 1)
                for g in range(FH // P):
                    last = pe.transpose(pht[u % 2][:, g * P:(g + 1) * P], ha[:, g * P:(g + 1) * P], ident[:, :])
                last.then_inc(s_pht, 1)

            def out(u, e):
                pe.wait_ge(s_hlo, u + 1)
                if u >= 2:
                    pe.wait_ge(s_pyr, u - 1)
                if u % N_TILES == 0:
                    split.wait_lo(pe, u // N_TILES, W2S)
                for g in range(FH // P):
                    last = product(pe, py[u % 2][:, 0:D], [s[:, g, :] for s in ht[u % 2]],
                                   [s[:, g, bass.ds(e * D, D)] for s in w2], g == 0, g == FH // P - 1)
                last.then_inc(s_py, 1)

            pe.wait_ge(s_names, 16)
            pe.wait_ge(sems["row"], 1)
            pe.transpose(py[0][:, 0:N_TILES], names[0:N_TILES, 0:P], ident[0:N_TILES, 0:N_TILES]).then_inc(s_turned, 1)
            turn_x(0)
            turn_x(1)
            pe.wait_ge(s_tables, 3)
            e = {}
            for u in range(TURNS + LAG):
                if u == N_TILES:
                    turn_h(u - 1)
                    for v in range(u - LAG, u):
                        out(v, e[v])
                if u < TURNS:
                    e[u] = expert_of(pe, u)
                    if u % N_TILES == 0:
                        split.wait_lo(pe, u // N_TILES, W1S)
                    hidden(u, e[u])
                if u == N_TILES:
                    continue
                if 1 <= u < N_TILES - 1:
                    turn_x(u + 1)
                if 1 <= u <= TURNS:
                    turn_h(u - 1)
                if u >= LAG and not N_TILES <= u < N_TILES + LAG:
                    out(u - LAG, e[u - LAG])

        @program("vector")
        def _(dve):
            def lo_x(u):
                dve.wait_ge(s_xhi, u + 1)
                dve.tensor_tensor(xt[u % NT][:, 1], px[u % 2][:, 0:D].rearrange("p (k t) -> p k t", k=KD),
                                  xt[u % NT][:, 0].bitcast(F32), ALU.subtract).then_inc(s_xlo, 1)

            def finish(u, e):
                t = u % N_TILES
                dve.wait_ge(s_py, u + 1)
                if u < N_TILES:
                    dve.wait_ge(s_b2, 16)
                    if u >= NY:
                        dve.wait_ge(s_y1st[u % NY], 16 * (u // NY))
                    dve.tensor_tensor(y1[u % NY][:, :], py[u % 2][:, 0:D], b2[:, bass.ds(e * D, D)], ALU.add)\
                        .then_inc(s_pyr, 1)
                    return
                dve.wait_ge(s_y1ld[t % NY], 16 * (t // NY + 1))
                if t >= NO:
                    dve.wait_ge(s_add, 16 * (t - NO + 1))
                dve.tensor_tensor(yo[t % NO][:, :], py[u % 2][:, 0:D], y1[t % NY][:, :], ALU.add).then_inc(s_pyr, 1)
                dve.wait_ge(s_pyr, u + 1)
                dve.tensor_scalar(yo[t % NO][:, :], yo[t % NO][:, :], wcol[:, t:t + 1], None, ALU.mult)\
                    .then_inc(s_yo, 1)

            dve.wait_ge(sems["row"], 1)
            dve.tensor_tensor(ge[:, :, :], iota_t[:, :].unsqueeze(1).to_broadcast([P, E - 1, N_TILES]),
                              first[:, 0:E - 1].unsqueeze(2).to_broadcast([P, E - 1, N_TILES]), ALU.is_ge)\
                .then_inc(s_tables, 1)
            dve.wait_ge(s_tables, 1)
            dve.tensor_reduce(expf[:, :], ge[:, :, :].rearrange("p e t -> p t e"), AX_X, ALU.add).then_inc(s_tables, 1)
            dve.wait_ge(s_tables, 2)
            dve.tensor_copy(expert[:, :], expf[:, :]).then_inc(s_tables, 1)
            dve.tensor_tensor(mine[:, :, :], iota8[:, :].unsqueeze(1).to_broadcast([P, N_TILES, E]),
                              expf[:, :].unsqueeze(2).to_broadcast([P, N_TILES, E]), ALU.is_equal).then_inc(s_tables, 1)
            split.make_lo(dve, "dve", 0, W2S[:4])
            dve.wait_ge(s_turned, 1)
            dve.tensor_copy(token[:, :], py[0][:, 0:N_TILES]).then_inc(s_token, 1)
            split.make_lo(dve, "dve", 0, W2S[4:])
            dve.wait_ge(s_tables, 4)
            lo_x(0)
            lo_x(1)
            dve.wait_ge(s_b1, 16)
            def add_bias(u, e):
                dve.wait_ge(s_ph, u + 1)
                if u:
                    dve.wait_ge(s_ha, u)
                dve.tensor_tensor(hb[:, :], ph[u % 2][:, :], b1[:, bass.ds(e * FH, FH)], ALU.add).then_inc(s_hb, 1)

            def take_weights(u):
                dve.wait_ge(s_g[u % NX], 16 * (u // NX + 1))
                if u:
                    dve.wait_ge(s_w, u)
                dve.scalar_tensor_tensor(out=wjunk[:, :], in0=xg[u % NX][:, D:ROW], scalar=1.0,
                                         in1=mine[:, u, :], op0=ALU.mult, op1=ALU.mult,
                                         accum_out=wcol[:, u:u + 1]).then_inc(s_w, 1)

            def lo_h(u):
                if u == 0:
                    raw_split(dve)
                dve.wait_ge(s_hhi, u + 1)
                dve.tensor_tensor(ht[u % 2][1][:, :, :], pht[u % 2][:, :].rearrange("p (g t) -> p g t", g=FH // P),
                                  ht[u % 2][0][:, :, :].bitcast(F32), ALU.subtract).then_inc(s_hlo, 1)

            e = {}
            for u in range(TURNS + LAG):
                if u < TURNS:
                    e[u] = expert_of(dve, u)
                if u == N_TILES:
                    lo_h(u - 1)
                    for v in range(u - LAG, u):
                        finish(v, e[v])
                    split.make_lo(dve, "dve", 1, W1S)
                    dve.wait_ge(s_b1, 32)
                    dve.wait_ge(s_w, N_TILES)
                    add_bias(u, e[u])
                    continue
                if u < TURNS:
                    add_bias(u, e[u])
                if 1 <= u < N_TILES - 1:
                    lo_x(u + 1)
                if u < N_TILES:
                    take_weights(u)
                if 1 <= u <= TURNS:
                    lo_h(u - 1)
                if u == N_TILES + 1:
                    split.make_lo(dve, "dve", 1, W2S)
                if u >= LAG and not N_TILES <= u < N_TILES + LAG:
                    finish(u - LAG, e[u - LAG])

        @program("scalar")
        def _(act):
            def hi_x(u):
                act.wait_ge(s_px, u + 1)
                if u >= NT:
                    act.wait_ge(s_ph, u - NT + 1)
                    act.wait_ge(s_xst[u % NT], 16 * (u // NT))
                act.activation(xt[u % NT][:, 0], px[u % 2][:, 0:D].rearrange("p (k t) -> p k t", k=KD), ACT.Copy)\
                    .then_inc(s_xhi, 1)

            act.wait_ge(sems["row"], 1)
            for i in range(2):
                act.wait_ge(sems["x2st"][i], 16 * (B // 2))
                act.wait_ge(sems["rowst"][i], 16 * (B // 2))
            split.make_hi(act, 0, W2S)
            hi_x(0)
            hi_x(1)
            for u in range(TURNS + 1):
                if 1 <= u < N_TILES - 1:
                    hi_x(u + 1)
                if u:
                    v = u - 1
                    if v == 0:
                        raw_split(act)
                    act.wait_ge(s_pht, v + 1)
                    if v >= 2:
                        act.wait_ge(s_py, v - 1)
                    act.activation(ht[v % 2][0][:, :, :], pht[v % 2][:, :].rearrange("p (g t) -> p g t", g=FH // P),
                                   ACT.Copy).then_inc(s_hhi, 1)
                if u == N_TILES:
                    split.make_hi(act, 1, W1S[1:])
                    act.wait_ge(s_py, N_TILES)
                    split.make_hi(act, 1, W2S[:SOON])
                if u < TURNS:
                    act.wait_ge(s_hb, u + 1)
                    if u:
                        act.wait_ge(s_pht, u)
                    act.activation(ha[:, :], hb[:, :], ACT.Silu).then_inc(s_ha, 1)
                if u == N_TILES - 1:
                    act.wait_ge(s_ph, N_TILES)
                    split.make_hi(act, 1, W1S[:1])
                if u == N_TILES + 1:
                    split.make_hi(act, 1, W2S[SOON:])


_INS = ['x', 'ctx_1024', 'g_xattn', 'g_ffn', 'L0_xattn_gamma_media', 'L0_xattn_beta_media', 'L0_xattn_gamma_lat',
        'L0_xattn_beta_lat', 'L0_xattn_Wq', 'L0_xattn_bq', 'L0_xattn_Wkv', 'L0_xattn_bkv', 'L0_xattn_Wo',
        'L0_xattn_bo', 'L0_ffn_Wg', 'L0_ffn_bg', 'L0_ffn_W1', 'L0_ffn_b1', 'L0_ffn_W2', 'L0_ffn_b2']


def kernel(**inputs):
    import numpy as np
    import concourse.bacc as bacc
    from concourse.bass_utils import run_bass_kernel_spmd

    nc = bacc.Bacc("TRN2", target_bir_lowering=False, num_devices=1)
    arrays, aps = {}, {}
    for name in _INS:
        a = np.ascontiguousarray(inputs[name])
        arrays["in_" + name] = a
        aps[name] = nc.dram_tensor("in_" + name, a.shape, mybir.dt.from_np(a.dtype), kind="ExternalInput").ap()
    aps["out"] = nc.dram_tensor("out_rows", (TOKENS + P, D), F32, kind="ExternalOutput").ap()
    build(nc, aps)
    got = run_bass_kernel_spmd(nc, [arrays], core_ids=[0]).results[0]["out_rows"]
    return got[0:TOKENS].reshape(B, T, D)
```
